# Optimizing a Trainium2 kernel written in Bass

```python
import numpy as np
import jax
import jax.numpy as jnp

def _softmax(x, axis=-1):
    return jax.nn.softmax(x, axis=axis)

def _gelu(x):
    return jax.nn.gelu(x, approximate=True)

def _silu(x):
    return jax.nn.silu(x)

def _sigmoid(x):
    return jax.nn.sigmoid(x)

def _layernorm(x, axis=-1, eps=1e-05):
    m = jnp.mean(x, axis=axis, keepdims=True)
    v = jnp.var(x, axis=axis, keepdims=True)
    return (x - m) / jnp.sqrt(v + eps)

def _scatter_add(tgt, idx, src, axis=0):
    return tgt.at[idx].add(src)

def _segment_sum(src, seg, n):
    return jax.ops.segment_sum(src, seg, n)
kernel_name = 'mk_gnn_resnorm_d2_gnn_r8_1ea1d9'

def setup_inputs(seed: int=0):
    np.random.seed(seed)
    _w = jnp.asarray

    def _rec_inputs():
        import jax
        import jax.numpy as jnp
        _gk = jax.random.key(seed)
        x = -0.0003713 + 1 * jax.random.normal(jax.random.fold_in(_gk, 1), (6250, 128), jnp.float32)
        _s = jax.random.randint(jax.random.fold_in(_gk, 2), (50000,), 0, 6250, jnp.int32)
        _d = jax.random.randint(jax.random.fold_in(_gk, 3), (50000,), 0, 6250, jnp.int32)
        _loop = jnp.arange(6250, dtype=jnp.int32)
        src = jnp.concatenate([_s, _d, _loop])
        dst = jnp.concatenate([_d, _s, _loop])
        _o = jnp.argsort(dst, stable=True)
        src = src[_o]
        dst = dst[_o]
        edge_attr_32 = 0.000196303 + 1.00016 * jax.random.normal(jax.random.fold_in(_gk, 11), (106250, 32), jnp.float32)
        return (x, src, dst, edge_attr_32)
    x, src, dst, edge_attr_32 = _rec_inputs()

    def _L0_gnn_setup():
        import jax, jax.numpy as jnp
        import numpy as np
        N_NODES = 12500
        N_EDGES = 100000
        H_DIM = 128
        E_DIM = 32
        N_LAYER = 3
        key = jax.random.key(seed)
        ks = jax.random.split(key, 5)
        x = jax.random.normal(ks[0], (N_NODES, H_DIM), dtype=jnp.float32)
        edge_index = jax.random.randint(ks[1], (2, N_EDGES), 0, N_NODES, dtype=jnp.int64)
        edge_attr = jax.random.normal(ks[2], (N_EDGES, E_DIM), dtype=jnp.float32)
        fan_in = 2 * H_DIM + E_DIM
        Wm = jax.random.normal(ks[3], (N_LAYER, H_DIM, fan_in), dtype=jnp.float32) / jnp.sqrt(fan_in)
        bm = jax.random.normal(ks[4], (N_LAYER, H_DIM), dtype=jnp.float32) * 0.01
        return {'x': x, 'edge_index': edge_index, 'edge_attr': edge_attr, 'Wm': Wm, 'bm': bm}
    _L0_gnn_all = _L0_gnn_setup()
    _L0_gnn_in = {k: v for k, v in _L0_gnn_all.items() if k in ('Wm', 'bm')}
    del _L0_gnn_all

    def _L1_gnn_setup():
        import jax, jax.numpy as jnp
        import numpy as np
        N = 12500
        E = 200000
        D = 128
        NEG_SLOPE = 0.2
        key = jax.random.key(seed)
        ks = jax.random.split(key, 5)
        x = jax.random.normal(ks[0], (N, D), jnp.float32)
        edge_index = jax.random.randint(ks[1], (2, E), 0, N, dtype=jnp.int64)
        W = jax.random.normal(ks[2], (D, D), jnp.float32) / np.sqrt(D).astype(np.float32)
        att_src = jax.random.normal(ks[3], (D,), jnp.float32) / np.sqrt(D).astype(np.float32)
        att_dst = jax.random.normal(ks[4], (D,), jnp.float32) / np.sqrt(D).astype(np.float32)
        bias = jnp.zeros((D,), jnp.float32)
        return {'x': x, 'edge_index': edge_index, 'W': W, 'att_src': att_src, 'att_dst': att_dst, 'bias': bias}
    _L1_gnn_all = _L1_gnn_setup()
    _L1_gnn_in = {k: v for k, v in _L1_gnn_all.items() if k in ('W', 'att_src', 'att_dst', 'bias')}
    del _L1_gnn_all
    return {'x': x, 'src': src, 'dst': dst, 'edge_attr_32': edge_attr_32, 'L0_gnn_Wm': _L0_gnn_in['Wm'], 'L0_gnn_bm': _L0_gnn_in['bm'], 'L1_gnn_W': _L1_gnn_in['W'], 'L1_gnn_att_src': _L1_gnn_in['att_src'], 'L1_gnn_att_dst': _L1_gnn_in['att_dst'], 'L1_gnn_bias': _L1_gnn_in['bias']}

def reference(x, src, dst, edge_attr_32, L0_gnn_Wm, L0_gnn_bm, L1_gnn_W, L1_gnn_att_src, L1_gnn_att_dst, L1_gnn_bias):
    import jax
    import jax.numpy as jnp

    def _L0_gnn_ref(x, edge_index, edge_attr, Wm, bm):
        import jax, jax.numpy as jnp
        import numpy as np
        N_NODES = 12500
        N_EDGES = 100000
        H_DIM = 128
        E_DIM = 32
        N_LAYER = 3
        src = edge_index[0]
        dst = edge_index[1]
        n_nodes = x.shape[0]
        n_layer = Wm.shape[0]
        for l in range(n_layer):
            m = jnp.concatenate([x[src], x[dst], edge_attr], axis=1)
            m = jnp.einsum('ef,hf->eh', m, Wm[l]) + bm[l]
            x = jax.ops.segment_sum(m, dst, num_segments=n_nodes)
            x = jax.nn.leaky_relu(x, negative_slope=0.01)
        x = jax.nn.leaky_relu(x, negative_slope=0.01)
        return x

    def _L1_gnn_ref(x, edge_index, W, att_src, att_dst, bias):
        import jax, jax.numpy as jnp
        import numpy as np
        N = 12500
        E = 200000
        D = 128
        NEG_SLOPE = 0.2
        n = x.shape[0]
        h = x @ W
        a_src = h @ att_src
        a_dst = h @ att_dst
        loop = jnp.arange(n, dtype=edge_index.dtype)
        src = jnp.concatenate([edge_index[0], loop])
        dst = jnp.concatenate([edge_index[1], loop])
        e = jax.nn.leaky_relu(a_src[src] + a_dst[dst], NEG_SLOPE)
        e_max = jax.ops.segment_max(e, dst, num_segments=n)
        e_exp = jnp.exp(e - e_max[dst])
        denom = jax.ops.segment_sum(e_exp, dst, num_segments=n)
        alpha = e_exp / denom[dst]
        out = jax.ops.segment_sum(alpha[:, None] * h[src], dst, num_segments=n)
        return out + bias
    edge_index = jnp.stack([src, dst])
    x = _layernorm(x + _L0_gnn_ref(x, edge_index, edge_attr_32, L0_gnn_Wm, L0_gnn_bm), axis=-1)
    x = _layernorm(x + _L1_gnn_ref(x, edge_index, L1_gnn_W, L1_gnn_att_src, L1_gnn_att_dst, L1_gnn_bias), axis=-1)
    return x

_drawn_inputs = setup_inputs


def setup_inputs(seed=0):
    import zlib

    import numpy as np

    out = dict(_drawn_inputs(seed))
    spreads = {'L1_gnn_bias': (0.0, 0.1)}
    factors = {'L0_gnn_bm': 3.085, 'L1_gnn_att_dst': 4.55}
    for name, (base, spread) in spreads.items():
        noise = np.random.default_rng([zlib.crc32(name.encode()), seed]).standard_normal(out[name].shape)
        drawn = base * np.exp(spread * noise) if base else spread * noise
        out[name] = jnp.asarray(drawn.astype(out[name].dtype))
    for name, factor in factors.items():
        out[name] = (out[name] * factor).astype(out[name].dtype)
    return out
```

```python
from contextlib import ExitStack

import numpy as np
import concourse.bass as bass
from concourse import mybir

F32 = mybir.dt.float32
I32 = mybir.dt.int32
U32 = mybir.dt.uint32
ALU = mybir.AluOpType
ACT = mybir.ActivationFunctionType
AX = mybir.AxisListType

P = 128
D = 128
EA = 32
EA1 = EA + 1
C = 3
U = 4
SB = 7
HB = SB * P // 2
ROW = D + 4
NO_NODE = 8191
NEG = -1.0e30
EPS = 1e-5


def shapes(n_nodes, n_edges):
    nb = -(-n_nodes // P)
    tiles = -(-n_edges // P)
    ta = -(-(tiles + C) // 8) * 8
    most = nb * -(-tiles // C) + U
    nc_cols = -(-most // P)
    return nb, tiles, ta, nc_cols


def build(nc, x, xT, srcT, dstT, dst_rows, ea, W0, W1, att, bias, out):
    n_nodes = out.shape[0]
    NB = x.shape[0] // P
    NP = NB * P
    TA = srcT.shape[1]
    NT = NB // SB
    LAST = n_nodes - (NB - 1) * P
    NCC = shapes(n_nodes, TA * P)[3]
    RJ = 8
    RP = TA // RJ
    BIG_T = float(TA)
    assert NB % SB == 0 and TA < 1024 and NB <= P

    table = [x, nc.dram_tensor("table_1", [NP, D], F32).ap(), nc.dram_tensor("table_2", [NP, D], F32).ap()]
    table_h = nc.dram_tensor("table_h", [NP, ROW], F32).ap()
    x1_dram = nc.dram_tensor("x1_rows", [NP, D], F32).ap()
    lohi_dram = nc.dram_tensor("tile_lo_hi", [2, TA], F32).ap()
    chunk_dram = nc.dram_tensor("chunk_list", [P * NCC], I32).ap()

    with ExitStack() as ctx:
        def sb(name, shape, dt=F32):
            return ctx.enter_context(nc.sbuf_tensor(name, shape, dt))

        def ps(name, shape):
            return ctx.enter_context(nc.psum_tensor(name, shape, F32))

        def sem(name):
            return ctx.enter_context(nc.semaphore(name))

        chunks = sb("chunks", [1, P * NCC], I32)
        turns = sb("turns", [1, 1], I32)
        src = sb("src", [P, TA], I32)
        dst = sb("dst", [P, TA])
        feat = sb("feat", [P, NP])
        acc = sb("acc", [P, NP])
        eaT = sb("eaT", [EA1, NP])
        ident = sb("ident", [P, P])
        iota = sb("iota", [P, P])
        base = sb("base", [P, NB])
        w0 = sb("w0", [P, 3, 2, D])
        w0e = sb("w0e", [EA1, 3, D])
        sel = sb("sel", [EA1, P])
        w1 = sb("w1", [P, D])
        att_row = sb("att_row", [P, 2, D])
        bias_row = sb("bias_row", [P, D])
        a_dst = sb("a_dst", [P, NB])
        peak = sb("peak", [P, NB])
        denom = sb("denom", [P, NB])
        eps = sb("eps", [P, 1])
        bank = [ps(f"bank{i}", [P, 512]) for i in range(8)]

        s_in, s_exit = sem("inputs_loaded"), sem("pass_done")
        s_tick = sem("wait_carrier")
        s_const = sem("constants_ready")
        s_dve, s_act, s_pe = sem("vector_step"), sem("scalar_step"), sem("tensor_step")

        row_got = [[sem(f"row_got{p}_{u}") for u in range(U)] for p in range(4)]
        G16 = 16 * C

        NIN = 14
        with ExitStack() as c0:
            def sb0(name, shape, dt=F32):
                return c0.enter_context(nc.sbuf_tensor(name, shape, dt))
            dr = sb0("dst_rows_sb", [RP, RJ, P], I32)
            di = sb0("dst_int", [P, TA], I32)
            lohi = sb0("lohi", [RP, 2, RJ])
            lo_b = sb0("lo_b", [NB, TA])
            hi_b = sb0("hi_b", [NB, TA])
            hit = sb0("hit", [NB, TA])
            t1 = sb0("t1", [NB, TA])
            t2 = sb0("t2", [NB, TA])
            blk = sb0("blk", [NB, 2])
            rng = sb0("rng", [NB, 8])
            rngi = sb0("rngi", [NB, 2], I32)
            tri = sb0("tri", [NB, NB + 1])
            nbc = sb0("nbc", [NB, 2, P])
            cum = sb0("cum", [P, NB + 1])
            q = sb0("q", [P, NB])
            dq = sb0("dq", [P, NB])
            sidx = sb0("sidx", [P, NCC])
            step = sb0("step", [P, NCC])
            v = sb0("v", [P, NCC])
            vi = sb0("vi", [P, NCC], I32)
            turns_i = sb0("turns_i", [P, 1], I32)
            s_lohi, s_back, s_list, s_rng, s_cum = (sem("lohi_stored"), sem("lohi_back"), sem("list_stored"),
                                                    sem("ranges_ready"), sem("cum_ready"))
            s_ones = sem("iotas_ready")
            s_c = sem("stage0_step")
            block = c0.enter_context(nc.Block())

            @block.sync
            def _(sp):
                sp.dma_start(dr[:], dst_rows.rearrange("(p j) e -> p j e", j=RJ)).then_inc(s_back, 16)
                sp.dma_start(di[:], dstT).then_inc(s_in, 16)
                sp.dma_start(src[:], srcT).then_inc(s_in, 16)
                sp.dma_start(feat[:], xT).then_inc(s_in, 16)
                for l in range(3):
                    sp.dma_start(w0[:, l, :, :], W0[l, 0:2 * D, :].rearrange("(k p) f -> p k f", p=P)).then_inc(s_in, 16)
                    sp.dma_start(w0e[:, l, :], W0[l, 2 * D:2 * D + EA1, :]).then_inc(s_in, 16)
                sp.dma_start(w1[:], W1).then_inc(s_in, 16)
                for k in range(2):
                    sp.dma_start(att_row[:, k, :], att[k:k + 1, :].partition_broadcast(P)).then_inc(s_in, 16)
                sp.dma_start(bias_row[:], bias.partition_broadcast(P)).then_inc(s_in, 16)
                sp.wait_ge(s_c, 2)
                for k in range(2):
                    sp.dma_start(lohi_dram[k].rearrange("(p j) -> p j", j=RJ), lohi[:, k, :]).then_inc(s_lohi, 16)
                sp.wait_ge(s_lohi, 32)
                sp.dma_start(lo_b[:], lohi_dram[0:1, :].partition_broadcast(NB)).then_inc(s_back, 16)
                sp.dma_start(hi_b[:], lohi_dram[1:2, :].partition_broadcast(NB)).then_inc(s_back, 16)
                sp.wait_ge(s_list, 1)
                sp.dma_start(chunk_dram.rearrange("(p c) -> p c", c=NCC), vi[:]).then_inc(s_lohi, 16)
                sp.wait_ge(s_lohi, 48)
                sp.dma_start(chunks[:], chunk_dram.rearrange("(a n) -> a n", a=1)).then_inc(s_in, 16)
                sp.wait_ge(s_in, 16 * NIN)

            @block.gpsimd
            def _(pool):
                nc.gpsimd.memset(tri[:], 1.0).then_inc(s_tick, 1)
                nc.gpsimd.memset(ident[:], 0.0).then_inc(s_tick, 1)
                nc.gpsimd.memset(sel[:], 0.0).then_inc(s_tick, 1)
                nc.gpsimd.iota(iota[:], [[1, P]], channel_multiplier=0, allow_small_or_imprecise_dtypes=True).then_inc(s_ones, 1)
                nc.gpsimd.iota(base[:], [[P, NB]], channel_multiplier=0, allow_small_or_imprecise_dtypes=True).then_inc(s_ones, 1)
                nc.gpsimd.iota(blk[:], [[P - 1, 2]], channel_multiplier=P, allow_small_or_imprecise_dtypes=True).then_inc(s_ones, 1)
                nc.gpsimd.iota(t1[:], [[1, TA]], base=1, channel_multiplier=0, allow_small_or_imprecise_dtypes=True).then_inc(s_ones, 1)
                nc.gpsimd.iota(t2[:], [[-1, TA]], base=TA, channel_multiplier=0, allow_small_or_imprecise_dtypes=True).then_inc(s_ones, 1)
                nc.gpsimd.iota(sidx[:], [[1, NCC]], channel_multiplier=NCC, allow_small_or_imprecise_dtypes=True).then_inc(s_ones, 1)
                pool.wait_ge(s_tick, 3)
                nc.gpsimd.affine_select(out=ident[:], in_=ident[:], compare_op=ALU.not_equal, fill=1.0, base=0,
                                        pattern=[[-1, P]], channel_multiplier=1).then_inc(s_const, 1)
                nc.gpsimd.affine_select(out=tri[:], in_=tri[:], compare_op=ALU.is_gt, fill=0.0, base=0,
                                        pattern=[[1, NB + 1]], channel_multiplier=-1).then_inc(s_const, 1)
                nc.gpsimd.affine_select(out=sel[:], in_=sel[:], compare_op=ALU.not_equal, fill=1.0, base=-EA,
                                        pattern=[[0, P]], channel_multiplier=1).then_inc(s_const, 1)

            @block.vector
            def _(dve):
                k = [0]

                def link(ins):
                    k[0] += 1
                    ins.then_inc(s_c, 1)
                    dve.wait_ge(s_c, k[0])

                dve.wait_ge(s_back, 16)
                nc.vector.tensor_reduce(lohi[:, 0, :], dr[:], AX.X, ALU.min).then_inc(s_c, 1)
                nc.vector.tensor_reduce(lohi[:, 1, :], dr[:], AX.X, ALU.max).then_inc(s_c, 1)
                k[0] = 2
                nc.vector.memset(acc[:], 0.0)
                nc.vector.memset(eaT[:], 0.0)
                nc.vector.memset(denom[:], 1.0)
                link(nc.vector.memset(eps[:], EPS))
                dve.wait_ge(s_ones, 6)
                dve.wait_ge(s_back, 48)
                link(nc.vector.tensor_scalar(lo_b[:], lo_b[:], blk[:, 1:2], None, ALU.is_le))
                link(nc.vector.scalar_tensor_tensor(out=hit[:], in0=hi_b[:], scalar=blk[:, 0:1], in1=lo_b[:],
                                                    op0=ALU.is_ge, op1=ALU.mult))
                link(nc.vector.tensor_tensor(lo_b[:], hit[:], t1[:], ALU.mult))
                link(nc.vector.tensor_tensor(hi_b[:], hit[:], t2[:], ALU.mult))
                link(nc.vector.tensor_reduce(rng[:, 0:1], lo_b[:], AX.X, ALU.max))
                link(nc.vector.tensor_reduce(rng[:, 1:2], hi_b[:], AX.X, ALU.max))
                link(nc.vector.tensor_scalar(rng[:, 2:3], rng[:, 1:2], -1.0, BIG_T, ALU.mult, ALU.add))
                link(nc.vector.tensor_tensor(rng[:, 3:4], rng[:, 0:1], rng[:, 2:3], ALU.subtract))
                link(nc.vector.tensor_scalar(rng[:, 4:5], rng[:, 3:4], 0.0, float(C - 1), ALU.max, ALU.add))
                link(nc.vector.tensor_scalar(rngi[:, 0:1], rng[:, 4:5], float(-(-2 ** 14 // C)), None, ALU.mult))
                link(nc.vector.tensor_scalar(rngi[:, 1:2], rngi[:, 0:1], 14, None, ALU.arith_shift_right))
                link(nc.vector.tensor_copy(rng[:, 5:6], rngi[:, 1:2]))
                nc.vector.tensor_copy(nbc[:, 0, :], rng[:, 5:6].to_broadcast([NB, P]))
                nc.vector.tensor_copy(nbc[:, 1, :], rng[:, 2:3].to_broadcast([NB, P])).then_inc(s_rng, 1)
                dve.wait_ge(s_cum, 1)
                link(nc.vector.tensor_copy(cum[:], bank[0][:, 0:NB + 1]))
                link(nc.vector.scalar_tensor_tensor(out=q[:], in0=cum[:, 0:NB], scalar=-float(C),
                                                    in1=bank[1][:, 0:NB], op0=ALU.mult, op1=ALU.add))
                link(nc.vector.tensor_tensor(dq[:, 1:NB], q[:, 1:NB], q[:, 0:NB - 1], ALU.subtract))
                link(nc.vector.tensor_scalar(dq[:, 1:NB], dq[:, 1:NB], 1024.0, None, ALU.add))
                link(nc.vector.tensor_scalar(v[:], sidx[:], float(C), q[:, 0:1], ALU.mult, ALU.add))
                for b in range(1, NB):
                    link(nc.vector.tensor_scalar(step[:], sidx[:], cum[:, b:b + 1], dq[:, b:b + 1], ALU.is_ge, ALU.mult))
                    link(nc.vector.tensor_tensor(v[:], v[:], step[:], ALU.add))
                link(nc.vector.tensor_scalar(step[:], sidx[:], cum[:, NB:NB + 1], None, ALU.is_lt))
                link(nc.vector.tensor_scalar(v[:], v[:], float(-(TA - C)), None, ALU.add))
                link(nc.vector.tensor_tensor(v[:], v[:], step[:], ALU.mult))
                link(nc.vector.tensor_scalar(vi[:], v[:], float(TA - C), None, ALU.add))
                dve.sem_inc(s_list, 1)
                link(nc.vector.tensor_scalar(turns_i[:], cum[:, NB:NB + 1], float(U - 1), None, ALU.add))
                link(nc.vector.tensor_scalar(turns_i[:], turns_i[:], U.bit_length() - 1, None, ALU.arith_shift_right))
                link(nc.vector.tensor_scalar(turns[:], turns_i[0:1, :], 1.0, None, ALU.max))
                dve.wait_ge(s_in, 16 * NIN)
                nc.vector.tensor_copy(dst[:], di[:]).then_inc(s_dve, 1)

            @block.tensor
            def _(pe):
                pe.wait_ge(s_rng, 1)
                pe.wait_ge(s_const, 3)
                nc.tensor.matmul(bank[0][:, 0:NB + 1], nbc[:, 0, :], tri[:], start=True, stop=True)
                nc.tensor.matmul(bank[1][:, 0:NB], nbc[:, 1, :], ident[0:NB, 0:NB], start=True, stop=True).then_inc(s_cum, 1)

        def chunk_of(eng, at):
            both = eng.value_load(chunks[0:1, bass.ds(at, 1)], min_val=0, max_val=(NB - 1) * 1024 + TA - 1)
            return both >> 10, (both & 1023)

        for l in range(3):
            last = l == 2
            with ExitStack() as c1:
                def sm(name):
                    return ctx.enter_context(nc.semaphore(f"l{l}_{name}"))

                def ring(name, shape, dt=F32):
                    return c1.enter_context(nc.sbuf_tensor(f"l{l}_{name}", shape, dt))
                idx = ring("idx", [P, U, C], U32)
                rows_l = ring("rows", [P, U * C, D])
                onehot = ring("onehot", [P, 2, C, P])
                eas = ring("eas", [P, U, C, EA1])
                idx_ready = [sm(f"idx_ready{u}") for u in range(U)]
                got = row_got[l]
                ea_got = [sm(f"ea_got{u}") for u in range(U)] if l == 0 else None
                hot_ready, mm_done, added = sm("onehot_ready"), sm("sum_ready"), sm("sum_added")
                block = c1.enter_context(nc.Block())

                @block.gpsimd
                def _(pool):
                    n = pool.value_load(turns[0:1, 0:1], min_val=1, max_val=P * NCC // U - 2)
                    with pool.Fori(0, n) as i:
                        for u in range(U):
                            pool.wait_ge(idx_ready[u], i + 1)
                            pool.sem_inc(s_tick, 1)
                            for j in range(C):
                                pool.indirect_dma_start(rows_l[:, u * C + j, :], None, table[l],
                                                        bass.IndirectOffsetOnAxis(ap=idx[:, u, j:j + 1], axis=0)
                                                        ).then_inc(got[u], 16)

                @block.scalar
                def _(act):
                    n = act.value_load(turns[0:1, 0:1], min_val=1, max_val=P * NCC // U - 2)

                    def fetch(i, u):
                        _, t = chunk_of(act, i * U + u)
                        t = t.with_bounds(min_val=0, max_val=TA - C)
                        nc.scalar.copy(idx[:, u, :], src[:, bass.ds(t, C)]).then_inc(idx_ready[u], 1)
                    for u in range(U):
                        fetch(0, u)
                    with act.Fori(1, n + 1) as i:
                        for u in range(U):
                            act.wait_ge(mm_done, i * U + u + 1)
                            act.sem_inc(s_tick, 1)
                            fetch(i, u)

                @block.sync
                def _(sp):
                    if l == 0:
                        n = sp.value_load(turns[0:1, 0:1], min_val=1, max_val=P * NCC // U - 2)
                        with sp.Fori(0, n) as i:
                            for u in range(U):
                                _, t = chunk_of(sp, i * U + u)
                                t = t.with_bounds(min_val=0, max_val=TA - C)
                                sp.wait_ge(mm_done, i * U + u + 1)
                                sp.sem_inc(s_tick, 1)
                                sp.dma_start(eas[:, u, :, :], ea[:, bass.ds(t, C), :]).then_inc(ea_got[u], 16)

                @block.vector
                def _(dve):
                    n = dve.value_load(turns[0:1, 0:1], min_val=1, max_val=P * NCC // U - 2)
                    with dve.Fori(0, n) as i:
                        for u in range(U):
                            b, t = chunk_of(dve, i * U + u)
                            t = t.with_bounds(min_val=0, max_val=TA - C)
                            b = b.with_bounds(min_val=0, max_val=NB - 1)
                            dve.wait_ge(mm_done, i * U + u + U - 1)
                            nc.vector.scalar_tensor_tensor(
                                out=onehot[:, u % 2, :, :],
                                in0=dst[:, bass.ds(t, C)].unsqueeze(2).to_broadcast([P, C, P]),
                                scalar=base[:, bass.ds(b, 1)],
                                in1=iota[:].unsqueeze(1).to_broadcast([P, C, P]),
                                op0=ALU.subtract, op1=ALU.is_equal).then_inc(hot_ready, 1)
                            dve.wait_ge(mm_done, i * U + u + U + 1)
                            dve.wait_ge(added, (i * U + u) + 1)
                            cols = acc[:, bass.ds(b * P, P)]
                            if l == 0:
                                nc.vector.tensor_tensor(eaT[:, bass.ds(b * P, P)], eaT[:, bass.ds(b * P, P)],
                                                        bank[2 + u % 2][0:EA1, 0:P], ALU.add)
                            nc.vector.tensor_tensor(cols, cols, bank[u % 2][:, 0:P], ALU.add).then_inc(added, 1)

                @block.tensor
                def _(pe):
                    n = pe.value_load(turns[0:1, 0:1], min_val=1, max_val=P * NCC // U - 2)
                    pe.sem_inc(mm_done, U)
                    pe.sem_inc(added, 1)
                    with pe.Fori(0, n) as i:
                        for u in range(U):
                            pe.wait_ge(hot_ready, i * U + u + 1)
                            if l == 0:
                                pe.wait_ge(ea_got[u], 16 * (i + 1))
                                for j in range(C):
                                    nc.tensor.matmul(bank[2 + u % 2][0:EA1, 0:P], eas[:, u, j, :], onehot[:, u % 2, j, :],
                                                     start=(j == 0), stop=(j == C - 1))
                            pe.wait_ge(got[u], G16 * (i + 1))
                            for j in range(C):
                                mm = nc.tensor.matmul(bank[u % 2][:, 0:P], rows_l[:, u * C + j, :],
                                                      onehot[:, u % 2, j, :], start=(j == 0), stop=(j == C - 1))
                            mm.then_inc(mm_done, 1)

            with ExitStack() as c2:
                def sm(name):
                    return ctx.enter_context(nc.semaphore(f"n{l}_{name}"))

                def tile(name, shape, dt=F32):
                    return c2.enter_context(nc.sbuf_tensor(f"n{l}_{name}", shape, dt))
                xd = tile("xd", [P, SB * P])
                y = tile("y", [P, SB * P])
                nodes = tile("nodes", [P, SB, D])
                resid = tile("resid", [P, SB, D])
                hrow = tile("hrow", [P, SB, ROW])
                stats = tile("stats", [P, SB, 6])
                mv = tile("mv", [P, SB, 2])
                rstd = tile("rstd", [P, SB])
                adst_t = tile("adst_t", [P, SB])
                self_e = tile("self_e", [P, SB])
                junk = tile("junk", [P, 2 * SB, D])
                SK = 32 if last else 16
                deg_ps, xd_ready, y_ps, y_ready, tr_ps, nodes_ready, stored = (
                    sm("deg_in_psum"), sm("xd_ready"), sm("y_in_psum"), sm("y_ready"), sm("rows_in_psum"),
                    sm("rows_ready"), sm("rows_stored"))
                y_done = sm("feat_updated")
                lin = sm("y_scaled")
                stat, x1T = sm("stats_step"), sm("x1T_ready")
                if last:
                    res_got, x1_ready, x1T_ps, h_ps, h_ready = (
                        sm("resid_got"), sm("x1_ready"), sm("x1T_in_psum"), sm("h_in_psum"), sm("h_ready"))
                    sq = sm("sqrt_ready")
                    hc, trc = sm("h_copied"), sm("rows_copied")
                block = c2.enter_context(nc.Block())
                tb = [(bank[4 + k // 4], (k % 4) * P) for k in range(SB)]
                tc_ = [(bank[6 + k // 4], (k % 4) * P) for k in range(SB)]
                slope = 0.01

                @block.tensor
                def _(pe):
                    with pe.Fori(0, NT) as i:
                        for g in range(2):
                            cols = eaT[:, bass.ds(i * (SB * P) + g * HB, HB)]
                            if g == 0:
                                pe.wait_ge(xd_ready, 2 * i + 1)
                            mm = nc.tensor.matmul(bank[g][:, 0:HB], sel[:], cols, start=True, stop=True)
                        mm.then_inc(deg_ps, 1)
                        for g in range(2):
                            at = bass.ds(i * (SB * P) + g * HB, HB)
                            if g == 0:
                                pe.wait_ge(y_ready, i + 1)
                            nc.tensor.matmul(bank[2 + g][:, 0:HB], w0[:, l, 0, :], acc[:, at], start=True, stop=False)
                            nc.tensor.matmul(bank[2 + g][:, 0:HB], w0e[:, l, :], eaT[:, at], start=False, stop=False)
                            if g == 0:
                                pe.wait_ge(xd_ready, 2 * i + 2 + 1)
                            mm = nc.tensor.matmul(bank[2 + g][:, 0:HB], w0[:, l, 1, :], xd[:, g * HB:(g + 1) * HB],
                                                  start=False, stop=True)
                        mm.then_inc(y_ps, 1)
                        pe.wait_ge(y_ready, i + 2)
                        pe.wait_ge(nodes_ready, i + 1)
                        for k in range(SB):
                            bk, o = tb[k]
                            tr = nc.tensor.transpose(bk[:, o:o + P], y[:, k * P:(k + 1) * P], ident[:])
                        tr.then_inc(tr_ps, 1)
                        if last:
                            pe.wait_ge(x1_ready, i + 1)
                            pe.wait_ge(x1T, i + 1)
                            for k in range(SB):
                                bk, o = tc_[k]
                                tr = nc.tensor.transpose(bk[:, o:o + P], nodes[:, k, :], ident[:])
                            tr.then_inc(x1T_ps, 1)
                            pe.wait_ge(x1T, i + 2)
                            for k in range(SB):
                                bk, o = tb[k]
                                mm = nc.tensor.matmul(bk[:, o:o + P], y[:, k * P:(k + 1) * P], w1[:], start=True, stop=True)
                            mm.then_inc(h_ps, 1)

                @block.vector
                def _(dve):
                    nc.vector.memset(hrow[:, :, D + 1:ROW], 0.0)
                    dve.sem_inc(xd_ready, 1)
                    dve.sem_inc(y_ready, 1)
                    with dve.Fori(0, NT) as i:
                        for g in range(2):
                            at = bass.ds(i * (SB * P) + g * HB, HB)
                            if g == 0:
                                dve.wait_ge(deg_ps, i + 1)
                                dve.wait_ge(y_done, i + 1)
                            nc.vector.tensor_tensor(xd[:, g * HB:(g + 1) * HB], feat[:, at], bank[g][:, 0:HB],
                                                    ALU.mult).then_inc(xd_ready, 1)
                        dve.wait_ge(lin, i + 1)
                        for g in range(2):
                            mx = nc.vector.scalar_tensor_tensor(
                                out=y[:, g * HB:(g + 1) * HB], in0=bank[2 + g][:, 0:HB], scalar=slope,
                                in1=feat[:, bass.ds(i * (SB * P) + g * HB, HB)], op0=ALU.mult, op1=ALU.max)
                            mx.then_inc(stat, 1)
                        if last:
                            dve.wait_ge(stat, 5 * i + 2)
                            mx = nc.vector.scalar_tensor_tensor(out=y[:], in0=y[:], scalar=slope, in1=y[:],
                                                                op0=ALU.mult, op1=ALU.max)
                            mx.then_inc(y_ready, 1)
                        else:
                            dve.wait_ge(stat, 2 * i + 2)
                            dve.sem_inc(s_tick, 1)
                            nc.vector.tensor_copy(feat[:, bass.ds(i * (SB * P), SB * P)], y[:]).then_inc(y_ready, 1)
                        if last:
                            dve.wait_ge(trc, i + 1)
                            dve.wait_ge(res_got, 16 * (i + 1))
                            nc.vector.tensor_tensor(resid[:], resid[:], nodes[:], ALU.add).then_inc(stat, 1)
                            dve.wait_ge(stat, 5 * i + 3)
                            for k in range(SB):
                                bn = nc.vector.bn_stats(out=stats[:, k, :], in_=resid[:, k, :])
                            bn.then_inc(stat, 1)
                            dve.wait_ge(stat, 5 * i + 4)
                            dve.sem_inc(s_tick, 1)
                            for k in range(SB):
                                bn = nc.vector.bn_aggr(out=mv[:, k, :], in_=stats[:, k, :])
                            bn.then_inc(stat, 1)
                            dve.wait_ge(sq, i + 1)
                            nc.vector.reciprocal(rstd[:], rstd[:]).then_inc(hc, 1)
                            dve.wait_ge(hc, 3 * i + 1)
                            for k in range(SB):
                                nm = nc.vector.tensor_scalar(nodes[:, k, :], resid[:, k, :], mv[:, k, 0:1],
                                                             rstd[:, k:k + 1], ALU.subtract, ALU.mult)
                            nm.then_inc(x1_ready, 1)
                            dve.wait_ge(h_ready, i + 1)
                            for k in range(SB):
                                nc.vector.tensor_tensor_reduce(
                                    out=junk[:, k, :], in0=hrow[:, k, 0:D], in1=att_row[:, 0, :], scale=1.0, scalar=0.0,
                                    op0=ALU.mult, op1=ALU.add, accum_out=hrow[:, k, D:D + 1])
                                tt = nc.vector.tensor_tensor_reduce(
                                    out=junk[:, SB + k, :], in0=hrow[:, k, 0:D], in1=att_row[:, 1, :], scale=1.0, scalar=0.0,
                                    op0=ALU.mult, op1=ALU.add, accum_out=adst_t[:, k:k + 1])
                            tt.then_inc(hc, 1)
                            dve.wait_ge(hc, 3 * i + 2)
                            dve.sem_inc(s_tick, 1)
                            nc.vector.tensor_copy(a_dst[:, bass.ds(i * SB, SB)], adst_t[:])
                            nc.vector.tensor_copy(acc[:, bass.ds(i * (SB * P), SB * P)].rearrange("p (k f) -> p k f", f=D),
                                                  hrow[:, :, 0:D])
                            nc.vector.tensor_tensor(self_e[:], adst_t[:], hrow[:, :, D], ALU.add).then_inc(hc, 1)
                            dve.wait_ge(hc, 3 * i + 3)
                            dve.sem_inc(s_tick, 1)
                            nc.vector.scalar_tensor_tensor(out=peak[:, bass.ds(i * SB, SB)], in0=self_e[:], scalar=0.2,
                                                           in1=self_e[:], op0=ALU.mult, op1=ALU.max).then_inc(s_dve, 1)

                @block.scalar
                def _(act):
                    act.sem_inc(y_done, 1)
                    act.sem_inc(nodes_ready, 1)
                    act.sem_inc(x1T, 1)
                    with act.Fori(0, NT) as i:
                        act.wait_ge(y_ps, i + 1)
                        act.sem_inc(s_tick, 1)
                        for g in range(2):
                            cp = nc.scalar.copy(feat[:, bass.ds(i * (SB * P) + g * HB, HB)], bank[2 + g][:, 0:HB])
                        cp.then_inc(lin, 1)
                        act.wait_ge(tr_ps, i + 1)
                        act.wait_ge(stored, SK * (i + 1))
                        act.sem_inc(s_tick, 1)
                        nc.scalar.copy(nodes[:, 0:4, :], bank[4][:, 0:512].rearrange("p (k f) -> p k f", f=D))
                        cp = nc.scalar.copy(nodes[:, 4:SB, :], bank[5][:, 0:3 * P].rearrange("p (k f) -> p k f", f=D))
                        if not last:
                            cp.then_inc(nodes_ready, 1)
                            act.sem_inc(y_done, 1)
                        else:
                            cp.then_inc(trc, 1)
                            act.wait_ge(stat, 5 * i + 5)
                            nc.scalar.activation(rstd[:], mv[:, :, 1], ACT.Sqrt, bias=eps[:, 0:1], scale=1.0).then_inc(sq, 1)
                            act.wait_ge(x1T_ps, i + 1)
                            act.sem_inc(s_tick, 1)
                            nc.scalar.copy(y[:, 0:512], bank[6][:, 0:512])
                            nc.scalar.copy(y[:, 512:SB * P], bank[7][:, 0:3 * P]).then_inc(x1T, 1)
                            act.wait_ge(h_ps, i + 1)
                            act.sem_inc(s_tick, 1)
                            nc.scalar.copy(hrow[:, 0:4, 0:D], bank[4][:, 0:512].rearrange("p (k f) -> p k f", f=D))
                            cp = nc.scalar.copy(hrow[:, 4:SB, 0:D], bank[5][:, 0:3 * P].rearrange("p (k f) -> p k f", f=D))
                            cp.then_inc(h_ready, 1)
                            act.wait_ge(h_ready, i + 1)
                            act.sem_inc(nodes_ready, 1)
                            act.sem_inc(y_done, 1)

                @block.sync
                def _(sp):
                    sp.sem_inc(stored, SK)
                    with sp.Fori(0, NT) as i:
                        turn = bass.ds(i * SB, SB)
                        if not last:
                            sp.wait_ge(nodes_ready, i + 2)
                            sp.sem_inc(s_tick, 1)
                            sp.dma_start(table[l + 1].rearrange("(k p) f -> p k f", p=P)[:, turn, :],
                                         nodes[:]).then_inc(stored, 16)
                        else:
                            sp.dma_start(resid[:], x.rearrange("(k p) f -> p k f", p=P)[:, turn, :]).then_inc(res_got, 16)
                            sp.wait_ge(x1_ready, i + 1)
                            sp.sem_inc(s_tick, 1)
                            sp.dma_start(x1_dram.rearrange("(k p) f -> p k f", p=P)[:, turn, :],
                                         nodes[:]).then_inc(stored, 16)
                            sp.wait_ge(hc, 3 * i + 2)
                            sp.sem_inc(s_tick, 1)
                            sp.dma_start(table_h.rearrange("(k p) f -> p k f", p=P)[:, turn, :],
                                         hrow[:]).then_inc(stored, 16)
                    sp.wait_ge(stored, SK * (NT + 1))

            if not last:
                with nc.Block() as block:
                    @block.vector
                    def _(dve):
                        nc.vector.memset(acc[:], 0.0)

        K = 6
        with ExitStack() as c3:
            def sm(name):
                return ctx.enter_context(nc.semaphore(f"gat_{name}"))

            def ring(name, shape, dt=F32):
                return c3.enter_context(nc.sbuf_tensor(f"gat_{name}", shape, dt))
            idx = ring("idx", [P, U, C], U32)
            rows = ring("rows", [P, U, C, ROW])
            other = ring("other", [P, 2, C, P])
            masked = ring("masked", [P, 2, C, P])
            eT = ring("eT", [P, 2, C * P])
            wT = ring("wT", [P, 2, C * P])
            wgt = ring("wgt", [P, 2, C, P])
            ad, top, mtop, fall, scale, wsum = (ring(f"s_{k}", [P, U]) for k in ("ad", "top", "mtop", "fall", "scale", "wsum"))
            idx_ready = [sm(f"idx_ready{u}") for u in range(U)]
            got = row_got[3]
            other_ready, masked_ready, mT_ps, link, max_ready, z_ready, e_ready, w_ready, w_ps, wgt_ready, mm_done, added = (
                sm("mask_ready"), sm("masked_ready"), sm("maskedT_in_psum"), sm("vector_link"), sm("max_ready"),
                sm("z_ready"), sm("e_ready"), sm("weightsT_ready"), sm("weights_in_psum"), sm("weights_ready"), sm("sum_ready"),
                sm("sum_added"))
            block = c3.enter_context(nc.Block())

            @block.gpsimd
            def _(pool):
                n = pool.value_load(turns[0:1, 0:1], min_val=1, max_val=P * NCC // U - 2)
                with pool.Fori(0, n) as i:
                    for u in range(U):
                        pool.wait_ge(idx_ready[u], i + 1)
                        pool.sem_inc(s_tick, 1)
                        for j in range(C):
                            pool.indirect_dma_start(rows[:, u, j, :], None, table_h,
                                                    bass.IndirectOffsetOnAxis(ap=idx[:, u, j:j + 1], axis=0)
                                                    ).then_inc(got[u], 16)

            @block.scalar
            def _(act):
                n = act.value_load(turns[0:1, 0:1], min_val=1, max_val=P * NCC // U - 2)

                def fetch(i, u):
                    _, t = chunk_of(act, i * U + u)
                    t = t.with_bounds(min_val=0, max_val=TA - C)
                    nc.scalar.copy(idx[:, u, :], src[:, bass.ds(t, C)]).then_inc(idx_ready[u], 1)

                def weigh(s, u):
                    act.wait_ge(mT_ps, s + 3)
                    act.wait_ge(link, s * K + 2)
                    act.wait_ge(w_ps, s + 1)
                    nc.scalar.activation(eT[:, u % 2, :], bank[u % 2][:, 0:C * P], ACT.Identity,
                                         bias=ad[:, u:u + 1], scale=1.0).then_inc(z_ready, 1)
                    act.wait_ge(max_ready, s + 1)
                    nc.scalar.activation(scale[:, u:u + 1], fall[:, u:u + 1], ACT.Exp)
                    act.wait_ge(e_ready, s + 1)
                    nc.scalar.activation(wT[:, u % 2, :], eT[:, u % 2, :], ACT.Exp, bias=mtop[:, u:u + 1],
                                         scale=1.0, accum_out=wsum[:, u:u + 1]).then_inc(w_ready, 1)

                def keep(s, u):
                    act.wait_ge(w_ps, s + 3)
                    act.sem_inc(s_tick, 1)
                    act.wait_ge(mm_done, s + U - 1)
                    nc.scalar.copy(wgt[:, u % 2, :, :], bank[2 + u % 2][:, 0:C * P].rearrange("p (j d) -> p j d", d=P)
                                   ).then_inc(wgt_ready, 1)

                for u in range(U):
                    fetch(0, u)
                with act.Fori(0, n) as i:
                    for ph in range(U + 2):
                        if 1 <= ph <= U:
                            weigh(i * U + ph - 1, ph - 1)
                            keep(i * U + ph - 1, ph - 1)
                        if ph >= 2:
                            act.wait_ge(mm_done, i * U + ph - 2 + U + 1)
                            act.sem_inc(s_tick, 1)
                            fetch(i + 1, ph - 2)

            @block.vector
            def _(dve):
                n = dve.value_load(turns[0:1, 0:1], min_val=1, max_val=P * NCC // U - 2)
                with dve.Fori(0, n) as i:
                    col = [None] * U

                    def mask(s, u):
                        b, t = chunk_of(dve, s)
                        t = t.with_bounds(min_val=0, max_val=TA - C)
                        col[u] = b.with_bounds(min_val=0, max_val=NB - 1)
                        nc.vector.scalar_tensor_tensor(
                            out=other[:, u % 2, :, :],
                            in0=dst[:, bass.ds(t, C)].unsqueeze(2).to_broadcast([P, C, P]),
                            scalar=base[:, bass.ds(col[u], 1)],
                            in1=iota[:].unsqueeze(1).to_broadcast([P, C, P]),
                            op0=ALU.subtract, op1=ALU.not_equal).then_inc(other_ready, 1)
                        dve.wait_ge(other_ready, s + 1)
                        dve.wait_ge(got[u], G16 * (i + 1))
                        dve.wait_ge(mT_ps, s + 1)
                        nc.vector.scalar_tensor_tensor(
                            out=masked[:, u % 2, :, :], in0=other[:, u % 2, :, :], scalar=NEG,
                            in1=rows[:, u, :, D:D + 1].to_broadcast([P, C, P]), op0=ALU.mult, op1=ALU.add
                        ).then_inc(masked_ready, 1)

                    def maximum(s, u):
                        c, a, m = bass.ds(col[u], 1), ad[:, u:u + 1], top[:, u:u + 1]
                        dve.wait_ge(mT_ps, s + 3)
                        nc.vector.tensor_reduce(m, bank[u % 2][:, 0:C * P], AX.X, ALU.max).then_inc(link, 1)
                        nc.vector.tensor_copy(a, a_dst[:, c]).then_inc(link, 1)
                        dve.wait_ge(link, s * K + 2)
                        nc.vector.tensor_tensor(m, m, a, ALU.add).then_inc(link, 1)
                        dve.wait_ge(link, s * K + 3)
                        nc.vector.scalar_tensor_tensor(out=m, in0=m, scalar=0.2, in1=m, op0=ALU.mult, op1=ALU.max
                                                       ).then_inc(link, 1)
                        dve.wait_ge(link, s * K + 4)
                        nc.vector.tensor_tensor(m, m, peak[:, c], ALU.max).then_inc(link, 1)
                        dve.wait_ge(link, s * K + 5)
                        nc.vector.tensor_scalar(mtop[:, u:u + 1], m, -1.0, None, ALU.mult)
                        nc.vector.tensor_tensor(fall[:, u:u + 1], peak[:, c], m, ALU.subtract).then_inc(max_ready, 1)
                        dve.wait_ge(max_ready, s + 1)
                        dve.sem_inc(s_tick, 1)
                        nc.vector.tensor_copy(peak[:, c], m).then_inc(link, 1)
                        dve.wait_ge(z_ready, s + 3)
                        nc.vector.scalar_tensor_tensor(out=eT[:, u % 2, :], in0=eT[:, u % 2, :], scalar=0.2,
                                                       in1=eT[:, u % 2, :], op0=ALU.mult, op1=ALU.max).then_inc(e_ready, 1)

                    def add(s, u):
                        c = bass.ds(col[u], 1)
                        dve.wait_ge(mm_done, s + U + 1)
                        dve.wait_ge(added, s + 2)
                        nc.vector.scalar_tensor_tensor(out=denom[:, c], in0=denom[:, c], scalar=scale[:, u:u + 1],
                                                       in1=wsum[:, u:u + 1], op0=ALU.mult, op1=ALU.add)
                        cols = acc[:, bass.ds(col[u] * P, P)]
                        nc.vector.scalar_tensor_tensor(out=cols, in0=cols, scalar=scale[:, u:u + 1],
                                                       in1=bank[4 + u % 2][:, 0:P], op0=ALU.mult, op1=ALU.add
                                                       ).then_inc(added, 1)

                    for ph in range(U + 2):
                        if ph < U:
                            mask(i * U + ph, ph)
                        if 1 <= ph <= U:
                            maximum(i * U + ph - 1, ph - 1)
                        if ph >= 2:
                            add(i * U + ph - 2, ph - 2)

            @block.tensor
            def _(pe):
                n = pe.value_load(turns[0:1, 0:1], min_val=1, max_val=P * NCC // U - 2)
                pe.sem_inc(mm_done, U)
                for s2 in (added, w_ps, mT_ps, z_ready, wgt_ready):
                    pe.sem_inc(s2, 2)

                def turn_masked(s, u):
                    pe.wait_ge(masked_ready, s + 1)
                    pe.wait_ge(z_ready, s + 1)
                    for j in range(C):
                        tr = nc.tensor.transpose(bank[u % 2][:, j * P:(j + 1) * P], masked[:, u % 2, j, :], ident[:])
                    tr.then_inc(mT_ps, 1)

                def turn_weights(s, u):
                    pe.wait_ge(w_ready, s + 1)
                    pe.wait_ge(wgt_ready, s + 1)
                    for j in range(C):
                        tr = nc.tensor.transpose(bank[2 + u % 2][:, j * P:(j + 1) * P],
                                                 wT[:, u % 2, j * P:(j + 1) * P], ident[:])
                    tr.then_inc(w_ps, 1)

                def product(s, u):
                    pe.wait_ge(wgt_ready, s + 3)
                    pe.wait_ge(added, s + 1)
                    for j in range(C):
                        mm = nc.tensor.matmul(bank[4 + u % 2][:, 0:P], wgt[:, u % 2, j, :], rows[:, u, j, 0:D],
                                              start=(j == 0), stop=(j == C - 1))
                    mm.then_inc(mm_done, 1)

                with pe.Fori(0, n) as i:
                    for ph in range(U + 2):
                        if ph < U:
                            turn_masked(i * U + ph, ph)
                        if 1 <= ph <= U:
                            turn_weights(i * U + ph - 1, ph - 1)
                        if ph >= 2:
                            product(i * U + ph - 2, ph - 2)

        with ExitStack() as c4:
            def sm(name):
                return ctx.enter_context(nc.semaphore(f"out_{name}"))

            def tile(name, shape, dt=F32):
                return c4.enter_context(nc.sbuf_tensor(f"out_{name}", shape, dt))
            nodes = tile("nodes", [P, SB, D])
            resid = tile("resid", [P, SB, D])
            stats = tile("stats", [P, SB, 6])
            mv = tile("mv", [P, SB, 2])
            rstd = tile("rstd", [P, SB])
            res_got, lnk, sq, rows_ready, stored = sm("resid_got"), sm("link"), sm("sqrt"), sm("rows_ready"), sm("stored")
            block = c4.enter_context(nc.Block())
            FULL = NT - 1
            NL = 6

            @block.sync
            def _(sp):
                sp.sem_inc(stored, 16)
                x1v = x1_dram.rearrange("(k p) f -> p k f", p=P)
                with sp.Fori(0, NT) as i:
                    sp.wait_ge(rows_ready, i + 1)
                    sp.sem_inc(s_tick, 1)
                    sp.dma_start(resid[:], x1v[:, bass.ds(i * SB, SB), :]).then_inc(res_got, 16)

            @block.scalar
            def _(act):
                outv = out[0:FULL * SB * P, :].rearrange("(k p) f -> p k f", p=P)
                with act.Fori(0, FULL) as i:
                    act.wait_ge(lnk, NL * i + NL - 1)
                    act.sem_inc(s_tick, 1)
                    nc.scalar.activation(rstd[:], mv[:, :, 1], ACT.Sqrt, bias=eps[:, 0:1], scale=1.0).then_inc(sq, 1)
                    act.wait_ge(rows_ready, i + 2)
                    act.dma_start(outv[:, bass.ds(i * SB, SB), :], nodes[:]).then_inc(stored, 16)
                act.wait_ge(lnk, NL * FULL + NL - 1)
                nc.scalar.activation(rstd[:], mv[:, :, 1], ACT.Sqrt, bias=eps[:, 0:1], scale=1.0).then_inc(sq, 1)
                act.wait_ge(rows_ready, NT + 1)
                rest = out[FULL * SB * P:FULL * SB * P + (SB - 1) * P, :].rearrange("(k p) f -> p k f", p=P)
                act.dma_start(rest, nodes[:, 0:SB - 1, :]).then_inc(stored, 16)
                act.dma_start(out[(NB - 1) * P:n_nodes, :], nodes[0:LAST, SB - 1, :]).then_inc(stored, 16)
                act.wait_ge(stored, 16 * (1 + FULL + 2))

            @block.vector
            def _(dve):
                dve.sem_inc(rows_ready, 1)
                nc.vector.reciprocal(denom[:], denom[:]).then_inc(s_dve, 1)
                dve.wait_ge(s_dve, 1 + NT + 1)
                with dve.Fori(0, NT) as i:
                    dve.wait_ge(res_got, 16 * (i + 1))
                    nc.vector.tensor_tensor(resid[:], resid[:], bias_row[:].unsqueeze(1).to_broadcast([P, SB, D]),
                                            ALU.add).then_inc(lnk, 1)
                    dve.wait_ge(lnk, NL * i + 1)
                    for k in range(SB):
                        a = nc.vector.scalar_tensor_tensor(
                            out=resid[:, k, :], in0=acc[:, bass.ds(i * (SB * P) + k * P, P)],
                            scalar=denom[:, bass.ds(i * SB + k, 1)], in1=resid[:, k, :], op0=ALU.mult, op1=ALU.add)
                    a.then_inc(lnk, 1)
                    dve.wait_ge(lnk, NL * i + 2)
                    for k in range(SB):
                        bn = nc.vector.bn_stats(out=stats[:, k, :], in_=resid[:, k, :])
                    bn.then_inc(lnk, 1)
                    dve.wait_ge(lnk, NL * i + 3)
                    dve.sem_inc(s_tick, 1)
                    for k in range(SB):
                        bn = nc.vector.bn_aggr(out=mv[:, k, :], in_=stats[:, k, :])
                    bn.then_inc(lnk, 2)
                    dve.wait_ge(sq, i + 1)
                    nc.vector.reciprocal(rstd[:], rstd[:]).then_inc(lnk, 1)
                    dve.wait_ge(lnk, NL * i + NL)
                    dve.wait_ge(stored, 16 * (i + 1))
                    for k in range(SB):
                        nm = nc.vector.tensor_scalar(nodes[:, k, :], resid[:, k, :], mv[:, k, 0:1],
                                                     rstd[:, k:k + 1], ALU.subtract, ALU.mult)
                    nm.then_inc(rows_ready, 1)


def kernel(x, src, dst, edge_attr_32, L0_gnn_Wm, L0_gnn_bm, L1_gnn_W, L1_gnn_att_src, L1_gnn_att_dst, L1_gnn_bias):
    import concourse.bacc as bacc
    from concourse.bass_utils import run_bass_kernel_spmd as run

    x, src, dst, ea = (np.asarray(a) for a in (x, src, dst, edge_attr_32))
    n, e = x.shape[0], src.shape[0]
    nb, tiles, ta, _ = shapes(n, e)
    xp = np.concatenate([x, np.zeros((nb * P - n, D), x.dtype)])
    src_p = np.concatenate([src, np.zeros(ta * P - e, src.dtype)]).reshape(ta, P)
    dst_p = np.concatenate([dst, np.full(ta * P - e, NO_NODE, dst.dtype)]).reshape(ta, P)
    ea_p = np.concatenate([ea, np.zeros((ta * P - e, EA), ea.dtype)])
    ea_p = np.concatenate([ea_p, np.ones((ta * P, 1), ea.dtype)], axis=1).reshape(ta, P, EA1).transpose(1, 0, 2)
    W0 = np.concatenate([np.asarray(L0_gnn_Wm).transpose(0, 2, 1), np.asarray(L0_gnn_bm)[:, None, :]], axis=1)
    arrays = {
        "in_x": xp, "in_xT": xp.T, "in_srcT": src_p.T, "in_dstT": dst_p.T, "in_dst_rows": dst_p, "in_ea": ea_p,
        "in_W0": W0, "in_W1": np.asarray(L1_gnn_W),
        "in_att": np.stack([np.asarray(L1_gnn_att_src), np.asarray(L1_gnn_att_dst)]),
        "in_bias": np.asarray(L1_gnn_bias)[None, :],
    }
    arrays = {k: np.ascontiguousarray(a) for k, a in arrays.items()}
    nc = bacc.Bacc("TRN2", target_bir_lowering=False, num_devices=1)
    args = [nc.dram_tensor(k, a.shape, mybir.dt.from_np(a.dtype), kind="ExternalInput").ap() for k, a in arrays.items()]
    out = nc.dram_tensor("out", [n, D], F32, kind="ExternalOutput").ap()
    build(nc, *args, out)
    return run(nc, [arrays], core_ids=[0]).results[0]["out"]
```

```python
from contextlib import ExitStack

import numpy as np
import concourse.bass as bass
from concourse import mybir

F32 = mybir.dt.float32
F16 = mybir.dt.float16
I32 = mybir.dt.int32
U32 = mybir.dt.uint32
ALU = mybir.AluOpType
ACT = mybir.ActivationFunctionType
AX = mybir.AxisListType

P = 128
D = 128
EA = 32
EA1 = EA + 1
C = 3
U = 4
SB = 7
HB = SB * P // 2
ROW = D + 4
W = 16
GT = 3
GP = P // W
QP = 4
INFO = 3
EXPONENT = 0x7F800000
NO_NODE = 8191
NEG = -1.0e30
EPS = 1e-5
SPREAD = 10.0


def shapes(n_nodes, n_edges):
    nb = -(-n_nodes // P)
    tiles = -(-n_edges // P)
    ta = -(-(tiles + C) // 8) * 8
    most = nb * -(-tiles // C) + 2 * U
    nc_cols = -(-most // P)
    return nb, tiles, ta, nc_cols


def build(nc, x, xT, srcT, dstT, src_line, dst_line, ea, W0, W1, att, bias, out):
    n_nodes = out.shape[0]
    NB = x.shape[0] // P
    NP = NB * P
    TA = srcT.shape[1]
    NT = NB // SB
    LAST = n_nodes - (NB - 1) * P
    NCC = shapes(n_nodes, TA * P)[3]
    RJ = 8
    RP = TA // RJ
    BIG_T = float(TA)
    EE = ea.shape[0]
    RW = EE // P
    assert RW * P == EE and EE >= (TA + GT) * P and dst_line.shape[0] == EE + 1
    dst_rows = dst_line[0:TA * P].rearrange("(t e) -> t e", e=P)
    ea_tiles = ea[0:TA * P, :].rearrange("(t p) f -> p t f", p=P)
    assert NB % SB == 0 and TA < 1024 and NB <= P

    table = [x, nc.dram_tensor("table_1", [NP, D], F32).ap(), nc.dram_tensor("table_2", [NP, D], F32).ap()]
    table_h = nc.dram_tensor("table_h", [NP, ROW], F32).ap()
    x1_dram = nc.dram_tensor("x1_rows", [NP, D], F32).ap()
    lohi_dram = nc.dram_tensor("tile_lo_hi", [2, TA], F32).ap()
    NG = NP // W
    GR = 4
    GQ = NG // GR
    NPAN = NG // GP
    HC = NB * W
    HA = (NB + 1) // 2
    PC = 7
    PH = NB // PC
    assert NG == GR * GQ and NPAN * GP == NG and NPAN == NB and NPAN % (2 * QP) == 1 and HA * W <= 512 and PC * PH == NB and GQ <= P
    group_dram = nc.dram_tensor("group_list", [NG], I32).ap()
    counts = nc.dram_tensor("counts", [NPAN, P, NB * P], F16).ap()
    info_dram = nc.dram_tensor("edge_info", [EE, INFO], F32).ap()
    chunk_dram = nc.dram_tensor("chunk_list", [P * NCC], I32).ap()

    with ExitStack() as ctx:
        def sb(name, shape, dt=F32):
            return ctx.enter_context(nc.sbuf_tensor(name, shape, dt))

        def ps(name, shape):
            return ctx.enter_context(nc.psum_tensor(name, shape, F32))

        def sem(name):
            return ctx.enter_context(nc.semaphore(name))

        shared = sb("shared", [P, P * NCC])
        chunks = shared[96:97, :].bitcast(I32)
        eaT = shared[0:EA1, 0:NP]
        turns = sb("turns", [1, 1], I32)
        fast = sb("fast", [1, 1], I32)
        groups = sb("groups", [1, NG], I32)
        gbase = sb("gbase", [P, NG])
        gend = sb("gend", [P, NG])
        src = sb("src", [P, TA], I32)
        unit = sb("unit", [P, 4])
        dst = sb("dst", [P, TA])
        feat = sb("feat", [P, NP])
        acc = sb("acc", [P, NP])
        ident = sb("ident", [P, P])
        ones = sb("ones", [3, P])
        iota = sb("iota", [P, P])
        base = sb("base", [P, NB])
        w0 = sb("w0", [P, 3, 2, D])
        w0e = sb("w0e", [EA1, 3, D])
        sel = sb("sel", [EA1, P])
        w1 = sb("w1", [P, D])
        att_row = sb("att_row", [P, 2, D])
        bias_row = sb("bias_row", [P, D])
        a_src = sb("a_src", [P, NB])
        a_dst = sb("a_dst", [P, NB])
        tops = sb("tops", [P, 3])
        short = sb("short", [1, 1], I32)
        peak = sb("peak", [P, NB])
        denom = sb("denom", [P, NB])
        eps = sb("eps", [P, 1])
        bank = [ps(f"bank{i}", [P, 512]) for i in range(8)]

        s_in = sem("inputs_loaded")
        s_tick = sem("wait_carrier")
        s_const = sem("constants_ready")
        s_dve = sem("vector_step")

        idx_ready = [sem(f"idx_ready{u}") for u in range(U)]
        row_got = [sem(f"row_got{u}") for u in range(U)]
        ES = 4
        ea_got = [sem(f"ea_got{k}") for k in range(max(ES, U))]
        G16 = 16 * C

        NIN = 16
        with ExitStack() as c0:
            def sb0(name, shape, dt=F32):
                return c0.enter_context(nc.sbuf_tensor(name, shape, dt))
            dr = sb0("dst_rows_sb", [RP, RJ, P], I32)
            di = sb0("dst_int", [P, TA], I32)
            lohi = sb0("lohi", [RP, 2, RJ])
            lo_b = sb0("lo_b", [GQ, TA])
            hi_b = sb0("hi_b", [GQ, TA])
            below, hit, t1, t2 = (acc[0:GQ, k * TA:(k + 1) * TA] for k in range(4))
            prod = acc[0:GQ, 4 * TA:6 * TA].rearrange("p (k t) -> p k t", k=2)
            glo = sb0("glo", [GQ, GR])
            ghi = sb0("ghi", [GQ, GR])
            gt = sb0("gt", [GQ, 4, GR])
            gti = sb0("gti", [GQ, GR], I32)
            dn = sb0("dst_line_sb", [P, RW + 1], I32)
            sn = sb0("src_line_sb", [P, RW], I32)
            parts = sb0("parts", [P, 2, RW], I32)
            info = sb0("info", [P, RW, INFO])
            worst = sb0("worst", [P, 1])
            edge_rows = sb0("edge_rows", [GQ, 2, GR, P], I32)
            which = sb0("which", [GQ, 2, GR])
            whichi = sb0("whichi", [GQ, 2, GR], U32)
            under = sb0("under", [GQ, 2, GR, P])
            num = sb0("num", [GQ, 4, GR])
            s_line, s_info, s_which, s_rows = sem("lines_loaded"), sem("info_ready"), sem("tiles_found"), sem("edge_rows_in")
            blk = sb0("blk", [NB, 2])
            rng = sb0("rng", [NB, 8])
            rngi = sb0("rngi", [NB, 2], I32)
            tri = sb0("tri", [NB, NB + 1])
            nbc = sb0("nbc", [NB, 2, P])
            cum = sb0("cum", [P, NB + 1])
            q = sb0("q", [P, NB])
            dq = sb0("dq", [P, NB])
            sidx = sb0("sidx", [P, NCC])
            step = sb0("step", [P, NCC])
            v = sb0("v", [P, NCC])
            vi = sb0("vi", [P, NCC], I32)
            turns_i = sb0("turns_i", [P, 2], I32)
            s_lohi, s_back, s_list, s_rng, s_cum = (sem("lohi_stored"), sem("lohi_back"), sem("list_stored"),
                                                    sem("ranges_ready"), sem("cum_ready"))
            s_ones = sem("iotas_ready")
            s_c = sem("stage0_step")
            block = c0.enter_context(nc.Block())

            @block.sync
            def _(sp):
                sp.dma_start(dr[:], dst_rows.rearrange("(p j) e -> p j e", j=RJ)).then_inc(s_back, 16)
                line = dst_line[0:EE]
                sp.dma_start(dn[:, 0:RW], line.rearrange("(p e) -> p e", e=RW)).then_inc(s_line, 16)
                with nc.allow_non_contiguous_dma(reason="each partition's next dst"):
                    sp.dma_start(dn[:, RW:RW + 1], dst_line[1:EE + 1].rearrange("(p e) -> p e", e=RW)[:, RW - 1:RW]).then_inc(s_line, 16)
                sp.dma_start(sn[:], src_line.rearrange("(p e) -> p e", e=RW)).then_inc(s_line, 16)
                sp.dma_start(di[:], dstT).then_inc(s_in, 16)
                sp.dma_start(src[:], srcT).then_inc(s_in, 16)
                sp.dma_start(feat[:], xT).then_inc(s_in, 16)
                for l in range(3):
                    sp.dma_start(w0[:, l, :, :], W0[l, 0:2 * D, :].rearrange("(k p) f -> p k f", p=P)).then_inc(s_in, 16)
                    sp.dma_start(w0e[:, l, :], W0[l, 2 * D:2 * D + EA1, :]).then_inc(s_in, 16)
                sp.dma_start(w1[:], W1).then_inc(s_in, 16)
                for k in range(2):
                    sp.dma_start(att_row[:, k, :], att[k:k + 1, :].partition_broadcast(P)).then_inc(s_in, 16)
                sp.dma_start(bias_row[:], bias.partition_broadcast(P)).then_inc(s_in, 16)
                sp.wait_ge(s_c, 2)
                for k in range(2):
                    sp.dma_start(lohi_dram[k].rearrange("(p j) -> p j", j=RJ), lohi[:, k, :]).then_inc(s_lohi, 16)
                sp.wait_ge(s_lohi, 32)
                sp.dma_start(lo_b[:], lohi_dram[0:1, :].partition_broadcast(GQ)).then_inc(s_back, 16)
                sp.dma_start(hi_b[:], lohi_dram[1:2, :].partition_broadcast(GQ)).then_inc(s_back, 16)
                sp.wait_ge(s_info, 2)
                sp.dma_start(info_dram.rearrange("(p e) f -> p (e f)", e=RW), info[:].rearrange("p e f -> p (e f)")).then_inc(s_in, 16)
                sp.wait_ge(s_list, 1)
                sp.dma_start(chunk_dram.rearrange("(p c) -> p c", c=NCC), vi[:]).then_inc(s_lohi, 16)
                with nc.allow_non_contiguous_dma(reason="one tile number of each group"):
                    sp.dma_start(group_dram.rearrange("(r p) -> p r", p=GQ), gti[:]).then_inc(s_lohi, 16)
                sp.wait_ge(s_lohi, 64)
                sp.dma_start(groups[:], group_dram.rearrange("(a n) -> a n", a=1)).then_inc(s_in, 16)
                sp.dma_start(chunks, chunk_dram.rearrange("(a n) -> a n", a=1)).then_inc(s_in, 16)
                sp.wait_ge(s_in, 16 * NIN)

            @block.gpsimd
            def _(pool):
                nc.gpsimd.memset(tri[:], 1.0).then_inc(s_tick, 1)
                nc.gpsimd.memset(ident[:], 0.0).then_inc(s_tick, 1)
                nc.gpsimd.memset(sel[:], 0.0).then_inc(s_tick, 1)
                nc.gpsimd.iota(iota[:], [[1, P]], channel_multiplier=0, allow_small_or_imprecise_dtypes=True).then_inc(s_ones, 1)
                nc.gpsimd.iota(base[:], [[P, NB]], channel_multiplier=0, allow_small_or_imprecise_dtypes=True).then_inc(s_ones, 1)
                nc.gpsimd.iota(blk[:], [[P - 1, 2]], channel_multiplier=P, allow_small_or_imprecise_dtypes=True).then_inc(s_ones, 1)
                nc.gpsimd.iota(t1, [[1, TA]], base=1, channel_multiplier=0, allow_small_or_imprecise_dtypes=True).then_inc(s_ones, 1)
                nc.gpsimd.iota(t2, [[-1, TA]], base=TA, channel_multiplier=0, allow_small_or_imprecise_dtypes=True).then_inc(s_ones, 1)
                nc.gpsimd.iota(glo[:], [[W * GQ, GR]], channel_multiplier=W, allow_small_or_imprecise_dtypes=True).then_inc(s_ones, 1)
                nc.gpsimd.iota(ghi[:], [[W * GQ, GR]], base=W - 1, channel_multiplier=W, allow_small_or_imprecise_dtypes=True).then_inc(s_ones, 1)
                nc.gpsimd.iota(gbase[:], [[W, NG]], channel_multiplier=0, allow_small_or_imprecise_dtypes=True).then_inc(s_ones, 1)
                nc.gpsimd.iota(sidx[:], [[1, NCC]], channel_multiplier=NCC, allow_small_or_imprecise_dtypes=True).then_inc(s_ones, 1)
                nc.gpsimd.iota(gend[:], [[W, NG]], base=W, channel_multiplier=0,
                               allow_small_or_imprecise_dtypes=True).then_inc(s_ones, 1)
                pool.wait_ge(s_tick, 3)
                nc.gpsimd.affine_select(out=ident[:], in_=ident[:], compare_op=ALU.not_equal, fill=1.0, base=0,
                                        pattern=[[-1, P]], channel_multiplier=1).then_inc(s_const, 1)
                nc.gpsimd.affine_select(out=tri[:], in_=tri[:], compare_op=ALU.is_gt, fill=0.0, base=0,
                                        pattern=[[1, NB + 1]], channel_multiplier=-1).then_inc(s_const, 1)
                nc.gpsimd.affine_select(out=sel[:], in_=sel[:], compare_op=ALU.not_equal, fill=1.0, base=-EA,
                                        pattern=[[0, P]], channel_multiplier=1).then_inc(s_const, 1)

                for r in range(GR):
                    for j in range(2):
                        if r == 0 and j == 0:
                            pool.wait_ge(s_which, 1)
                            pool.sem_inc(s_tick, 1)
                        pool.indirect_dma_start(edge_rows[:, j, r, :], None, dst_rows,
                                                bass.IndirectOffsetOnAxis(ap=whichi[:, j, r:r + 1], axis=0)).then_inc(s_rows, 16)

            @block.vector
            def _(dve):
                k = [0]

                def link(ins):
                    k[0] += 1
                    ins.then_inc(s_c, 1)
                    dve.wait_ge(s_c, k[0])

                dve.wait_ge(s_back, 16)
                nc.vector.tensor_reduce(lohi[:, 0, :], dr[:], AX.X, ALU.min).then_inc(s_c, 1)
                nc.vector.tensor_reduce(lohi[:, 1, :], dr[:], AX.X, ALU.max).then_inc(s_c, 1)
                k[0] = 2
                nc.vector.memset(eaT, 0.0)
                nc.vector.memset(ones[:], 1.0)
                nc.vector.memset(denom[:], 1.0)
                link(nc.vector.memset(eps[:], EPS))
                dve.wait_ge(s_ones, 10)
                dve.wait_ge(s_back, 48)
                def tiles_of(n, first, final, end, start):
                    link(nc.vector.tensor_scalar(below[0:n, :], lo_b[0:n, :], final, None, ALU.is_le))
                    link(nc.vector.scalar_tensor_tensor(out=hit[0:n, :], in0=hi_b[0:n, :], scalar=first,
                                                        in1=below[0:n, :], op0=ALU.is_ge, op1=ALU.mult))
                    link(nc.vector.tensor_tensor(prod[0:n, 0, :], hit[0:n, :], t1[0:n, :], ALU.mult))
                    link(nc.vector.tensor_tensor(prod[0:n, 1, :], hit[0:n, :], t2[0:n, :], ALU.mult))
                    link(nc.vector.tensor_reduce(end, prod[0:n, 0, :], AX.X, ALU.max))
                    link(nc.vector.tensor_reduce(start, prod[0:n, 1, :], AX.X, ALU.max))

                tiles_of(NB, blk[:, 0:1], blk[:, 1:2], rng[:, 0:1], rng[:, 1:2])
                for r in range(GR):
                    tiles_of(GQ, glo[:, r:r + 1], ghi[:, r:r + 1], gt[:, 0, r:r + 1], gt[:, 1, r:r + 1])
                link(nc.vector.tensor_scalar(gt[:, 2, :], gt[:, 1, :], -1.0, BIG_T, ALU.mult, ALU.add))
                link(nc.vector.tensor_scalar(which[:, 0, :], gt[:, 2, :], BIG_T - 1.0, None, ALU.min))
                link(nc.vector.tensor_scalar(which[:, 1, :], gt[:, 0, :], -1.0, 0.0, ALU.add, ALU.max))
                nc.vector.tensor_copy(whichi[:], which[:]).then_inc(s_which, 1)
                dve.wait_ge(s_line, 48)
                link(nc.vector.tensor_tensor(info[:, :, 0], dn[:, 0:RW], dn[:, 1:RW + 1], ALU.is_gt))
                link(nc.vector.tensor_reduce(worst[:], info[:, :, 0], AX.X, ALU.max))
                link(nc.vector.tensor_scalar(worst[:], worst[:], 2.0 ** 20, None, ALU.mult))
                link(nc.vector.tensor_scalar(parts[:, 0, :], sn[:], 7, None, ALU.arith_shift_right))
                link(nc.vector.tensor_scalar(parts[:, 1, :], dn[:, 0:RW], W - 1, None, ALU.bitwise_and))
                nc.vector.scalar_tensor_tensor(out=info[:, :, 0], in0=parts[:, 0, :], scalar=float(W), in1=parts[:, 1, :],
                                               op0=ALU.mult, op1=ALU.add).then_inc(s_info, 1)
                dve.wait_ge(s_info, 1)
                link(nc.vector.tensor_scalar(parts[:, 1, :], sn[:], P - 1, None, ALU.bitwise_and))
                nc.vector.tensor_copy(info[:, :, 1], parts[:, 1, :])
                nc.vector.tensor_copy(info[:, :, 2], dn[:, 0:RW]).then_inc(s_info, 1)
                dve.wait_ge(s_rows, 16 * 2 * GR)
                for r in range(GR):
                    nc.vector.tensor_scalar(under[:, 0, r, :], edge_rows[:, 0, r, :], glo[:, r:r + 1], None, ALU.is_lt)
                    un = nc.vector.tensor_scalar(under[:, 1, r, :], edge_rows[:, 1, r, :], ghi[:, r:r + 1], None, ALU.is_le)
                link(un)
                link(nc.vector.tensor_reduce(num[:, 0:2, :], under[:], AX.X, ALU.add))
                link(nc.vector.scalar_tensor_tensor(out=num[:, 2:4, :], in0=which[:], scalar=float(P), in1=num[:, 0:2, :],
                                                    op0=ALU.mult, op1=ALU.add))
                link(nc.vector.tensor_copy(gti[:], num[:, 2, :]))
                link(nc.vector.tensor_tensor(num[:, 0, :], num[:, 3, :], num[:, 2, :], ALU.subtract))
                link(nc.vector.tensor_reduce(num[:, 1, 0:1], num[:, 0, :], AX.X, ALU.max))
                link(nc.vector.tensor_tensor(worst[0:GQ, :], worst[0:GQ, :], num[:, 1, 0:1], ALU.max))
                dve.sem_inc(s_rng, 1)
                link(nc.vector.tensor_scalar(rng[:, 2:3], rng[:, 1:2], -1.0, BIG_T, ALU.mult, ALU.add))
                link(nc.vector.tensor_tensor(rng[:, 3:4], rng[:, 0:1], rng[:, 2:3], ALU.subtract))
                link(nc.vector.tensor_scalar(rng[:, 4:5], rng[:, 3:4], 0.0, float(C - 1), ALU.max, ALU.add))
                link(nc.vector.tensor_scalar(rngi[:, 0:1], rng[:, 4:5], float(-(-2 ** 14 // C)), None, ALU.mult))
                link(nc.vector.tensor_scalar(rngi[:, 1:2], rngi[:, 0:1], 14, None, ALU.arith_shift_right))
                link(nc.vector.tensor_copy(rng[:, 5:6], rngi[:, 1:2]))
                nc.vector.tensor_copy(nbc[:, 0, :], rng[:, 5:6].to_broadcast([NB, P]))
                nc.vector.tensor_copy(nbc[:, 1, :], rng[:, 2:3].to_broadcast([NB, P])).then_inc(s_rng, 1)
                dve.wait_ge(s_cum, 1)
                link(nc.vector.tensor_reduce(unit[0:1, 0:1], bank[2][0:1, 0:P], AX.X, ALU.max))
                link(nc.vector.tensor_scalar(fast[:], unit[0:1, 0:1], GT * P + 0.5, None, ALU.is_lt))
                link(nc.vector.tensor_copy(cum[:], bank[0][:, 0:NB + 1]))
                link(nc.vector.scalar_tensor_tensor(out=q[:], in0=cum[:, 0:NB], scalar=-float(C),
                                                    in1=bank[1][:, 0:NB], op0=ALU.mult, op1=ALU.add))
                link(nc.vector.tensor_tensor(dq[:, 1:NB], q[:, 1:NB], q[:, 0:NB - 1], ALU.subtract))
                link(nc.vector.tensor_scalar(dq[:, 1:NB], dq[:, 1:NB], 1024.0, None, ALU.add))
                link(nc.vector.tensor_scalar(v[:], sidx[:], float(C), q[:, 0:1], ALU.mult, ALU.add))
                for b in range(1, NB):
                    link(nc.vector.tensor_scalar(step[:], sidx[:], cum[:, b:b + 1], dq[:, b:b + 1], ALU.is_ge, ALU.mult))
                    link(nc.vector.tensor_tensor(v[:], v[:], step[:], ALU.add))
                link(nc.vector.tensor_scalar(step[:], sidx[:], cum[:, NB:NB + 1], None, ALU.is_lt))
                link(nc.vector.tensor_scalar(v[:], v[:], float(-(TA - C)), None, ALU.add))
                link(nc.vector.tensor_tensor(v[:], v[:], step[:], ALU.mult))
                link(nc.vector.tensor_scalar(vi[:], v[:], float(TA - C), None, ALU.add))
                dve.sem_inc(s_list, 1)
                link(nc.vector.tensor_scalar(turns_i[:, 0:1], cum[:, NB:NB + 1], float(U - 1), None, ALU.add))
                link(nc.vector.tensor_scalar(turns_i[:, 1:2], turns_i[:, 0:1], U.bit_length() - 1, None,
                                             ALU.arith_shift_right))
                link(nc.vector.tensor_scalar(turns[:], turns_i[0:1, 1:2], 1.0, None, ALU.max))
                dve.wait_ge(s_in, 16 * NIN)
                nc.vector.tensor_copy(dst[:], di[:]).then_inc(s_dve, 1)

            @block.tensor
            def _(pe):
                pe.wait_ge(s_rng, 2)
                pe.wait_ge(s_const, 3)
                nc.tensor.transpose(bank[2][0:1, 0:P], worst[:], ident[:])
                nc.tensor.matmul(bank[0][:, 0:NB + 1], nbc[:, 0, :], tri[:], start=True, stop=True)
                nc.tensor.matmul(bank[1][:, 0:NB], nbc[:, 1, :], ident[0:NB, 0:NB], start=True, stop=True).then_inc(s_cum, 1)

        def chunk_of(eng, at):
            both = eng.value_load(chunks[0:1, bass.ds(at, 1)], min_val=0, max_val=(NB - 1) * 1024 + TA - 1)
            return both >> 10, (both & 1023)


        def way(eng):
            return eng.value_load(fast[0:1, 0:1], min_val=0, max_val=1) > 0

        with ExitStack() as cc:
            def sm(name):
                return ctx.enter_context(nc.semaphore(f"count_{name}"))

            def ring(name, shape, dt=F32):
                return cc.enter_context(nc.sbuf_tensor(f"count_{name}", shape, dt))
            NV = 4
            PR = 2 * ES
            assert GP == 2 * ES and GP % NV == 0
            stage = ring("stage", [P, 2, NB, P], F16)
            keys = ring("keys", [P, HC], F16)
            low_keys = ring("low_keys", [P, P], F16)
            past = ring("past", [P, NV, GT])
            low = ring("low", [P, NV, GT])
            info = ring("info", [P, 2 * ES, GT, INFO])
            to = ring("to", [P, NV, GT, W])
            room = acc[:].bitcast(F16)
            cols = room[:, 0:NV * GT * HC].rearrange("p (v j n) -> p v j n", v=NV, j=GT)
            lows = room[:, NV * GT * HC:NV * GT * (HC + P)].rearrange("p (v j n) -> p v j n", v=NV, j=GT)
            eas = ring("eas", [P, 2 * ES, GT, EA1])
            keys_ready, past_ready, low_ready, cols_ready, counted, taken, stored = (
                sm("keys_ready"), sm("past_ready"), sm("low_ready"), sm("cols_ready"),
                sm("counted"), sm("taken"), sm("stored"))
            block = cc.enter_context(nc.Block())

            @block.sync
            def _(sp):
                with sp.If(way(sp)):
                    with sp.Fori(0, NPAN) as o:
                        for k in range(GP):
                            g = o * GP + k
                            e = sp.value_load(groups[0:1, bass.ds(g, 1)], min_val=0, max_val=EE - GT * P)
                            if k % 2 == 0:
                                sp.wait_ge(counted, g + 2)
                                sp.sem_inc(s_tick, 1)
                            at = bass.ds(e, GT * P)
                            sp.dma_start(info[:, k, :, :].rearrange("p j f -> p (j f)"),
                                         info_dram[at, :].rearrange("(p j) f -> p (j f)", j=GT)).then_inc(ea_got[k // 2], 16)
                            sp.dma_start(eas[:, k, :, :].rearrange("p j f -> p (j f)"),
                                         ea[at, :].rearrange("(p j) f -> p (j f)", j=GT)).then_inc(ea_got[k // 2], 16)
                with sp.Else():
                    sp.sem_inc(s_tick, 1)

            @block.gpsimd
            def _(pool):
                with pool.If(way(pool)):
                    nc.gpsimd.iota(keys[:], [[1, HC]], channel_multiplier=0,
                                   allow_small_or_imprecise_dtypes=True).then_inc(keys_ready, 1)
                    nc.gpsimd.iota(low_keys[:], [[1, P]], channel_multiplier=0,
                                   allow_small_or_imprecise_dtypes=True).then_inc(keys_ready, 1)
                    with pool.Fori(0, NPAN) as o:
                        for k in range(GP):
                            g = o * GP + k
                            v = k % NV
                            pool.wait_ge(ea_got[k // 2], 64 * (o + 1))
                            pool.wait_ge(counted, g + 1 - NV + PR)
                            nc.gpsimd.tensor_tensor(past[:, v, :], info[:, k, :, 2],
                                                    gend[:, bass.ds(g, 1)].to_broadcast([P, GT]), ALU.subtract
                                                    ).then_inc(past_ready, 1)
                            pool.wait_ge(past_ready, g * 2 + 1)
                            pool.sem_inc(s_tick, 1)
                            nc.gpsimd.tensor_scalar(past[:, v, :], past[:, v, :], 0.0, float(P), ALU.is_ge, ALU.mult
                                                    ).then_inc(past_ready, 1)
                            pool.wait_ge(past_ready, g * 2 + 2)
                            nc.gpsimd.tensor_tensor(low[:, v, :], past[:, v, :], info[:, k, :, 1], ALU.add
                                                    ).then_inc(low_ready, 1)
                with pool.Else():
                    pool.sem_inc(s_tick, 1)

            @block.vector
            def _(dve):
                with dve.If(way(dve)):
                    dve.wait_ge(keys_ready, 2)
                    with dve.Fori(0, NPAN) as o:
                        for k in range(GP):
                            g = o * GP + k
                            v = k % NV
                            slot = info[:, k, :, :]
                            dve.wait_ge(counted, g + 1 - NV + PR)
                            dve.wait_ge(ea_got[k // 2], 64 * (o + 1))
                            nc.vector.scalar_tensor_tensor(out=to[:, v, :, :],
                                                           in0=slot[:, :, 2:3].to_broadcast([P, GT, W]),
                                                           scalar=gbase[:, bass.ds(g, 1)],
                                                           in1=iota[:, 0:W].unsqueeze(1).to_broadcast([P, GT, W]),
                                                           op0=ALU.subtract, op1=ALU.is_equal)
                            for j in range(GT):
                                nc.vector.tensor_scalar(cols[:, v, j, :], keys[:], slot[:, j, 0:1], None, ALU.is_equal)
                            dve.wait_ge(low_ready, g + 1)
                            for j in range(GT):
                                oh = nc.vector.tensor_scalar(lows[:, v, j, :], low_keys[:], low[:, v, j:j + 1], None,
                                                             ALU.is_equal)
                            oh.then_inc(cols_ready, 1)
                with dve.Else():
                    dve.sem_inc(s_tick, 1)

            @block.tensor
            def _(pe):
                with pe.If(way(pe)):
                    pe.sem_inc(counted, PR)
                    pe.sem_inc(taken, 2)
                    with pe.Fori(0, NPAN) as o:
                        for k in range(GP):
                            g = o * GP + k
                            v = k % 2
                            pe.wait_ge(taken, g + 1)
                            pe.wait_ge(cols_ready, g + 1)
                            for j in range(GT):
                                for h, (c0, c1) in enumerate(((0, HA * W), (HA * W, HC))):
                                    nc.tensor.matmul(bank[2 * v + h][:, 0:c1 - c0], lows[:, k % NV, j, :], cols[:, k % NV, j, c0:c1],
                                                     start=(j == 0), stop=(j == GT - 1))
                            pe.wait_ge(ea_got[k // 2], 64 * (o + 1))
                            for j in range(GT):
                                mm = nc.tensor.matmul(bank[4 + v][0:EA1, 0:W], eas[:, k, j, :], to[:, k % NV, j, :],
                                                      start=(j == 0), stop=(j == GT - 1))
                            mm.then_inc(counted, 1)
                with pe.Else():
                    pe.sem_inc(s_tick, 1)

            @block.scalar
            def _(act):
                with act.If(way(act)):
                    act.sem_inc(stored, 16)
                    with act.Fori(0, NPAN) as o:
                        half = bass.ds(o & 1, 1)
                        for k in range(GP):
                            g = o * GP + k
                            v = k % 2
                            if k == GP // 2:
                                act.wait_ge(stored, 16 * (o + 1))
                                act.sem_inc(s_tick, 1)
                            act.wait_ge(counted, g + 1 + PR)
                            act.sem_inc(s_tick, 1)
                            nc.scalar.copy(stage[:, half, 0:HA, k * W:(k + 1) * W],
                                           bank[2 * v][:, 0:HA * W].rearrange("p (a b w) -> p a b w", a=1, w=W))
                            nc.scalar.copy(stage[:, half, HA:NB, k * W:(k + 1) * W],
                                           bank[2 * v + 1][:, 0:HC - HA * W].rearrange("p (a b w) -> p a b w", a=1, w=W))
                            nc.scalar.copy(eaT[:, bass.ds(g * W, W)], bank[4 + v][0:EA1, 0:W]).then_inc(taken, 1)
                        act.wait_ge(taken, (o + 1) * GP + 2)
                        act.sem_inc(s_tick, 1)
                        act.dma_start(counts[bass.ds(o, 1), :, :].rearrange("a l n -> l (a n)"),
                                      stage[:, half, :, :].rearrange("p a b w -> p (a b w)")).then_inc(stored, 16)
                    act.wait_ge(stored, 16 * (NPAN + 1))
                with act.Else():
                    act.sem_inc(s_tick, 1)

        NQ = NPAN // QP + 1
        piece_got = [sem(f"piece_got{c}") for c in range(PC)]
        rows_in, scaled, hi_ready, lo_ready, peak_ready, peak_row, used, taken, cleared = (
            sem("rows_in"), sem("scaled"), sem("hi_ready"), sem("lo_ready"), sem("peak_ready"), sem("peak_row"),
            sem("piece_used"), sem("sums_taken"), sem("sums_cleared"))
        for l in range(3):
            last = l == 2
            with ExitStack() as c1:
                def sm(name):
                    return ctx.enter_context(nc.semaphore(f"l{l}_{name}"))

                def ring(name, shape, dt=F32):
                    return c1.enter_context(nc.sbuf_tensor(f"l{l}_{name}", shape, dt))
                idx = ring("idx", [P, U, C], U32)
                hot_ready, mm_done, added = sm("onehot_ready"), sm("sum_ready"), sm("sum_added")
                piece = ring("piece", [P, PC, QP, PH * P], F16)
                room = piece[:].rearrange("p c s n -> p (c s n)").bitcast(F32)
                n_rows, n_hot, n_ea = U * C * D, 2 * C * P, U * C * EA1
                rows_l = room[:, 0:n_rows].rearrange("p (k f) -> p k f", f=D)
                onehot = room[:, n_rows:n_rows + n_hot].rearrange("p (v j n) -> p v j n", v=2, j=C)
                eas = room[:, n_rows + n_hot:n_rows + n_hot + n_ea].rearrange("p (u j f) -> p u j f", u=U, j=C)
                x_hi, x_lo = (c1.enter_context(nc.sbuf_tensor(f"l{l}_{k}", [P, NB, D], F16)) for k in ("x_hi", "x_lo"))
                xh, xl = (a[:].rearrange("p k f -> p (k f)") for a in (x_hi, x_lo))
                block = c1.enter_context(nc.Block())

                @block.gpsimd
                def _(pool):
                    with pool.If(way(pool)):
                        pool.sem_inc(s_tick, 1)
                    with pool.Else():
                        n = pool.value_load(turns[0:1, 0:1], min_val=1, max_val=P * NCC // U - 2)
                        with pool.Fori(0, n) as i:
                            for u in range(U):
                                pool.wait_ge(idx_ready[u], i + 1 + (n + 1) * l if l else i + 1)
                                pool.sem_inc(s_tick, 1)
                                for j in range(C):
                                    pool.indirect_dma_start(rows_l[:, u * C + j, :], None, table[l],
                                                            bass.IndirectOffsetOnAxis(ap=idx[:, u, j:j + 1], axis=0)
                                                            ).then_inc(row_got[u], 16)

                @block.scalar
                def _(act):
                    with act.If(way(act)):
                        act.wait_ge(scaled, 4 * (l + 1))
                        for c in range(2):
                            half = slice(c * NP // 2, (c + 1) * NP // 2)
                            nc.scalar.activation(xh[:, half], acc[:, half], ACT.Copy, scale=unit[:, 2:3]).then_inc(hi_ready, 1)

                        def take(q, v, n):
                            act.wait_ge(used, (l * NQ + q + 2) * PC)
                            act.sem_inc(s_tick, 1)
                            nc.scalar.activation(acc[:, bass.ds(q * (QP * P), n * P)], bank[v][:, 0:n * P],
                                                 ACT.Copy, scale=unit[:, 3:4]).then_inc(taken, 1)

                        with act.Fori(0, (NQ - 1) // 2) as i:
                            take(i * 2, 0, QP)
                            take(i * 2 + 1, 1, QP)
                        take(NQ - 1, 0, 1)
                    with act.Else():
                        n = act.value_load(turns[0:1, 0:1], min_val=1, max_val=P * NCC // U - 2)

                        def fetch(i, u):
                            _, t = chunk_of(act, i * U + u)
                            t = t.with_bounds(min_val=0, max_val=TA - C)
                            nc.scalar.copy(idx[:, u, :], src[:, bass.ds(t, C)]).then_inc(idx_ready[u], 1)
                        for u in range(U):
                            fetch(0, u)
                        with act.Fori(1, n + 1) as i:
                            for u in range(U):
                                act.wait_ge(mm_done, i * U + u + 1)
                                act.sem_inc(s_tick, 1)
                                fetch(i, u)

                @block.sync
                def _(sp):
                    with sp.If(way(sp)):
                        if l == 0:
                            sp.dma_start(acc[:].rearrange("p (k f) -> p k f", f=D),
                                         x.rearrange("(k p) f -> p k f", p=P)).then_inc(rows_in, 16)

                        def read(q, n):
                            for c in range(PC):
                                sp.wait_ge(used, (l * NQ + q) * PC + c + 1)
                                sp.sem_inc(s_tick, 1)
                                sp.dma_start(piece[:, c, 0:n, :], counts.rearrange("s l n -> l s n")[
                                    :, bass.ds(q * QP, n), c * PH * P:(c + 1) * PH * P]).then_inc(piece_got[c], 16)

                        with sp.Fori(0, NQ - 1) as q:
                            read(q, QP)
                        read(NQ - 1, 1)
                    with sp.Else():
                        sp.sem_inc(s_tick, 1)
                        if l == 0:
                            n = sp.value_load(turns[0:1, 0:1], min_val=1, max_val=P * NCC // U - 2)
                            with sp.Fori(0, n) as i:
                                for u in range(U):
                                    _, t = chunk_of(sp, i * U + u)
                                    t = t.with_bounds(min_val=0, max_val=TA - C)
                                    sp.wait_ge(mm_done, i * U + u + 1)
                                    sp.sem_inc(s_tick, 1)
                                    sp.dma_start(eas[:, u, :, :], ea_tiles[:, bass.ds(t, C), :]).then_inc(ea_got[u], 16)

                @block.vector
                def _(dve):
                    with dve.If(way(dve)):
                        if l == 0:
                            dve.wait_ge(rows_in, 16)
                        nc.vector.tensor_reduce(unit[:, 0:1], acc[:], AX.X, ALU.max, apply_absolute_value=True).then_inc(peak_ready, 1)
                        dve.wait_ge(peak_row, 2 * l + 1)
                        nc.vector.tensor_reduce(unit[0:1, 1:2], bank[2][0:1, 0:P], AX.X, ALU.max).then_inc(peak_ready, 1)
                        dve.wait_ge(peak_row, 2 * l + 2)
                        nc.vector.tensor_scalar(unit[:, 0:1], bank[3][:, 0:1], 2.0 ** -100, None, ALU.max).then_inc(scaled, 1)
                        dve.wait_ge(scaled, 4 * l + 1)
                        bits = unit[:].bitcast(I32)
                        nc.vector.tensor_scalar(bits[:, 1:2], bits[:, 0:1], EXPONENT, None, ALU.bitwise_and).then_inc(scaled, 1)
                        dve.wait_ge(scaled, 4 * l + 2)
                        nc.vector.tensor_scalar(bits[:, 2:3], bits[:, 1:2], -1.0, float(267 << 23), ALU.mult, ALU.add).then_inc(scaled, 1)
                        nc.vector.tensor_scalar(bits[:, 3:4], bits[:, 1:2], float(13 << 23), None, ALU.subtract).then_inc(scaled, 1)
                        dve.wait_ge(scaled, 4 * l + 4)
                        for c in range(2):
                            half = slice(c * NP // 2, (c + 1) * NP // 2)
                            dve.wait_ge(hi_ready, 2 * l + c + 1)
                            nc.vector.scalar_tensor_tensor(out=xl[:, half], in0=acc[:, half], scalar=unit[:, 2:3],
                                                           in1=xh[:, half], op0=ALU.mult, op1=ALU.subtract).then_inc(lo_ready, 1)
                    with dve.Else():
                        nc.vector.memset(acc[:], 0.0).then_inc(cleared, 1)
                        dve.wait_ge(cleared, l + 1)
                        n = dve.value_load(turns[0:1, 0:1], min_val=1, max_val=P * NCC // U - 2)
                        with dve.Fori(0, n) as i:
                            for u in range(U):
                                b, t = chunk_of(dve, i * U + u)
                                t = t.with_bounds(min_val=0, max_val=TA - C)
                                b = b.with_bounds(min_val=0, max_val=NB - 1)
                                dve.wait_ge(mm_done, i * U + u + U - 1)
                                nc.vector.scalar_tensor_tensor(
                                    out=onehot[:, u % 2, :, :],
                                    in0=dst[:, bass.ds(t, C)].unsqueeze(2).to_broadcast([P, C, P]),
                                    scalar=base[:, bass.ds(b, 1)],
                                    in1=iota[:].unsqueeze(1).to_broadcast([P, C, P]),
                                    op0=ALU.subtract, op1=ALU.is_equal).then_inc(hot_ready, 1)
                                dve.wait_ge(mm_done, i * U + u + U + 1)
                                dve.wait_ge(added, (i * U + u) + 1)
                                cols = acc[:, bass.ds(b * P, P)]
                                if l == 0:
                                    nc.vector.tensor_tensor(eaT[:, bass.ds(b * P, P)], eaT[:, bass.ds(b * P, P)],
                                                            bank[2 + u % 2][0:EA1, 0:P], ALU.add)
                                nc.vector.tensor_tensor(cols, cols, bank[u % 2][:, 0:P], ALU.add).then_inc(added, 1)

                @block.tensor
                def _(pe):
                    with pe.If(way(pe)):
                        if l == 0:
                            pe.sem_inc(used, PC)
                            pe.sem_inc(taken, 2)
                        pe.wait_ge(peak_ready, 2 * l + 1)
                        nc.tensor.transpose(bank[2][0:1, 0:P], unit[:, 0:1], ident[:]).then_inc(peak_row, 1)
                        pe.wait_ge(peak_ready, 2 * l + 2)
                        nc.tensor.matmul(bank[3][:, 0:1], ones[0:1, :], unit[0:1, 1:2], start=True, stop=True).then_inc(peak_row, 1)
                        pe.wait_ge(lo_ready, 2 * l + 2)

                        def sums(q, v, n):
                            pe.wait_ge(taken, l * NQ + q + 1)
                            for c in range(PC):
                                pe.wait_ge(piece_got[c], 16 * (l * NQ + q + 1))
                                for h in range(PH):
                                    blk_h = c * PH + h
                                    moving = piece[:, c, 0:n, h * P:(h + 1) * P]
                                    nc.tensor.matmul(bank[v][:, 0:n * P], x_hi[:, blk_h, :], moving,
                                                     start=(blk_h == 0), stop=False)
                                    mm = nc.tensor.matmul(bank[v][:, 0:n * P], x_lo[:, blk_h, :], moving,
                                                          start=False, stop=(blk_h == NB - 1))
                                mm.then_inc(used, 1)

                        with pe.Fori(0, (NQ - 1) // 2) as i:
                            sums(i * 2, 0, QP)
                            sums(i * 2 + 1, 1, QP)
                        sums(NQ - 1, 0, 1)
                    with pe.Else():
                        n = pe.value_load(turns[0:1, 0:1], min_val=1, max_val=P * NCC // U - 2)
                        pe.sem_inc(mm_done, U)
                        pe.sem_inc(added, 1)
                        with pe.Fori(0, n) as i:
                            for u in range(U):
                                pe.wait_ge(hot_ready, i * U + u + 1)
                                if l == 0:
                                    pe.wait_ge(ea_got[u], 16 * (i + 1))
                                    for j in range(C):
                                        nc.tensor.matmul(bank[2 + u % 2][0:EA1, 0:P], eas[:, u, j, :], onehot[:, u % 2, j, :],
                                                         start=(j == 0), stop=(j == C - 1))
                                pe.wait_ge(row_got[u], (i + 1 + n * l) * G16 if l else (i + 1) * G16)
                                for j in range(C):
                                    mm = nc.tensor.matmul(bank[u % 2][:, 0:P], rows_l[:, u * C + j, :],
                                                          onehot[:, u % 2, j, :], start=(j == 0), stop=(j == C - 1))
                                mm.then_inc(mm_done, 1)

            with ExitStack() as c2:
                def sm(name):
                    return ctx.enter_context(nc.semaphore(f"n{l}_{name}"))

                def tile(name, shape, dt=F32):
                    return c2.enter_context(nc.sbuf_tensor(f"n{l}_{name}", shape, dt))
                xd = tile("xd", [P, SB * P])
                y = tile("y", [P, SB * P])
                nodes = tile("nodes", [P, SB, D])
                resid = tile("resid", [P, SB, D])
                hrow = tile("hrow", [P, SB, ROW])
                stats = tile("stats", [P, SB, 6])
                mv = tile("mv", [P, SB, 2])
                rstd = tile("rstd", [P, SB])
                adst_t = tile("adst_t", [P, SB])
                self_e = tile("self_e", [P, SB])
                junk = tile("junk", [P, 2 * SB, D])
                SK = 32 if last else 16
                deg_ps, xd_ready, y_ps, y_ready, tr_ps, nodes_ready, stored = (
                    sm("deg_in_psum"), sm("xd_ready"), sm("y_in_psum"), sm("y_ready"), sm("rows_in_psum"),
                    sm("rows_ready"), sm("rows_stored"))
                y_done = sm("feat_updated")
                lin = sm("y_scaled")
                stat = sm("stats_step")
                if last:
                    x1T = sm("x1T_ready")
                    res_got, x1_ready, x1T_ps, h_ps, h_ready = (
                        sm("resid_got"), sm("x1_ready"), sm("x1T_in_psum"), sm("h_in_psum"), sm("h_ready"))
                    sq = sm("sqrt_ready")
                    hc, trc = sm("h_copied"), sm("rows_copied")
                block = c2.enter_context(nc.Block())
                tb = [(bank[4 + k // 4], (k % 4) * P) for k in range(SB)]
                tc_ = [(bank[6 + k // 4], (k % 4) * P) for k in range(SB)]
                slope = 0.01

                @block.tensor
                def _(pe):
                    with pe.Fori(0, NT) as i:
                        for g in range(2):
                            cols = eaT[:, bass.ds(i * (SB * P) + g * HB, HB)]
                            if g == 0:
                                pe.wait_ge(xd_ready, 2 * i + 1)
                            mm = nc.tensor.matmul(bank[g][:, 0:HB], sel[:], cols, start=True, stop=True)
                        mm.then_inc(deg_ps, 1)
                        for g in range(2):
                            at = bass.ds(i * (SB * P) + g * HB, HB)
                            if g == 0:
                                pe.wait_ge(y_ready, i + 1)
                            nc.tensor.matmul(bank[2 + g][:, 0:HB], w0[:, l, 0, :], acc[:, at], start=True, stop=False)
                            nc.tensor.matmul(bank[2 + g][:, 0:HB], w0e[:, l, :], eaT[:, at], start=False, stop=False)
                            if g == 0:
                                pe.wait_ge(xd_ready, 2 * i + 2 + 1)
                            mm = nc.tensor.matmul(bank[2 + g][:, 0:HB], w0[:, l, 1, :], xd[:, g * HB:(g + 1) * HB],
                                                  start=False, stop=True)
                        mm.then_inc(y_ps, 1)
                        pe.wait_ge(y_ready, i + 2)
                        pe.wait_ge(nodes_ready, i + 1)
                        for k in range(SB):
                            bk, o = tb[k]
                            tr = nc.tensor.transpose(bk[:, o:o + P], y[:, k * P:(k + 1) * P], ident[:])
                        tr.then_inc(tr_ps, 1)
                        if last:
                            pe.wait_ge(x1_ready, i + 1)
                            pe.wait_ge(x1T, i + 1)
                            for k in range(SB):
                                bk, o = tc_[k]
                                tr = nc.tensor.transpose(bk[:, o:o + P], nodes[:, k, :], ident[:])
                            tr.then_inc(x1T_ps, 1)
                            pe.wait_ge(x1T, i + 2)
                            for k in range(SB):
                                bk, o = tb[k]
                                mm = nc.tensor.matmul(bk[:, o:o + P], y[:, k * P:(k + 1) * P], w1[:], start=True, stop=True)
                            mm.then_inc(h_ps, 1)

                @block.vector
                def _(dve):
                    nc.vector.memset(hrow[:, :, D + 1:ROW], 0.0)
                    dve.sem_inc(xd_ready, 1)
                    dve.sem_inc(y_ready, 1)
                    with dve.Fori(0, NT) as i:
                        for g in range(2):
                            at = bass.ds(i * (SB * P) + g * HB, HB)
                            if g == 0:
                                dve.wait_ge(deg_ps, i + 1)
                                dve.wait_ge(y_done, i + 1)
                            nc.vector.tensor_tensor(xd[:, g * HB:(g + 1) * HB], feat[:, at], bank[g][:, 0:HB],
                                                    ALU.mult).then_inc(xd_ready, 1)
                        dve.wait_ge(lin, i + 1)
                        for g in range(2):
                            mx = nc.vector.scalar_tensor_tensor(
                                out=y[:, g * HB:(g + 1) * HB], in0=bank[2 + g][:, 0:HB], scalar=slope,
                                in1=feat[:, bass.ds(i * (SB * P) + g * HB, HB)], op0=ALU.mult, op1=ALU.max)
                            mx.then_inc(stat, 1)
                        if last:
                            dve.wait_ge(stat, 5 * i + 2)
                            mx = nc.vector.scalar_tensor_tensor(out=y[:], in0=y[:], scalar=slope, in1=y[:],
                                                                op0=ALU.mult, op1=ALU.max)
                            mx.then_inc(y_ready, 1)
                        else:
                            dve.wait_ge(stat, 2 * i + 2)
                            dve.sem_inc(s_tick, 1)
                            nc.vector.tensor_copy(feat[:, bass.ds(i * (SB * P), SB * P)], y[:]).then_inc(y_ready, 1)
                        if last:
                            dve.wait_ge(trc, i + 1)
                            dve.wait_ge(res_got, 16 * (i + 1))
                            nc.vector.tensor_tensor(resid[:], resid[:], nodes[:], ALU.add).then_inc(stat, 1)
                            dve.wait_ge(stat, 5 * i + 3)
                            for k in range(SB):
                                bn = nc.vector.bn_stats(out=stats[:, k, :], in_=resid[:, k, :])
                            bn.then_inc(stat, 1)
                            dve.wait_ge(stat, 5 * i + 4)
                            dve.sem_inc(s_tick, 1)
                            for k in range(SB):
                                bn = nc.vector.bn_aggr(out=mv[:, k, :], in_=stats[:, k, :])
                            bn.then_inc(stat, 1)
                            dve.wait_ge(sq, i + 1)
                            nc.vector.reciprocal(rstd[:], rstd[:]).then_inc(hc, 1)
                            dve.wait_ge(hc, 3 * i + 1)
                            for k in range(SB):
                                nm = nc.vector.tensor_scalar(nodes[:, k, :], resid[:, k, :], mv[:, k, 0:1],
                                                             rstd[:, k:k + 1], ALU.subtract, ALU.mult)
                            nm.then_inc(x1_ready, 1)
                            dve.wait_ge(h_ready, i + 1)
                            for k in range(SB):
                                nc.vector.tensor_tensor_reduce(
                                    out=junk[:, k, :], in0=hrow[:, k, 0:D], in1=att_row[:, 0, :], scale=1.0, scalar=0.0,
                                    op0=ALU.mult, op1=ALU.add, accum_out=hrow[:, k, D:D + 1])
                                tt = nc.vector.tensor_tensor_reduce(
                                    out=junk[:, SB + k, :], in0=hrow[:, k, 0:D], in1=att_row[:, 1, :], scale=1.0, scalar=0.0,
                                    op0=ALU.mult, op1=ALU.add, accum_out=adst_t[:, k:k + 1])
                            tt.then_inc(hc, 1)
                            dve.wait_ge(hc, 3 * i + 2)
                            dve.sem_inc(s_tick, 1)
                            nc.vector.tensor_copy(a_dst[:, bass.ds(i * SB, SB)], adst_t[:])
                            nc.vector.tensor_copy(a_src[:, bass.ds(i * SB, SB)], hrow[:, :, D])
                            nc.vector.tensor_copy(acc[:, bass.ds(i * (SB * P), SB * P)].rearrange("p (k f) -> p k f", f=D),
                                                  hrow[:, :, 0:D])
                            nc.vector.tensor_tensor(self_e[:], adst_t[:], hrow[:, :, D], ALU.add).then_inc(hc, 1)
                            dve.wait_ge(hc, 3 * i + 3)
                            dve.sem_inc(s_tick, 1)
                            nc.vector.scalar_tensor_tensor(out=peak[:, bass.ds(i * SB, SB)], in0=self_e[:], scalar=0.2,
                                                           in1=self_e[:], op0=ALU.mult, op1=ALU.max).then_inc(s_dve, 1)

                @block.scalar
                def _(act):
                    act.sem_inc(y_done, 1)
                    act.sem_inc(nodes_ready, 1)
                    if last:
                        act.sem_inc(x1T, 1)
                    with act.Fori(0, NT) as i:
                        act.wait_ge(y_ps, i + 1)
                        act.sem_inc(s_tick, 1)
                        for g in range(2):
                            cp = nc.scalar.copy(feat[:, bass.ds(i * (SB * P) + g * HB, HB)], bank[2 + g][:, 0:HB])
                        cp.then_inc(lin, 1)
                        act.wait_ge(tr_ps, i + 1)
                        act.wait_ge(stored, SK * (i + 1))
                        act.sem_inc(s_tick, 1)
                        if not last:
                            nc.scalar.copy(acc[:, bass.ds(i * (SB * P), 4 * P)], bank[4][:, 0:4 * P])
                            nc.scalar.copy(acc[:, bass.ds(i * (SB * P) + 4 * P, 3 * P)], bank[5][:, 0:3 * P])
                        nc.scalar.copy(nodes[:, 0:4, :], bank[4][:, 0:512].rearrange("p (k f) -> p k f", f=D))
                        cp = nc.scalar.copy(nodes[:, 4:SB, :], bank[5][:, 0:3 * P].rearrange("p (k f) -> p k f", f=D))
                        if not last:
                            cp.then_inc(nodes_ready, 1)
                            act.sem_inc(y_done, 1)
                        else:
                            cp.then_inc(trc, 1)
                            act.wait_ge(stat, 5 * i + 5)
                            nc.scalar.activation(rstd[:], mv[:, :, 1], ACT.Sqrt, bias=eps[:, 0:1], scale=1.0).then_inc(sq, 1)
                            act.wait_ge(x1T_ps, i + 1)
                            act.sem_inc(s_tick, 1)
                            nc.scalar.copy(y[:, 0:512], bank[6][:, 0:512])
                            nc.scalar.copy(y[:, 512:SB * P], bank[7][:, 0:3 * P]).then_inc(x1T, 1)
                            act.wait_ge(h_ps, i + 1)
                            act.sem_inc(s_tick, 1)
                            nc.scalar.copy(hrow[:, 0:4, 0:D], bank[4][:, 0:512].rearrange("p (k f) -> p k f", f=D))
                            cp = nc.scalar.copy(hrow[:, 4:SB, 0:D], bank[5][:, 0:3 * P].rearrange("p (k f) -> p k f", f=D))
                            cp.then_inc(h_ready, 1)
                            act.wait_ge(h_ready, i + 1)
                            act.sem_inc(nodes_ready, 1)
                            act.sem_inc(y_done, 1)

                @block.sync
                def _(sp):
                    sp.sem_inc(stored, SK)
                    with sp.Fori(0, NT) as i:
                        turn = bass.ds(i * SB, SB)
                        if not last:
                            sp.wait_ge(nodes_ready, i + 2)
                            sp.sem_inc(s_tick, 1)
                            sp.dma_start(table[l + 1].rearrange("(k p) f -> p k f", p=P)[:, turn, :],
                                         nodes[:]).then_inc(stored, 16)
                        else:
                            sp.dma_start(resid[:], x.rearrange("(k p) f -> p k f", p=P)[:, turn, :]).then_inc(res_got, 16)
                            sp.wait_ge(x1_ready, i + 1)
                            sp.sem_inc(s_tick, 1)
                            sp.dma_start(x1_dram.rearrange("(k p) f -> p k f", p=P)[:, turn, :],
                                         nodes[:]).then_inc(stored, 16)
                            sp.wait_ge(hc, 3 * i + 2)
                            sp.sem_inc(s_tick, 1)
                            sp.dma_start(table_h.rearrange("(k p) f -> p k f", p=P)[:, turn, :],
                                         hrow[:]).then_inc(stored, 16)
                    sp.wait_ge(stored, SK * (NT + 1))

        with ExitStack() as c3:
            def sm(name):
                return ctx.enter_context(nc.semaphore(f"top_{name}"))
            neg_src = c3.enter_context(nc.sbuf_tensor("neg_src0", [P, NB], F32))
            line = c3.enter_context(nc.sbuf_tensor("top_line", [3, 1], F32))
            diag = c3.enter_context(nc.sbuf_tensor("top_diag", [3, 3], F32))
            spread = c3.enter_context(nc.sbuf_tensor("spread", [1, 2], F32))
            step, turned = sm("vector_step"), sm("tensor_step")
            block = c3.enter_context(nc.Block())

            @block.tensor
            def _(pe):
                pe.wait_ge(step, 4)
                nc.tensor.transpose(bank[0][0:3, 0:P], tops[:], ident[:]).then_inc(turned, 1)
                pe.wait_ge(step, 6)
                nc.tensor.matmul(bank[1][:, 0:3], ones[:], diag[:], start=True, stop=True).then_inc(turned, 1)

            @block.vector
            def _(dve):
                n = 0

                def link(ins):
                    nonlocal n
                    n += 1
                    ins.then_inc(step, 1)
                    dve.wait_ge(step, n)
                link(nc.vector.tensor_scalar(neg_src[:], a_src[:], -1.0, None, ALU.mult))
                link(nc.vector.tensor_reduce(tops[:, 0:1], a_src[:], AX.X, ALU.max))
                link(nc.vector.tensor_reduce(tops[:, 1:2], neg_src[:], AX.X, ALU.max))
                link(nc.vector.tensor_reduce(tops[:, 2:3], acc[:], AX.X, ALU.max, apply_absolute_value=True))
                dve.wait_ge(turned, 1)
                link(nc.vector.tensor_reduce(line[:], bank[0][0:3, 0:P], AX.X, ALU.max))
                link(nc.vector.tensor_scalar(diag[:], ident[0:3, 0:3], line[:, 0:1], None, ALU.mult))
                dve.wait_ge(turned, 2)
                link(nc.vector.tensor_copy(tops[:], bank[1][:, 0:3]))
                link(nc.vector.tensor_tensor(spread[:, 0:1], tops[0:1, 0:1], tops[0:1, 1:2], ALU.add))
                link(nc.vector.tensor_scalar(spread[:, 1:2], spread[:, 0:1], SPREAD, None, ALU.is_le))
                link(nc.vector.tensor_tensor(short[:], spread[:, 1:2], fast[:], ALU.mult))

        def short_way(eng):
            return eng.value_load(short[0:1, 0:1], min_val=0, max_val=1) > 0

        with ExitStack() as c3:
            def sm(name):
                return ctx.enter_context(nc.semaphore(f"att_{name}"))

            def ring(name, shape, dt=F32):
                return c3.enter_context(nc.sbuf_tensor(f"att_{name}", shape, dt))
            NS = 4
            UNITS = ((0, 4, 3), (4, 3, 2))
            NU = len(UNITS)
            MB = UNITS[0][1]
            HE = D + 1
            n_piece, n_mask, n_tmp = NS * QP * PH * P, 2 * 2 * QP * MB * P, 2 * PH * D
            assert (n_piece + n_mask) // 2 + n_tmp <= P * NCC
            room16 = shared[:].bitcast(F16)
            piece = room16[:, 0:n_piece].rearrange("p (c s n) -> p c s n", c=NS, s=QP)
            masks = room16[:, n_piece:n_piece + n_mask].rearrange("p (v k s b n) -> p v k s b n", v=2, k=2, s=QP, b=MB)
            tmp = shared[:, (n_piece + n_mask) // 2:(n_piece + n_mask) // 2 + n_tmp].rearrange("p (v b f) -> p v b f", v=2, b=PH)
            wh = ring("wh", [P, NB, 2, 2, HE], F16)
            ev = ring("ev", [P, QP, 2, 2, HE])
            fin = ring("fin", [P, QP, HE])
            line = ring("line", [NB, P])
            neg_src = ring("neg_src", [P, NB])
            q_top = ring("q_top", [P, NB])
            m_top = ring("m_top", [P, NB])
            z = ring("z", [P, 3, NB])
            f = ring("f", [P, 3, NB])
            e = ring("e", [P, 2, NB])
            es = ring("es", [P, 2, NB])
            ew = ring("ew", [P, 2, NB])
            neg_top = ring("neg_top", [P, 2])
            back = ring("back", [P, 1])
            row = feat
            step, e_ready, f_ready, turned, line_ready, neg_ready, line_out, row_in, hw_ready, high_ready, low_ready, col_ready = (
                sm("vector_step"), sm("e_ready"), sm("f_ready"), sm("a_dst_in_psum"), sm("line_ready"), sm("negated"), sm("line_stored"),
                sm("row_in"), sm("weighted"), sm("high_ready"), sm("low_ready"), sm("columns_ready"))
            pos_ready, rest_ready, rest_ready2, mask_used, sums_done, banks_read, halves, halves_link, rows_done = (
                sm("mask_ready"), sm("rest_ready"), sm("rest_ready_pool"), sm("masks_used"), sm("sums_ready"),
                sm("banks_read"), sm("halves_added"), sm("kinds_added"), sm("rows_updated"))
            got = [sm(f"piece_got{c}") for c in range(NS)]
            line_dram = nc.dram_tensor("a_dst_line", [NB, P], F32).ap()
            block = c3.enter_context(nc.Block())
            SLOT_USES = [sum(1 for c in range(PC) if c % NS == k) for k in range(NS)]

            def before(c):
                return c - NS if c >= NS else max(k for k in range(PC) if k % NS == c) - PC

            def arrivals(q, c):
                return 16 * (q * SLOT_USES[c % NS] + c // NS + 1)

            @block.sync
            def _(sp):
                with sp.If(short_way(sp)):
                    sp.wait_ge(line_ready, 1)
                    sp.dma_start(line_dram, line[:]).then_inc(line_out, 16)
                    sp.wait_ge(line_out, 16)
                    sp.dma_start(row[:], line_dram.rearrange("(a b) p -> a (b p)", a=1).partition_broadcast(P)).then_inc(row_in, 16)

                    def read(q, n):
                        for c in range(PC):
                            sp.wait_ge(rest_ready, (q * PC + before(c) + 1 + PC) * NU)
                            sp.wait_ge(rest_ready2, (q * PC + before(c) + 1 + PC) * NU)
                            sp.sem_inc(s_tick, 1)
                            sp.dma_start(piece[:, c % NS, 0:n, :], counts.rearrange("s l n -> l s n")[
                                :, bass.ds(q * QP, n), c * PH * P:(c + 1) * PH * P]).then_inc(got[c % NS], 16)

                    with sp.Fori(0, NQ - 1) as q:
                        read(q, QP)
                    read(NQ - 1, 1)
                with sp.Else():
                    sp.sem_inc(s_tick, 1)

            @block.vector
            def _(dve):
                with dve.If(short_way(dve)):
                    n_link = 0

                    def link(ins):
                        nonlocal n_link
                        n_link += 1
                        ins.then_inc(step, 1)
                        dve.wait_ge(step, n_link)
                    dve.sem_inc(rest_ready, PC * NU)
                    dve.sem_inc(rows_done, 1)
                    link(nc.vector.tensor_scalar(unit[:, 0:1], tops[:, 2:3], 2.0 ** -100, None, ALU.max))
                    bits = unit[:].bitcast(I32)
                    link(nc.vector.tensor_scalar(bits[:, 1:2], bits[:, 0:1], EXPONENT, None, ALU.bitwise_and))
                    link(nc.vector.tensor_scalar(bits[:, 2:3], bits[:, 1:2], -1.0, float(267 << 23), ALU.mult, ALU.add))
                    link(nc.vector.tensor_scalar(bits[:, 3:4], bits[:, 1:2], float(13 << 23), None, ALU.subtract))
                    link(nc.vector.tensor_scalar(back[:], unit[:, 2:3], 2.0 ** -14, None, ALU.mult))
                    nc.vector.tensor_scalar(neg_top[:, 0:1], tops[:, 0:1], -1.0, None, ALU.mult)
                    nc.vector.tensor_scalar(neg_top[:, 1:2], tops[:, 0:1], -0.2, None, ALU.mult).then_inc(neg_ready, 1)
                    nc.vector.tensor_scalar(neg_src[:], a_src[:], -1.0, None, ALU.mult)
                    link(nc.vector.tensor_scalar(q_top[:], a_dst[:], tops[:, 0:1], None, ALU.add))
                    link(nc.vector.scalar_tensor_tensor(out=m_top[:], in0=q_top[:], scalar=0.2, in1=q_top[:],
                                                        op0=ALU.mult, op1=ALU.max))
                    nc.vector.tensor_tensor(z[:, 0, :], q_top[:], m_top[:], ALU.subtract)
                    nc.vector.tensor_tensor(z[:, 2, :], peak[:], m_top[:], ALU.subtract)
                    link(nc.vector.scalar_tensor_tensor(out=z[:, 1, :], in0=q_top[:], scalar=0.2, in1=m_top[:],
                                                        op0=ALU.mult, op1=ALU.subtract))
                    dve.wait_ge(e_ready, 1)
                    nc.vector.tensor_scalar(ew[:], e[:], 2.0 ** 14, None, ALU.mult)
                    link(nc.vector.tensor_scalar(es[:], e[:], unit[:, 2:3], None, ALU.mult))
                    link(nc.vector.tensor_copy(wh[:, :, :, 0, D].rearrange("p b k -> p k b"), ew[:]))
                    nc.vector.tensor_tensor(wh[:, :, :, 1, D].rearrange("p b k -> p k b"), ew[:],
                                            wh[:, :, :, 0, D].rearrange("p b k -> p k b"), ALU.subtract).then_inc(col_ready, 1)
                    for c in range(PC):
                        blocks = slice(c * PH, (c + 1) * PH)
                        h = acc[:, c * PH * P:(c + 1) * PH * P].rearrange("p (b f) -> p b f", f=D)
                        for k in range(2):
                            if c > 0:
                                dve.wait_ge(low_ready, 2 * c + k - 1)
                            nc.vector.tensor_tensor(tmp[:, k, :, :], h, es[:, k, blocks].unsqueeze(2).to_broadcast([P, PH, D]),
                                                    ALU.mult).then_inc(hw_ready, 1)
                    dve.wait_ge(f_ready, 1)
                    link(nc.vector.tensor_scalar(f[:, 0:2, :], f[:, 0:2, :], unit[:, 3:4], None, ALU.mult))
                    dve.wait_ge(row_in, 16)

                    def group(q, n, ending):
                        at = bass.ds(q * (QP * P), n * P)
                        for c in range(PC):
                            dve.wait_ge(got[c % NS], arrivals(q, c))
                            for k, (h0, hn, hd) in enumerate(UNITS):
                                s = (q * PC + c) * NU + k
                                v = (c * NU + k) % 2
                                dve.wait_ge(mask_used, s + 1)
                                for h in range(hn):
                                    b = c * PH + h0 + h
                                    mk = nc.vector.scalar_tensor_tensor(
                                        out=masks[:, v, 0, 0:n, h, :], in0=row[:, at].rearrange("p (s n) -> p s n", n=P),
                                        scalar=neg_src[:, b:b + 1],
                                        in1=piece[:, c % NS, 0:n, (h0 + h) * P:(h0 + h + 1) * P],
                                        op0=ALU.is_gt, op1=ALU.mult)
                                mk.then_inc(pos_ready, 1)
                                dve.wait_ge(pos_ready, s + 1)
                                nc.vector.tensor_tensor(
                                    masks[:, v, 1, 0:n, 0:hd, :].rearrange("p s b n -> p s (b n)"),
                                    piece[:, c % NS, 0:n, h0 * P:(h0 + hd) * P],
                                    masks[:, v, 0, 0:n, 0:hd, :].rearrange("p s b n -> p s (b n)"),
                                    ALU.subtract).then_inc(rest_ready, 1)
                            if c == 1 and ending is not None:
                                finish(*ending)

                    def finish(q, n):
                        dve.wait_ge(halves, q + 2)
                        for d in range(n):
                            cols = acc[:, bass.ds(q * (QP * P) + d * P, P)]
                            nc.vector.scalar_tensor_tensor(out=cols, in0=cols, scalar=f[:, 2, bass.ds(q * QP + d, 1)],
                                                           in1=fin[:, d, 0:D], op0=ALU.mult, op1=ALU.add)
                        at = bass.ds(q * QP, n)
                        nc.vector.scalar_tensor_tensor(out=denom[:, at], in0=fin[:, 0:n, D], scalar=back[:, 0:1],
                                                       in1=f[:, 2, at], op0=ALU.mult, op1=ALU.add).then_inc(rows_done, 1)

                    dve.wait_ge(low_ready, 2 * PC)
                    group(0, QP, None)
                    with dve.Fori(1, NQ - 1) as q:
                        group(q, QP, (q - 1, QP))
                    group(NQ - 1, 1, (NQ - 2, QP))
                    finish(NQ - 1, 1)
                with dve.Else():
                    dve.sem_inc(s_tick, 1)

            @block.gpsimd
            def _(pool):
                with pool.If(short_way(pool)):
                    pool.sem_inc(rest_ready2, PC * NU)
                    pool.sem_inc(halves, 1)
                    for c in range(PC):
                        for k in range(2):
                            pool.wait_ge(high_ready, 2 * c + k + 1)
                            nc.gpsimd.tensor_tensor(wh[:, c * PH:(c + 1) * PH, k, 1, 0:D], tmp[:, k, :, :],
                                                    wh[:, c * PH:(c + 1) * PH, k, 0, 0:D], ALU.subtract).then_inc(low_ready, 1)

                    def group(q, n, ending):
                        for c in range(PC):
                            for k, (h0, hn, hd) in enumerate(UNITS):
                                s = (q * PC + c) * NU + k
                                v = (c * NU + k) % 2
                                pool.wait_ge(pos_ready, s + 1)
                                nc.gpsimd.tensor_tensor(
                                    masks[:, v, 1, 0:n, hd:hn, :].rearrange("p s b n -> p s (b n)"),
                                    piece[:, c % NS, 0:n, (h0 + hd) * P:(h0 + hn) * P],
                                    masks[:, v, 0, 0:n, hd:hn, :].rearrange("p s b n -> p s (b n)"),
                                    ALU.subtract).then_inc(rest_ready2, 1)
                            if c == 0 and ending is not None:
                                finish(*ending)

                    def finish(q, n):
                        pool.wait_ge(banks_read, q * (2 * QP) + 2 * n + 2 * QP)
                        nc.gpsimd.tensor_tensor(ev[:, 0:n, 0, :, :], ev[:, 0:n, 0, :, :], ev[:, 0:n, 1, :, :], ALU.add
                                                ).then_inc(halves_link, 1)
                        pool.wait_ge(halves_link, q + 1)
                        pool.wait_ge(rows_done, q + 1)
                        nc.gpsimd.tensor_tensor(fin[:, 0:n, :], ev[:, 0:n, 0, 0, :], ev[:, 0:n, 0, 1, :], ALU.add
                                                ).then_inc(halves, 1)

                    group(0, QP, None)
                    with pool.Fori(1, NQ - 1) as q:
                        group(q, QP, (q - 1, QP))
                    group(NQ - 1, 1, (NQ - 2, QP))
                    finish(NQ - 1, 1)
                with pool.Else():
                    pool.sem_inc(s_tick, 1)

            @block.tensor
            def _(pe):
                with pe.If(short_way(pe)):
                    pe.sem_inc(mask_used, 2)
                    nc.tensor.transpose(bank[0][0:NB, 0:P], a_dst[:], ident[:]).then_inc(turned, 1)
                    pe.wait_ge(line_ready, 1)
                    pe.wait_ge(col_ready, 1)

                    def group(q, n):
                        for c in range(PC):
                            for k, (h0, hn, hd) in enumerate(UNITS):
                                s = (q * PC + c) * NU + k
                                v = (c * NU + k) % 2
                                for kind in range(2):
                                    pe.wait_ge(low_ready, 2 * c + kind + 1)
                                    if c == 0 and k == 0:
                                        pe.wait_ge(banks_read, q * (2 * QP) + (kind + 1) * QP)
                                    if kind == 0:
                                        pe.wait_ge(pos_ready, s + 1)
                                    else:
                                        pe.wait_ge(rest_ready, s + 1 + PC * NU)
                                        pe.wait_ge(rest_ready2, s + 1 + PC * NU)
                                    for h in range(hn):
                                        b = c * PH + h0 + h
                                        for d in range(n):
                                            mm = nc.tensor.matmul(bank[2 * d + kind][:, 0:2 * HE], masks[:, v, kind, d, h, :],
                                                                  wh[:, b, kind, :, :].rearrange("p a f -> p (a f)"),
                                                                  start=(b == 0), stop=(b == NB - 1))
                                    if kind == 1:
                                        mm.then_inc(mask_used, 1)
                                    elif c == PC - 1 and k == NU - 1:
                                        mm.then_inc(sums_done, 1)

                    with pe.Fori(0, NQ - 1) as q:
                        group(q, QP)
                    group(NQ - 1, 1)
                with pe.Else():
                    pe.sem_inc(s_tick, 1)

            @block.scalar
            def _(act):
                with act.If(short_way(act)):
                    act.sem_inc(banks_read, 2 * QP)
                    act.wait_ge(turned, 1)
                    nc.scalar.copy(line[:], bank[0][0:NB, 0:P]).then_inc(line_ready, 1)
                    act.wait_ge(neg_ready, 1)
                    nc.scalar.activation(e[:, 0, :], a_src[:], ACT.Exp, bias=neg_top[:, 0:1], scale=1.0)
                    nc.scalar.activation(e[:, 1, :], a_src[:], ACT.Exp, bias=neg_top[:, 1:2], scale=0.2).then_inc(e_ready, 1)
                    act.wait_ge(step, 8)
                    nc.scalar.activation(f[:], z[:], ACT.Exp).then_inc(f_ready, 1)
                    for c in range(PC):
                        for k in range(2):
                            act.wait_ge(hw_ready, 2 * c + k + 1)
                            nc.scalar.copy(wh[:, c * PH:(c + 1) * PH, k, 0, 0:D], tmp[:, k, :, :]).then_inc(high_ready, 1)
                    act.wait_ge(step, 11)

                    def group(q, n):
                        for kind in range(2):
                            if kind == 0:
                                act.wait_ge(sums_done, q + 1)
                                act.wait_ge(halves, q + 1)
                            else:
                                act.wait_ge(mask_used, (q + 1) * PC * NU + 2)
                            act.sem_inc(s_tick, 1)
                            for d in range(n):
                                nc.scalar.activation(ev[:, d, kind, :, :].rearrange("p a f -> p (a f)"),
                                                     bank[2 * d + kind][:, 0:2 * HE], ACT.Copy,
                                                     scale=f[:, kind, bass.ds(q * QP + d, 1)]).then_inc(banks_read, 1)

                    with act.Fori(0, NQ - 1) as q:
                        group(q, QP)
                    group(NQ - 1, 1)
                with act.Else():
                    act.sem_inc(s_tick, 1)

        K = 6
        with ExitStack() as c3:
            def sm(name):
                return ctx.enter_context(nc.semaphore(f"gat_{name}"))

            def ring(name, shape, dt=F32):
                return c3.enter_context(nc.sbuf_tensor(f"gat_{name}", shape, dt))
            idx = ring("idx", [P, U, C], U32)
            rows = ring("rows", [P, U, C, ROW])
            other = ring("other", [P, 2, C, P])
            masked = ring("masked", [P, 2, C, P])
            eT = ring("eT", [P, 2, C * P])
            wT = ring("wT", [P, 2, C * P])
            wgt = ring("wgt", [P, 2, C, P])
            ad, top, mtop, fall, scale, wsum = (ring(f"s_{k}", [P, U]) for k in ("ad", "top", "mtop", "fall", "scale", "wsum"))
            idx_ready = [sm(f"idx_ready{u}") for u in range(U)]
            row_got = [sm(f"row_got{u}") for u in range(U)]
            other_ready, masked_ready, mT_ps, link, max_ready, z_ready, e_ready, w_ready, w_ps, wgt_ready, mm_done, added = (
                sm("mask_ready"), sm("masked_ready"), sm("maskedT_in_psum"), sm("vector_link"), sm("max_ready"),
                sm("z_ready"), sm("e_ready"), sm("weightsT_ready"), sm("weights_in_psum"), sm("weights_ready"), sm("sum_ready"),
                sm("sum_added"))
            block = c3.enter_context(nc.Block())

            @block.gpsimd
            def _(pool):
                with pool.If(short_way(pool)):
                    pool.sem_inc(s_tick, 1)
                with pool.Else():
                    n = pool.value_load(turns[0:1, 0:1], min_val=1, max_val=P * NCC // U - 2)
                    with pool.Fori(0, n) as i:
                        for u in range(U):
                            pool.wait_ge(idx_ready[u], i + 1)
                            pool.sem_inc(s_tick, 1)
                            for j in range(C):
                                pool.indirect_dma_start(rows[:, u, j, :], None, table_h,
                                                        bass.IndirectOffsetOnAxis(ap=idx[:, u, j:j + 1], axis=0)
                                                        ).then_inc(row_got[u], 16)

            @block.scalar
            def _(act):
                with act.If(short_way(act)):
                    act.sem_inc(s_tick, 1)
                with act.Else():
                    n = act.value_load(turns[0:1, 0:1], min_val=1, max_val=P * NCC // U - 2)

                    def fetch(i, u):
                        _, t = chunk_of(act, i * U + u)
                        t = t.with_bounds(min_val=0, max_val=TA - C)
                        nc.scalar.copy(idx[:, u, :], src[:, bass.ds(t, C)]).then_inc(idx_ready[u], 1)

                    def shift(s, u):
                        act.wait_ge(mT_ps, s + 3)
                        act.wait_ge(link, s * K + 2)
                        act.wait_ge(w_ps, s + 1)
                        nc.scalar.activation(eT[:, u % 2, :], bank[u % 2][:, 0:C * P], ACT.Identity,
                                             bias=ad[:, u:u + 1], scale=1.0).then_inc(z_ready, 1)

                    def weigh(s, u):
                        act.wait_ge(max_ready, s + 1)
                        nc.scalar.activation(scale[:, u:u + 1], fall[:, u:u + 1], ACT.Exp)
                        act.wait_ge(e_ready, s + 1)
                        nc.scalar.activation(wT[:, u % 2, :], eT[:, u % 2, :], ACT.Exp, bias=mtop[:, u:u + 1],
                                             scale=1.0, accum_out=wsum[:, u:u + 1]).then_inc(w_ready, 1)

                    def keep(s, u):
                        act.wait_ge(w_ps, s + 3)
                        act.sem_inc(s_tick, 1)
                        act.wait_ge(mm_done, s + U - 1)
                        nc.scalar.copy(wgt[:, u % 2, :, :], bank[2 + u % 2][:, 0:C * P].rearrange("p (j d) -> p j d", d=P)
                                       ).then_inc(wgt_ready, 1)

                    for u in range(U):
                        fetch(0, u)
                    with act.Fori(0, n) as i:
                        for ph in range(U + 3):
                            if 1 <= ph <= U:
                                shift(i * U + ph - 1, ph - 1)
                            if 2 <= ph <= U + 1:
                                keep(i * U + ph - 2, ph - 2)
                            if 1 <= ph <= U:
                                weigh(i * U + ph - 1, ph - 1)
                            if ph >= 3:
                                act.wait_ge(mm_done, i * U + ph - 3 + U + 1)
                                act.sem_inc(s_tick, 1)
                                fetch(i + 1, ph - 3)

            @block.vector
            def _(dve):
                with dve.If(short_way(dve)):
                    dve.sem_inc(s_tick, 1)
                with dve.Else():
                    n = dve.value_load(turns[0:1, 0:1], min_val=1, max_val=P * NCC // U - 2)
                    with dve.Fori(0, n) as i:
                        col = [None] * U

                        def mask(s, u):
                            b, t = chunk_of(dve, s)
                            t = t.with_bounds(min_val=0, max_val=TA - C)
                            col[u] = b.with_bounds(min_val=0, max_val=NB - 1)
                            nc.vector.scalar_tensor_tensor(
                                out=other[:, u % 2, :, :],
                                in0=dst[:, bass.ds(t, C)].unsqueeze(2).to_broadcast([P, C, P]),
                                scalar=base[:, bass.ds(col[u], 1)],
                                in1=iota[:].unsqueeze(1).to_broadcast([P, C, P]),
                                op0=ALU.subtract, op1=ALU.not_equal).then_inc(other_ready, 1)
                            dve.wait_ge(other_ready, s + 1)
                            dve.wait_ge(row_got[u], (i + 1) * G16)
                            dve.wait_ge(mT_ps, s + 1)
                            nc.vector.scalar_tensor_tensor(
                                out=masked[:, u % 2, :, :], in0=other[:, u % 2, :, :], scalar=NEG,
                                in1=rows[:, u, :, D:D + 1].to_broadcast([P, C, P]), op0=ALU.mult, op1=ALU.add
                            ).then_inc(masked_ready, 1)

                        def maximum(s, u):
                            c, a, m = bass.ds(col[u], 1), ad[:, u:u + 1], top[:, u:u + 1]
                            dve.wait_ge(mT_ps, s + 3)
                            nc.vector.tensor_reduce(m, bank[u % 2][:, 0:C * P], AX.X, ALU.max).then_inc(link, 1)
                            nc.vector.tensor_copy(a, a_dst[:, c]).then_inc(link, 1)
                            dve.wait_ge(link, s * K + 2)
                            nc.vector.tensor_tensor(m, m, a, ALU.add).then_inc(link, 1)
                            dve.wait_ge(link, s * K + 3)
                            nc.vector.scalar_tensor_tensor(out=m, in0=m, scalar=0.2, in1=m, op0=ALU.mult, op1=ALU.max
                                                           ).then_inc(link, 1)
                            dve.wait_ge(link, s * K + 4)
                            nc.vector.tensor_tensor(m, m, peak[:, c], ALU.max).then_inc(link, 1)
                            dve.wait_ge(link, s * K + 5)
                            nc.vector.tensor_scalar(mtop[:, u:u + 1], m, -1.0, None, ALU.mult)
                            nc.vector.tensor_tensor(fall[:, u:u + 1], peak[:, c], m, ALU.subtract).then_inc(max_ready, 1)
                            dve.wait_ge(max_ready, s + 1)
                            dve.sem_inc(s_tick, 1)
                            nc.vector.tensor_copy(peak[:, c], m).then_inc(link, 1)
                            dve.wait_ge(z_ready, s + 3)
                            nc.vector.scalar_tensor_tensor(out=eT[:, u % 2, :], in0=eT[:, u % 2, :], scalar=0.2,
                                                           in1=eT[:, u % 2, :], op0=ALU.mult, op1=ALU.max).then_inc(e_ready, 1)

                        def add(s, u):
                            c = bass.ds(col[u], 1)
                            dve.wait_ge(mm_done, s + U + 1)
                            dve.wait_ge(added, s + 2)
                            nc.vector.scalar_tensor_tensor(out=denom[:, c], in0=denom[:, c], scalar=scale[:, u:u + 1],
                                                           in1=wsum[:, u:u + 1], op0=ALU.mult, op1=ALU.add)
                            cols = acc[:, bass.ds(col[u] * P, P)]
                            nc.vector.scalar_tensor_tensor(out=cols, in0=cols, scalar=scale[:, u:u + 1],
                                                           in1=bank[4 + u % 2][:, 0:P], op0=ALU.mult, op1=ALU.add
                                                           ).then_inc(added, 1)

                        for ph in range(U + 3):
                            if ph < U:
                                mask(i * U + ph, ph)
                            if 1 <= ph <= U:
                                maximum(i * U + ph - 1, ph - 1)
                            if ph >= 3:
                                add(i * U + ph - 3, ph - 3)

            @block.tensor
            def _(pe):
                with pe.If(short_way(pe)):
                    pe.sem_inc(s_tick, 1)
                with pe.Else():
                    n = pe.value_load(turns[0:1, 0:1], min_val=1, max_val=P * NCC // U - 2)
                    pe.sem_inc(mm_done, U)
                    for s2 in (added, w_ps, mT_ps, z_ready, wgt_ready):
                        pe.sem_inc(s2, 2)

                    def turn_masked(s, u):
                        pe.wait_ge(masked_ready, s + 1)
                        pe.wait_ge(z_ready, s + 1)
                        for j in range(C):
                            tr = nc.tensor.transpose(bank[u % 2][:, j * P:(j + 1) * P], masked[:, u % 2, j, :], ident[:])
                        tr.then_inc(mT_ps, 1)

                    def turn_weights(s, u):
                        pe.wait_ge(w_ready, s + 1)
                        pe.wait_ge(wgt_ready, s + 1)
                        for j in range(C):
                            tr = nc.tensor.transpose(bank[2 + u % 2][:, j * P:(j + 1) * P],
                                                     wT[:, u % 2, j * P:(j + 1) * P], ident[:])
                        tr.then_inc(w_ps, 1)

                    def product(s, u):
                        pe.wait_ge(wgt_ready, s + 3)
                        pe.wait_ge(added, s + 1)
                        for j in range(C):
                            mm = nc.tensor.matmul(bank[4 + u % 2][:, 0:P], wgt[:, u % 2, j, :], rows[:, u, j, 0:D],
                                                  start=(j == 0), stop=(j == C - 1))
                        mm.then_inc(mm_done, 1)

                    with pe.Fori(0, n) as i:
                        for ph in range(U + 3):
                            if ph >= 3:
                                product(i * U + ph - 3, ph - 3)
                            if 2 <= ph <= U + 1:
                                turn_weights(i * U + ph - 2, ph - 2)
                            if ph < U:
                                turn_masked(i * U + ph, ph)

        with ExitStack() as c4:
            def sm(name):
                return ctx.enter_context(nc.semaphore(f"out_{name}"))

            def tile(name, shape, dt=F32):
                return c4.enter_context(nc.sbuf_tensor(f"out_{name}", shape, dt))
            nodes = tile("nodes", [P, SB, D])
            resid = tile("resid", [P, SB, D])
            stats = tile("stats", [P, SB, 6])
            mv = tile("mv", [P, SB, 2])
            rstd = tile("rstd", [P, SB])
            res_got, lnk, sq, rows_ready, stored = sm("resid_got"), sm("link"), sm("sqrt"), sm("rows_ready"), sm("stored")
            block = c4.enter_context(nc.Block())
            FULL = NT - 1
            NL = 6

            @block.sync
            def _(sp):
                sp.sem_inc(stored, 16)
                x1v = x1_dram.rearrange("(k p) f -> p k f", p=P)
                with sp.Fori(0, NT) as i:
                    sp.wait_ge(rows_ready, i + 1)
                    sp.sem_inc(s_tick, 1)
                    sp.dma_start(resid[:], x1v[:, bass.ds(i * SB, SB), :]).then_inc(res_got, 16)

            @block.scalar
            def _(act):
                outv = out[0:FULL * SB * P, :].rearrange("(k p) f -> p k f", p=P)
                with act.Fori(0, FULL) as i:
                    act.wait_ge(lnk, NL * i + NL - 1)
                    act.sem_inc(s_tick, 1)
                    nc.scalar.activation(rstd[:], mv[:, :, 1], ACT.Sqrt, bias=eps[:, 0:1], scale=1.0).then_inc(sq, 1)
                    act.wait_ge(rows_ready, i + 2)
                    act.dma_start(outv[:, bass.ds(i * SB, SB), :], nodes[:]).then_inc(stored, 16)
                act.wait_ge(lnk, NL * FULL + NL - 1)
                nc.scalar.activation(rstd[:], mv[:, :, 1], ACT.Sqrt, bias=eps[:, 0:1], scale=1.0).then_inc(sq, 1)
                act.wait_ge(rows_ready, NT + 1)
                rest = out[FULL * SB * P:FULL * SB * P + (SB - 1) * P, :].rearrange("(k p) f -> p k f", p=P)
                act.dma_start(rest, nodes[:, 0:SB - 1, :]).then_inc(stored, 16)
                act.dma_start(out[(NB - 1) * P:n_nodes, :], nodes[0:LAST, SB - 1, :]).then_inc(stored, 16)
                act.wait_ge(stored, 16 * (1 + FULL + 2))

            @block.vector
            def _(dve):
                dve.sem_inc(rows_ready, 1)
                nc.vector.reciprocal(denom[:], denom[:]).then_inc(s_dve, 1)
                dve.wait_ge(s_dve, 1 + NT + 1)
                with dve.Fori(0, NT) as i:
                    dve.wait_ge(res_got, 16 * (i + 1))
                    nc.vector.tensor_tensor(resid[:], resid[:], bias_row[:].unsqueeze(1).to_broadcast([P, SB, D]),
                                            ALU.add).then_inc(lnk, 1)
                    dve.wait_ge(lnk, NL * i + 1)
                    for k in range(SB):
                        a = nc.vector.scalar_tensor_tensor(
                            out=resid[:, k, :], in0=acc[:, bass.ds(i * (SB * P) + k * P, P)],
                            scalar=denom[:, bass.ds(i * SB + k, 1)], in1=resid[:, k, :], op0=ALU.mult, op1=ALU.add)
                    a.then_inc(lnk, 1)
                    dve.wait_ge(lnk, NL * i + 2)
                    for k in range(SB):
                        bn = nc.vector.bn_stats(out=stats[:, k, :], in_=resid[:, k, :])
                    bn.then_inc(lnk, 1)
                    dve.wait_ge(lnk, NL * i + 3)
                    dve.sem_inc(s_tick, 1)
                    for k in range(SB):
                        bn = nc.vector.bn_aggr(out=mv[:, k, :], in_=stats[:, k, :])
                    bn.then_inc(lnk, 2)
                    dve.wait_ge(sq, i + 1)
                    nc.vector.reciprocal(rstd[:], rstd[:]).then_inc(lnk, 1)
                    dve.wait_ge(lnk, NL * i + NL)
                    dve.wait_ge(stored, 16 * (i + 1))
                    for k in range(SB):
                        nm = nc.vector.tensor_scalar(nodes[:, k, :], resid[:, k, :], mv[:, k, 0:1],
                                                     rstd[:, k:k + 1], ALU.subtract, ALU.mult)
                    nm.then_inc(rows_ready, 1)


def kernel(x, src, dst, edge_attr_32, L0_gnn_Wm, L0_gnn_bm, L1_gnn_W, L1_gnn_att_src, L1_gnn_att_dst, L1_gnn_bias):
    import concourse.bacc as bacc
    from concourse.bass_utils import run_bass_kernel_spmd as run

    x, src, dst, ea = (np.asarray(a) for a in (x, src, dst, edge_attr_32))
    n, e = x.shape[0], src.shape[0]
    nb, tiles, ta, _ = shapes(n, e)
    xp = np.concatenate([x, np.zeros((nb * P - n, D), x.dtype)])
    ee = (ta + GT) * P
    src_line = np.concatenate([src, np.zeros(ee - e, src.dtype)])
    dst_line = np.concatenate([dst, np.full(ee + 1 - e, NO_NODE, dst.dtype)])
    src_p, dst_p = (a[:ta * P].reshape(ta, P) for a in (src_line, dst_line))
    ea_p = np.concatenate([ea, np.zeros((ee - e, EA), ea.dtype)])
    ea_p = np.concatenate([ea_p, np.ones((ee, 1), ea.dtype)], axis=1)
    W0 = np.concatenate([np.asarray(L0_gnn_Wm).transpose(0, 2, 1), np.asarray(L0_gnn_bm)[:, None, :]], axis=1)
    arrays = {
        "in_x": xp, "in_xT": xp.T, "in_srcT": src_p.T, "in_dstT": dst_p.T, "in_src_line": src_line,
        "in_dst_line": dst_line, "in_ea": ea_p,
        "in_W0": W0, "in_W1": np.asarray(L1_gnn_W),
        "in_att": np.stack([np.asarray(L1_gnn_att_src), np.asarray(L1_gnn_att_dst)]),
        "in_bias": np.asarray(L1_gnn_bias)[None, :],
    }
    arrays = {k: np.ascontiguousarray(a) for k, a in arrays.items()}
    nc = bacc.Bacc("TRN2", target_bir_lowering=False, num_devices=1)
    args = [nc.dram_tensor(k, a.shape, mybir.dt.from_np(a.dtype), kind="ExternalInput").ap() for k, a in arrays.items()]
    out = nc.dram_tensor("out", [n, D], F32, kind="ExternalOutput").ap()
    build(nc, *args, out)
    return run(nc, [arrays], core_ids=[0]).results[0]["out"]
```

```python
from contextlib import ExitStack

import numpy as np
import concourse.bass as bass
from concourse import mybir

F32 = mybir.dt.float32
F16 = mybir.dt.float16
I32 = mybir.dt.int32
U32 = mybir.dt.uint32
ALU = mybir.AluOpType
ACT = mybir.ActivationFunctionType
AX = mybir.AxisListType

P = 128
D = 128
EA = 32
EA1 = EA + 1
C = 3
U = 4
SB = 7
HB = SB * P // 2
ROW = D + 4
W = 16
GT = 3
GP = P // W
QP = 4
INFO = 3
EXPONENT = 0x7F800000
NO_NODE = 8191
NEG = -1.0e30
EPS = 1e-5
SPREAD = 10.0


def shapes(n_nodes, n_edges):
    nb = -(-n_nodes // P)
    tiles = -(-n_edges // P)
    ta = -(-(tiles + C) // 8) * 8
    most = nb * -(-tiles // C) + 2 * U
    nc_cols = -(-most // P)
    return nb, tiles, ta, nc_cols


def build(nc, x, xT, srcT, dstT, src_line, dst_line, ea, W0, W1, att, bias, out):
    n_nodes = out.shape[0]
    NB = x.shape[0] // P
    NP = NB * P
    TA = srcT.shape[1]
    NT = NB // SB
    LAST = n_nodes - (NB - 1) * P
    NCC = shapes(n_nodes, TA * P)[3]
    RJ = 8
    RP = TA // RJ
    BIG_T = float(TA)
    EE = ea.shape[0]
    RW = EE // P
    assert RW * P == EE and EE >= (TA + GT) * P and dst_line.shape[0] == EE + 1
    dst_rows = dst_line[0:TA * P].rearrange("(t e) -> t e", e=P)
    ea_tiles = ea[0:TA * P, :].rearrange("(t p) f -> p t f", p=P)
    assert NB % SB == 0 and TA < 1024 and NB <= P

    table = [x, nc.dram_tensor("table_1", [NP, D], F32).ap(), nc.dram_tensor("table_2", [NP, D], F32).ap()]
    table_h = nc.dram_tensor("table_h", [NP, ROW], F32).ap()
    x1_dram = nc.dram_tensor("x1_rows", [NP, D], F32).ap()
    lohi_dram = nc.dram_tensor("tile_lo_hi", [2, TA], F32).ap()
    NG = NP // W
    GR = 4
    GQ = NG // GR
    NPAN = NG // GP
    HC = NB * W
    HA = (NB + 1) // 2
    PC = 7
    PH = NB // PC
    assert NG == GR * GQ and NPAN * GP == NG and NPAN == NB and NPAN % (2 * QP) == 1 and HA * W <= 512 and PC * PH == NB and GQ <= P
    group_dram = nc.dram_tensor("group_list", [NG], I32).ap()
    counts = nc.dram_tensor("counts", [NPAN, P, NB * P], F16).ap()
    info_dram = nc.dram_tensor("edge_info", [EE, INFO], F32).ap()
    chunk_dram = nc.dram_tensor("chunk_list", [P * NCC], I32).ap()

    with ExitStack() as ctx:
        def sb(name, shape, dt=F32):
            return ctx.enter_context(nc.sbuf_tensor(name, shape, dt))

        def ps(name, shape):
            return ctx.enter_context(nc.psum_tensor(name, shape, F32))

        def sem(name):
            return ctx.enter_context(nc.semaphore(name))

        shared = sb("shared", [P, P * NCC])
        chunks = shared[96:97, :].bitcast(I32)
        eaT = shared[0:EA1, 0:NP]
        turns = sb("turns", [1, 1], I32)
        fast = sb("fast", [1, 1], I32)
        groups = sb("groups", [1, NG], I32)
        src = sb("src", [P, TA], I32)
        unit = sb("unit", [P, 4])
        dst = sb("dst", [P, TA])
        feat = sb("feat", [P, NP])
        acc = sb("acc", [P, NP])
        ident = sb("ident", [P, P])
        ones = sb("ones", [3, P])
        iota = sb("iota", [P, P])
        base = sb("base", [P, NB])
        w0 = sb("w0", [P, 3, 2, D])
        w0e = sb("w0e", [EA1, 3, D])
        sel = sb("sel", [EA1, P])
        w1 = sb("w1", [P, D])
        att_row = sb("att_row", [P, 2, D])
        bias_row = sb("bias_row", [P, D])
        a_src = sb("a_src", [P, NB])
        a_dst = sb("a_dst", [P, NB])
        tops = sb("tops", [P, 3])
        short = sb("short", [1, 1], I32)
        peak = sb("peak", [P, NB])
        denom = sb("denom", [P, NB])
        eps = sb("eps", [P, 1])
        bank = [ps(f"bank{i}", [P, 512]) for i in range(8)]

        s_in = sem("inputs_loaded")
        s_tick = sem("wait_carrier")
        s_const = sem("constants_ready")
        s_dve = sem("vector_step")

        idx_ready = [sem(f"idx_ready{u}") for u in range(U)]
        row_got = [sem(f"row_got{u}") for u in range(U)]
        ES = 4
        ea_got = [sem(f"ea_got{k}") for k in range(max(ES, U))]
        G16 = 16 * C

        NIN = 16
        with ExitStack() as c0:
            def sb0(name, shape, dt=F32):
                return c0.enter_context(nc.sbuf_tensor(name, shape, dt))
            dr = sb0("dst_rows_sb", [RP, RJ, P], I32)
            di = sb0("dst_int", [P, TA], I32)
            lohi = sb0("lohi", [RP, 2, RJ])
            lo_b = sb0("lo_b", [GQ, TA])
            hi_b = sb0("hi_b", [GQ, TA])
            below, hit, t1, t2 = (acc[0:GQ, k * TA:(k + 1) * TA] for k in range(4))
            prod = acc[0:GQ, 4 * TA:6 * TA].rearrange("p (k t) -> p k t", k=2)
            glo = sb0("glo", [GQ, GR])
            ghi = sb0("ghi", [GQ, GR])
            gt = sb0("gt", [GQ, 4, GR])
            gti = sb0("gti", [GQ, 3, GR], I32)
            dn = sb0("dst_line_sb", [P, RW + 1], I32)
            sn = sb0("src_line_sb", [P, RW], I32)
            parts = sb0("parts", [P, 2, RW], I32)
            info = sb0("info", [P, RW, INFO])
            worst = sb0("worst", [P, 1])
            edge_rows = sb0("edge_rows", [GQ, 2, GR, P], I32)
            which = sb0("which", [GQ, 2, GR])
            whichi = sb0("whichi", [GQ, 2, GR], U32)
            under = sb0("under", [GQ, 2, GR, P])
            num = sb0("num", [GQ, 4, GR])
            s_line, s_info, s_which, s_rows = sem("lines_loaded"), sem("info_ready"), sem("tiles_found"), sem("edge_rows_in")
            blk = sb0("blk", [NB, 2])
            rng = sb0("rng", [NB, 8])
            rngi = sb0("rngi", [NB, 2], I32)
            tri = sb0("tri", [NB, NB + 1])
            nbc = sb0("nbc", [NB, 2, P])
            cum = sb0("cum", [P, NB + 1])
            q = sb0("q", [P, NB])
            dq = sb0("dq", [P, NB])
            sidx = sb0("sidx", [P, NCC])
            step = sb0("step", [P, NCC])
            v = sb0("v", [P, NCC])
            vi = sb0("vi", [P, NCC], I32)
            turns_i = sb0("turns_i", [P, 2], I32)
            s_lohi, s_back, s_list, s_rng, s_cum = (sem("lohi_stored"), sem("lohi_back"), sem("list_stored"),
                                                    sem("ranges_ready"), sem("cum_ready"))
            s_ones = sem("iotas_ready")
            s_c = sem("stage0_step")
            block = c0.enter_context(nc.Block())

            @block.sync
            def _(sp):
                sp.dma_start(dr[:], dst_rows.rearrange("(p j) e -> p j e", j=RJ)).then_inc(s_back, 16)
                line = dst_line[0:EE]
                sp.dma_start(dn[:, 0:RW], line.rearrange("(p e) -> p e", e=RW)).then_inc(s_line, 16)
                with nc.allow_non_contiguous_dma(reason="each partition's next dst"):
                    sp.dma_start(dn[:, RW:RW + 1], dst_line[1:EE + 1].rearrange("(p e) -> p e", e=RW)[:, RW - 1:RW]).then_inc(s_line, 16)
                sp.dma_start(sn[:], src_line.rearrange("(p e) -> p e", e=RW)).then_inc(s_line, 16)
                sp.dma_start(di[:], dstT).then_inc(s_in, 16)
                sp.dma_start(src[:], srcT).then_inc(s_in, 16)
                sp.dma_start(feat[:], xT).then_inc(s_in, 16)
                for l in range(3):
                    sp.dma_start(w0[:, l, :, :], W0[l, 0:2 * D, :].rearrange("(k p) f -> p k f", p=P)).then_inc(s_in, 16)
                    sp.dma_start(w0e[:, l, :], W0[l, 2 * D:2 * D + EA1, :]).then_inc(s_in, 16)
                sp.dma_start(w1[:], W1).then_inc(s_in, 16)
                for k in range(2):
                    sp.dma_start(att_row[:, k, :], att[k:k + 1, :].partition_broadcast(P)).then_inc(s_in, 16)
                sp.dma_start(bias_row[:], bias.partition_broadcast(P)).then_inc(s_in, 16)
                sp.wait_ge(s_c, 2)
                for k in range(2):
                    sp.dma_start(lohi_dram[k].rearrange("(p j) -> p j", j=RJ), lohi[:, k, :]).then_inc(s_lohi, 16)
                sp.wait_ge(s_lohi, 32)
                sp.dma_start(lo_b[:], lohi_dram[0:1, :].partition_broadcast(GQ)).then_inc(s_back, 16)
                sp.dma_start(hi_b[:], lohi_dram[1:2, :].partition_broadcast(GQ)).then_inc(s_back, 16)
                sp.wait_ge(s_info, 2)
                sp.dma_start(info_dram.rearrange("(p e) f -> p (e f)", e=RW), info[:].rearrange("p e f -> p (e f)")).then_inc(s_in, 16)
                sp.wait_ge(s_list, 1)
                sp.dma_start(chunk_dram.rearrange("(p c) -> p c", c=NCC), vi[:]).then_inc(s_lohi, 16)
                with nc.allow_non_contiguous_dma(reason="one tile number of each group"):
                    sp.dma_start(group_dram.rearrange("(r p) -> p r", p=GQ), gti[:, 0, :]).then_inc(s_lohi, 16)
                sp.wait_ge(s_lohi, 64)
                sp.dma_start(groups[:], group_dram.rearrange("(a n) -> a n", a=1)).then_inc(s_in, 16)
                sp.dma_start(chunks, chunk_dram.rearrange("(a n) -> a n", a=1)).then_inc(s_in, 16)
                sp.wait_ge(s_in, 16 * NIN)

            @block.gpsimd
            def _(pool):
                nc.gpsimd.memset(tri[:], 1.0).then_inc(s_tick, 1)
                nc.gpsimd.memset(ident[:], 0.0).then_inc(s_tick, 1)
                nc.gpsimd.memset(sel[:], 0.0).then_inc(s_tick, 1)
                nc.gpsimd.iota(iota[:], [[1, P]], channel_multiplier=0, allow_small_or_imprecise_dtypes=True).then_inc(s_ones, 1)
                nc.gpsimd.iota(base[:], [[P, NB]], channel_multiplier=0, allow_small_or_imprecise_dtypes=True).then_inc(s_ones, 1)
                nc.gpsimd.iota(blk[:], [[P - 1, 2]], channel_multiplier=P, allow_small_or_imprecise_dtypes=True).then_inc(s_ones, 1)
                nc.gpsimd.iota(t1, [[1, TA]], base=1, channel_multiplier=0, allow_small_or_imprecise_dtypes=True).then_inc(s_ones, 1)
                nc.gpsimd.iota(t2, [[-1, TA]], base=TA, channel_multiplier=0, allow_small_or_imprecise_dtypes=True).then_inc(s_ones, 1)
                nc.gpsimd.iota(glo[:], [[W * GQ, GR]], channel_multiplier=W, allow_small_or_imprecise_dtypes=True).then_inc(s_ones, 1)
                nc.gpsimd.iota(ghi[:], [[W * GQ, GR]], base=W - 1, channel_multiplier=W, allow_small_or_imprecise_dtypes=True).then_inc(s_ones, 1)
                nc.gpsimd.iota(sidx[:], [[1, NCC]], channel_multiplier=NCC, allow_small_or_imprecise_dtypes=True).then_inc(s_ones, 1)
                pool.wait_ge(s_tick, 3)
                nc.gpsimd.affine_select(out=ident[:], in_=ident[:], compare_op=ALU.not_equal, fill=1.0, base=0,
                                        pattern=[[-1, P]], channel_multiplier=1).then_inc(s_const, 1)
                nc.gpsimd.affine_select(out=tri[:], in_=tri[:], compare_op=ALU.is_gt, fill=0.0, base=0,
                                        pattern=[[1, NB + 1]], channel_multiplier=-1).then_inc(s_const, 1)
                nc.gpsimd.affine_select(out=sel[:], in_=sel[:], compare_op=ALU.not_equal, fill=1.0, base=-EA,
                                        pattern=[[0, P]], channel_multiplier=1).then_inc(s_const, 1)

                for r in range(GR):
                    for j in range(2):
                        if r == 0 and j == 0:
                            pool.wait_ge(s_which, 1)
                            pool.sem_inc(s_tick, 1)
                        pool.indirect_dma_start(edge_rows[:, j, r, :], None, dst_rows,
                                                bass.IndirectOffsetOnAxis(ap=whichi[:, j, r:r + 1], axis=0)).then_inc(s_rows, 16)

            @block.vector
            def _(dve):
                k = [0]

                def link(ins):
                    k[0] += 1
                    ins.then_inc(s_c, 1)
                    dve.wait_ge(s_c, k[0])

                dve.wait_ge(s_back, 16)
                nc.vector.tensor_reduce(lohi[:, 0, :], dr[:], AX.X, ALU.min).then_inc(s_c, 1)
                nc.vector.tensor_reduce(lohi[:, 1, :], dr[:], AX.X, ALU.max).then_inc(s_c, 1)
                k[0] = 2
                nc.vector.memset(eaT, 0.0)
                nc.vector.memset(ones[:], 1.0)
                nc.vector.memset(denom[:], 1.0)
                link(nc.vector.memset(eps[:], EPS))
                dve.wait_ge(s_ones, 8)
                dve.wait_ge(s_back, 48)
                def tiles_of(n, first, final, end, start):
                    link(nc.vector.tensor_scalar(below[0:n, :], lo_b[0:n, :], final, None, ALU.is_le))
                    link(nc.vector.scalar_tensor_tensor(out=hit[0:n, :], in0=hi_b[0:n, :], scalar=first,
                                                        in1=below[0:n, :], op0=ALU.is_ge, op1=ALU.mult))
                    link(nc.vector.tensor_tensor(prod[0:n, 0, :], hit[0:n, :], t1[0:n, :], ALU.mult))
                    link(nc.vector.tensor_tensor(prod[0:n, 1, :], hit[0:n, :], t2[0:n, :], ALU.mult))
                    link(nc.vector.tensor_reduce(end, prod[0:n, 0, :], AX.X, ALU.max))
                    link(nc.vector.tensor_reduce(start, prod[0:n, 1, :], AX.X, ALU.max))

                tiles_of(NB, blk[:, 0:1], blk[:, 1:2], rng[:, 0:1], rng[:, 1:2])
                for r in range(GR):
                    tiles_of(GQ, glo[:, r:r + 1], ghi[:, r:r + 1], gt[:, 0, r:r + 1], gt[:, 1, r:r + 1])
                link(nc.vector.tensor_scalar(gt[:, 2, :], gt[:, 1, :], -1.0, BIG_T, ALU.mult, ALU.add))
                link(nc.vector.tensor_scalar(which[:, 0, :], gt[:, 2, :], BIG_T - 1.0, None, ALU.min))
                link(nc.vector.tensor_scalar(which[:, 1, :], gt[:, 0, :], -1.0, 0.0, ALU.add, ALU.max))
                nc.vector.tensor_copy(whichi[:], which[:]).then_inc(s_which, 1)
                dve.wait_ge(s_line, 48)
                link(nc.vector.tensor_tensor(info[:, :, 0], dn[:, 0:RW], dn[:, 1:RW + 1], ALU.is_gt))
                link(nc.vector.tensor_reduce(worst[:], info[:, :, 0], AX.X, ALU.max))
                link(nc.vector.tensor_scalar(worst[:], worst[:], 2.0 ** 20, None, ALU.mult))
                link(nc.vector.tensor_scalar(parts[:, 0, :], sn[:], 7, None, ALU.arith_shift_right))
                link(nc.vector.tensor_scalar(parts[:, 1, :], dn[:, 0:RW], W - 1, None, ALU.bitwise_and))
                nc.vector.scalar_tensor_tensor(out=info[:, :, 0], in0=parts[:, 0, :], scalar=float(W), in1=parts[:, 1, :],
                                               op0=ALU.mult, op1=ALU.add).then_inc(s_info, 1)
                dve.wait_ge(s_info, 1)
                link(nc.vector.tensor_scalar(parts[:, 1, :], sn[:], P - 1, None, ALU.bitwise_and))
                nc.vector.tensor_copy(info[:, :, 1], parts[:, 1, :])
                nc.vector.tensor_copy(info[:, :, 2], dn[:, 0:RW]).then_inc(s_info, 1)
                dve.wait_ge(s_rows, 16 * 2 * GR)
                for r in range(GR):
                    nc.vector.tensor_scalar(under[:, 0, r, :], edge_rows[:, 0, r, :], glo[:, r:r + 1], None, ALU.is_lt)
                    un = nc.vector.tensor_scalar(under[:, 1, r, :], edge_rows[:, 1, r, :], ghi[:, r:r + 1], None, ALU.is_le)
                link(un)
                link(nc.vector.tensor_reduce(num[:, 0:2, :], under[:], AX.X, ALU.add))
                link(nc.vector.scalar_tensor_tensor(out=num[:, 2:4, :], in0=which[:], scalar=float(P), in1=num[:, 0:2, :],
                                                    op0=ALU.mult, op1=ALU.add))
                link(nc.vector.tensor_tensor(num[:, 0, :], num[:, 3, :], num[:, 2, :], ALU.subtract))
                nc.vector.tensor_copy(gti[:, 0, :], num[:, 2, :])
                link(nc.vector.tensor_copy(gti[:, 1, :], num[:, 0, :]))
                link(nc.vector.tensor_scalar(gti[:, 2, :], gti[:, 0, :], 9, None, ALU.logical_shift_left))
                link(nc.vector.tensor_tensor(gti[:, 0, :], gti[:, 2, :], gti[:, 1, :], ALU.bitwise_or))
                link(nc.vector.tensor_scalar(num[:, 1, :], num[:, 0, :], 0.5, 2.0 ** 20, ALU.is_lt, ALU.mult))
                link(nc.vector.scalar_tensor_tensor(out=num[:, 1, :], in0=glo[:], scalar=float(n_nodes), in1=num[:, 1, :],
                                                    op0=ALU.is_lt, op1=ALU.mult))
                link(nc.vector.tensor_tensor(num[:, 0, :], num[:, 0, :], num[:, 1, :], ALU.max))
                link(nc.vector.tensor_reduce(num[:, 1, 0:1], num[:, 0, :], AX.X, ALU.max))
                link(nc.vector.tensor_tensor(worst[0:GQ, :], worst[0:GQ, :], num[:, 1, 0:1], ALU.max))
                dve.sem_inc(s_rng, 1)
                link(nc.vector.tensor_scalar(rng[:, 2:3], rng[:, 1:2], -1.0, BIG_T, ALU.mult, ALU.add))
                link(nc.vector.tensor_tensor(rng[:, 3:4], rng[:, 0:1], rng[:, 2:3], ALU.subtract))
                link(nc.vector.tensor_scalar(rng[:, 4:5], rng[:, 3:4], 0.0, float(C - 1), ALU.max, ALU.add))
                link(nc.vector.tensor_scalar(rngi[:, 0:1], rng[:, 4:5], float(-(-2 ** 14 // C)), None, ALU.mult))
                link(nc.vector.tensor_scalar(rngi[:, 1:2], rngi[:, 0:1], 14, None, ALU.arith_shift_right))
                link(nc.vector.tensor_copy(rng[:, 5:6], rngi[:, 1:2]))
                nc.vector.tensor_copy(nbc[:, 0, :], rng[:, 5:6].to_broadcast([NB, P]))
                nc.vector.tensor_copy(nbc[:, 1, :], rng[:, 2:3].to_broadcast([NB, P])).then_inc(s_rng, 1)
                dve.wait_ge(s_cum, 1)
                link(nc.vector.tensor_reduce(unit[0:1, 0:1], bank[2][0:1, 0:P], AX.X, ALU.max))
                link(nc.vector.tensor_scalar(fast[:], unit[0:1, 0:1], GT * P + 0.5, None, ALU.is_lt))
                link(nc.vector.tensor_copy(cum[:], bank[0][:, 0:NB + 1]))
                link(nc.vector.scalar_tensor_tensor(out=q[:], in0=cum[:, 0:NB], scalar=-float(C),
                                                    in1=bank[1][:, 0:NB], op0=ALU.mult, op1=ALU.add))
                link(nc.vector.tensor_tensor(dq[:, 1:NB], q[:, 1:NB], q[:, 0:NB - 1], ALU.subtract))
                link(nc.vector.tensor_scalar(dq[:, 1:NB], dq[:, 1:NB], 1024.0, None, ALU.add))
                link(nc.vector.tensor_scalar(v[:], sidx[:], float(C), q[:, 0:1], ALU.mult, ALU.add))
                for b in range(1, NB):
                    link(nc.vector.tensor_scalar(step[:], sidx[:], cum[:, b:b + 1], dq[:, b:b + 1], ALU.is_ge, ALU.mult))
                    link(nc.vector.tensor_tensor(v[:], v[:], step[:], ALU.add))
                link(nc.vector.tensor_scalar(step[:], sidx[:], cum[:, NB:NB + 1], None, ALU.is_lt))
                link(nc.vector.tensor_scalar(v[:], v[:], float(-(TA - C)), None, ALU.add))
                link(nc.vector.tensor_tensor(v[:], v[:], step[:], ALU.mult))
                link(nc.vector.tensor_scalar(vi[:], v[:], float(TA - C), None, ALU.add))
                dve.sem_inc(s_list, 1)
                link(nc.vector.tensor_scalar(turns_i[:, 0:1], cum[:, NB:NB + 1], float(U - 1), None, ALU.add))
                link(nc.vector.tensor_scalar(turns_i[:, 1:2], turns_i[:, 0:1], U.bit_length() - 1, None,
                                             ALU.arith_shift_right))
                link(nc.vector.tensor_scalar(turns[:], turns_i[0:1, 1:2], 1.0, None, ALU.max))
                dve.wait_ge(s_in, 16 * NIN)
                nc.vector.tensor_copy(dst[:], di[:]).then_inc(s_dve, 1)

            @block.tensor
            def _(pe):
                pe.wait_ge(s_rng, 2)
                pe.wait_ge(s_const, 3)
                nc.tensor.transpose(bank[2][0:1, 0:P], worst[:], ident[:])
                nc.tensor.matmul(bank[0][:, 0:NB + 1], nbc[:, 0, :], tri[:], start=True, stop=True)
                nc.tensor.matmul(bank[1][:, 0:NB], nbc[:, 1, :], ident[0:NB, 0:NB], start=True, stop=True).then_inc(s_cum, 1)

        def chunk_of(eng, at):
            both = eng.value_load(chunks[0:1, bass.ds(at, 1)], min_val=0, max_val=(NB - 1) * 1024 + TA - 1)
            return both >> 10, (both & 1023)


        def way(eng):
            return eng.value_load(fast[0:1, 0:1], min_val=0, max_val=1) > 0

        with ExitStack() as cc:
            def sm(name):
                return ctx.enter_context(nc.semaphore(f"count_{name}"))

            def ring(name, shape, dt=F32):
                return cc.enter_context(nc.sbuf_tensor(f"count_{name}", shape, dt))
            NV = 4
            PR = 2 * ES
            assert GP == 2 * ES and GP % NV == 0 and PC <= GP
            stage = ring("stage", [P, 2, NB, P], F16)
            gbase = ring("gbase", [P, NG])
            gend = ring("gend", [P, NG])
            keys = ring("keys", [P, HC], F16)
            low_keys = ring("low_keys", [P, P], F16)
            past = ring("past", [P, NV, GT])
            low = ring("low", [P, NV, GT])
            info = ring("info", [P, 2 * ES, GT, INFO])
            to = ring("to", [P, NV, GT, W])
            room = acc[:].bitcast(F16)
            cols = room[:, 0:NV * GT * HC].rearrange("p (v j n) -> p v j n", v=NV, j=GT)
            lows = room[:, NV * GT * HC:NV * GT * (HC + P)].rearrange("p (v j n) -> p v j n", v=NV, j=GT)
            eas = ring("eas", [P, 2 * ES, GT, EA1])
            keys_ready, past_ready, low_ready, first_ready, cols_ready, counted, taken, stored = (
                sm("keys_ready"), sm("past_ready"), sm("low_ready"), sm("first_ready"), sm("cols_ready"),
                sm("counted"), sm("taken"), sm("stored"))
            block = cc.enter_context(nc.Block())

            @block.sync
            def _(sp):
                with sp.If(way(sp)):
                    with sp.Fori(0, NPAN) as o:
                        for k in range(GP):
                            g = o * GP + k
                            if k % 2 == 0:
                                both = sp.value_load(groups[0:1, bass.ds(g, 1)], min_val=0, max_val=(EE - GT * P) * 512 + 511)
                                e = (both >> 9).with_bounds(min_val=0, max_val=EE - GT * P)
                                e_next = (e + (both & 511)).with_bounds(min_val=0, max_val=EE - GT * P)
                                sp.wait_ge(counted, g + 2)
                                sp.sem_inc(s_tick, 1)
                            at = bass.ds(e_next if k % 2 else e, GT * P)
                            sp.dma_start(info[:, k, :, :].rearrange("p j f -> p (j f)"),
                                         info_dram[at, :].rearrange("(p j) f -> p (j f)", j=GT)).then_inc(ea_got[k // 2], 16)
                            sp.dma_start(eas[:, k, :, :].rearrange("p j f -> p (j f)"),
                                         ea[at, :].rearrange("(p j) f -> p (j f)", j=GT)).then_inc(ea_got[k // 2], 16)
                with sp.Else():
                    sp.sem_inc(s_tick, 1)

            @block.gpsimd
            def _(pool):
                with pool.If(way(pool)):
                    nc.gpsimd.iota(gbase[:], [[W, NG]], channel_multiplier=0,
                                   allow_small_or_imprecise_dtypes=True).then_inc(keys_ready, 1)
                    nc.gpsimd.iota(gend[:], [[W, NG]], base=W, channel_multiplier=0,
                                   allow_small_or_imprecise_dtypes=True).then_inc(keys_ready, 1)
                    nc.gpsimd.iota(keys[:], [[1, HC]], channel_multiplier=0,
                                   allow_small_or_imprecise_dtypes=True).then_inc(keys_ready, 1)
                    nc.gpsimd.iota(low_keys[:], [[1, P]], channel_multiplier=0,
                                   allow_small_or_imprecise_dtypes=True).then_inc(keys_ready, 1)
                    pool.wait_ge(keys_ready, 4)
                    with pool.Fori(0, NPAN) as o:
                        for k in range(GP):
                            g = o * GP + k
                            v = k % NV
                            pool.wait_ge(ea_got[k // 2], 64 * (o + 1))
                            pool.wait_ge(counted, g + 1 - NV + PR)
                            nc.gpsimd.tensor_tensor(past[:, v, :], info[:, k, :, 2],
                                                    gend[:, bass.ds(g, 1)].to_broadcast([P, GT]), ALU.subtract
                                                    ).then_inc(past_ready, 1)
                            pool.wait_ge(past_ready, g * 2 + 1)
                            pool.sem_inc(s_tick, 1)
                            nc.gpsimd.tensor_scalar(past[:, v, :], past[:, v, :], 0.0, float(P), ALU.is_ge, ALU.mult
                                                    ).then_inc(past_ready, 1)
                            pool.wait_ge(past_ready, g * 2 + 2)
                            nc.gpsimd.tensor_tensor(low[:, v, :], past[:, v, :], info[:, k, :, 1], ALU.add
                                                    ).then_inc(low_ready, 1)
                            pool.wait_ge(low_ready, g + 1)
                            pool.sem_inc(s_tick, 1)
                            nc.gpsimd.tensor_scalar(lows[:, v, 0, :], low_keys[:], low[:, v, 0:1], None, ALU.is_equal
                                                    ).then_inc(first_ready, 1)
                with pool.Else():
                    pool.sem_inc(s_tick, 1)

            @block.vector
            def _(dve):
                with dve.If(way(dve)):
                    dve.wait_ge(keys_ready, 4)
                    with dve.Fori(0, NPAN) as o:
                        for k in range(GP):
                            g = o * GP + k
                            v = k % NV
                            slot = info[:, k, :, :]
                            dve.wait_ge(counted, g + 1 - NV + PR)
                            dve.wait_ge(ea_got[k // 2], 64 * (o + 1))
                            nc.vector.scalar_tensor_tensor(out=to[:, v, :, :],
                                                           in0=slot[:, :, 2:3].to_broadcast([P, GT, W]),
                                                           scalar=gbase[:, bass.ds(g, 1)],
                                                           in1=iota[:, 0:W].unsqueeze(1).to_broadcast([P, GT, W]),
                                                           op0=ALU.subtract, op1=ALU.is_equal)
                            for j in range(GT):
                                nc.vector.tensor_scalar(cols[:, v, j, :], keys[:], slot[:, j, 0:1], None, ALU.is_equal)
                            dve.wait_ge(low_ready, g + 1)
                            for j in range(1, GT):
                                oh = nc.vector.tensor_scalar(lows[:, v, j, :], low_keys[:], low[:, v, j:j + 1], None,
                                                             ALU.is_equal)
                            oh.then_inc(cols_ready, 1)
                with dve.Else():
                    dve.sem_inc(s_tick, 1)

            @block.tensor
            def _(pe):
                with pe.If(way(pe)):
                    pe.sem_inc(counted, PR)
                    pe.sem_inc(taken, 2)
                    with pe.Fori(0, NPAN) as o:
                        for k in range(GP):
                            g = o * GP + k
                            v = k % 2
                            pe.wait_ge(taken, g + 1)
                            pe.wait_ge(cols_ready, g + 1)
                            pe.wait_ge(first_ready, g + 1)
                            for j in range(GT):
                                for h, (c0, c1) in enumerate(((0, HA * W), (HA * W, HC))):
                                    nc.tensor.matmul(bank[2 * v + h][:, 0:c1 - c0], lows[:, k % NV, j, :], cols[:, k % NV, j, c0:c1],
                                                     start=(j == 0), stop=(j == GT - 1))
                            pe.wait_ge(ea_got[k // 2], 64 * (o + 1))
                            for j in range(GT):
                                mm = nc.tensor.matmul(bank[4 + v][0:EA1, 0:W], eas[:, k, j, :], to[:, k % NV, j, :],
                                                      start=(j == 0), stop=(j == GT - 1))
                            mm.then_inc(counted, 1)
                with pe.Else():
                    pe.sem_inc(s_tick, 1)

            @block.scalar
            def _(act):
                with act.If(way(act)):
                    act.sem_inc(stored, 16 * PC)

                    def store(o, c):
                        part = slice(c * PH, (c + 1) * PH)
                        act.dma_start(counts[bass.ds(o, 1), :, c * PH * P:(c + 1) * PH * P].rearrange("a l n -> l (a n)"),
                                      stage[:, bass.ds(o & 1, 1), part, :].rearrange("p a b w -> p (a b w)")
                                      ).then_inc(stored, 16)

                    def panel(o, before):
                        half = bass.ds(o & 1, 1)
                        for k in range(GP):
                            g = o * GP + k
                            v = k % 2
                            if k == 0 and before is not None:
                                act.wait_ge(stored, 16 * PC * o)
                                act.sem_inc(s_tick, 1)
                            act.wait_ge(counted, g + 1 + PR)
                            act.sem_inc(s_tick, 1)
                            nc.scalar.copy(stage[:, half, 0:HA, k * W:(k + 1) * W],
                                           bank[2 * v][:, 0:HA * W].rearrange("p (a b w) -> p a b w", a=1, w=W))
                            nc.scalar.copy(stage[:, half, HA:NB, k * W:(k + 1) * W],
                                           bank[2 * v + 1][:, 0:HC - HA * W].rearrange("p (a b w) -> p a b w", a=1, w=W))
                            nc.scalar.copy(eaT[:, bass.ds(g * W, W)], bank[4 + v][0:EA1, 0:W]).then_inc(taken, 1)
                            if before is not None and k < PC:
                                store(before, k)
                        act.wait_ge(taken, (o + 1) * GP + 2)
                        act.sem_inc(s_tick, 1)

                    panel(0, None)
                    with act.Fori(1, NPAN) as o:
                        panel(o, o - 1)
                    for c in range(PC):
                        store(NPAN - 1, c)
                    act.wait_ge(stored, 16 * PC * (NPAN + 1))
                with act.Else():
                    act.sem_inc(s_tick, 1)

        NQ = NPAN // QP + 1
        piece_got = [sem(f"piece_got{c}") for c in range(PC)]
        rows_in, scaled, hi_ready, lo_ready, peak_ready, peak_row, used, taken, cleared = (
            sem("rows_in"), sem("scaled"), sem("hi_ready"), sem("lo_ready"), sem("peak_ready"), sem("peak_row"),
            sem("piece_used"), sem("sums_taken"), sem("sums_cleared"))
        deg_ps, xd_ready, y_ps, y_ready, tr_ps, nodes_ready, y_done, lin = (
            sem("deg_in_psum"), sem("xd_ready"), sem("y_in_psum"), sem("y_ready"), sem("rows_in_psum"),
            sem("rows_ready"), sem("feat_updated"), sem("y_scaled"))
        res_got, x1_ready, x1T, x1T_ps, h_ps, h_ready, sq, hc, trc, last_stat, last_stored = (
            sem("resid_got"), sem("x1_ready"), sem("x1T_ready"), sem("x1T_in_psum"), sem("h_in_psum"), sem("h_ready"),
            sem("sqrt_ready"), sem("h_copied"), sem("rows_copied"), sem("stats_step"), sem("rows_stored"))
        largest = sb("largest", [P, NQ])
        for l in range(3):
            last = l == 2
            with ExitStack() as c1:
                def sm(name):
                    return ctx.enter_context(nc.semaphore(f"l{l}_{name}"))

                def ring(name, shape, dt=F32):
                    return c1.enter_context(nc.sbuf_tensor(f"l{l}_{name}", shape, dt))
                idx = ring("idx", [P, U, C], U32)
                hot_ready, mm_done, added = sm("onehot_ready"), sm("sum_ready"), sm("sum_added")
                piece = ring("piece", [P, PC, QP, PH * P], F16)
                room = piece[:].rearrange("p c s n -> p (c s n)").bitcast(F32)
                n_rows, n_hot, n_ea = U * C * D, 2 * C * P, U * C * EA1
                rows_l = room[:, 0:n_rows].rearrange("p (k f) -> p k f", f=D)
                onehot = room[:, n_rows:n_rows + n_hot].rearrange("p (v j n) -> p v j n", v=2, j=C)
                eas = room[:, n_rows + n_hot:n_rows + n_hot + n_ea].rearrange("p (u j f) -> p u j f", u=U, j=C)
                x_hi, x_lo = (c1.enter_context(nc.sbuf_tensor(f"l{l}_{k}", [P, NB, D], F16)) for k in ("x_hi", "x_lo"))
                xh, xl = (a[:].rearrange("p k f -> p (k f)") for a in (x_hi, x_lo))
                QC = QP * P
                sums = ring("sums", [P, 2, QC])
                xd, y = ring("xd", [P, QC]), ring("y", [P, QC])
                if last:
                    x1t = xd
                    resid, hrow = ring("resid", [P, QP, D]), ring("hrow", [P, QP, ROW])
                    stats, mv, rstd = ring("stats", [P, QP, 6]), ring("mv", [P, QP, 2]), ring("rstd", [P, QP])
                    adst_t, self_e = ring("adst_t", [P, QP]), ring("self_e", [P, QP])
                stat = last_stat
                NL = 3
                base_q = l * NQ
                slope = 0.01
                block = c1.enter_context(nc.Block())

                @block.gpsimd
                def _(pool):
                    with pool.If(way(pool)):
                        pool.sem_inc(s_tick, 1)
                    with pool.Else():
                        n = pool.value_load(turns[0:1, 0:1], min_val=1, max_val=P * NCC // U - 2)
                        with pool.Fori(0, n) as i:
                            for u in range(U):
                                pool.wait_ge(idx_ready[u], i + 1 + (n + 1) * l if l else i + 1)
                                pool.sem_inc(s_tick, 1)
                                for j in range(C):
                                    pool.indirect_dma_start(rows_l[:, u * C + j, :], None, table[l],
                                                            bass.IndirectOffsetOnAxis(ap=idx[:, u, j:j + 1], axis=0)
                                                            ).then_inc(row_got[u], 16)

                @block.scalar
                def _(act):
                    with act.If(way(act)):
                        if last:
                            act.sem_inc(last_stored, 32)
                            act.sem_inc(x1T, 1)
                        if l == 0:
                            act.sem_inc(nodes_ready, 1)
                        act.wait_ge(scaled, 4 * (l + 1))
                        for c in range(PC):
                            part = slice(c * PH * P, (c + 1) * PH * P)
                            nc.scalar.activation(xh[:, part], acc[:, part], ACT.Copy, scale=unit[:, 2:3]).then_inc(hi_ready, 1)

                        def rows_of(dram, q, n):
                            return dram.rearrange("(k p) f -> p k f", p=P)[:, bass.ds(q * QP, n), :]

                        def take(q, v, n):
                            w = n * P
                            at = bass.ds(q * QC, w)
                            act.wait_ge(used, (base_q + q + 2) * PC)
                            act.sem_inc(s_tick, 1)
                            nc.scalar.activation(sums[:, v, 0:w], bank[v][:, 0:w], ACT.Copy, scale=unit[:, 3:4]).then_inc(taken, 1)
                            if last:
                                act.wait_ge(last_stored, 32 * (q + 1))
                                act.sem_inc(s_tick, 1)
                                act.dma_start(resid[:, 0:n, :], rows_of(x, q, n)).then_inc(res_got, 16)
                            act.wait_ge(y_ps, base_q + q + 1)
                            act.sem_inc(s_tick, 1)
                            nc.scalar.copy(feat[:, at], bank[3][:, 0:w]).then_inc(lin, 1)
                            if not last:
                                act.wait_ge(tr_ps, base_q + q + 1)
                                act.sem_inc(s_tick, 1)
                                nc.scalar.copy(acc[:, at], bank[4][:, 0:w]).then_inc(nodes_ready, 1)
                                return
                            act.wait_ge(stat, NL * q + 3)
                            nc.scalar.activation(rstd[:, 0:n], mv[:, 0:n, 1], ACT.Sqrt, bias=eps[:, 0:1], scale=1.0).then_inc(sq, 1)
                            act.wait_ge(x1T_ps, q + 1)
                            nc.scalar.copy(x1t[:, 0:w], bank[5][:, 0:w]).then_inc(x1T, 1)
                            act.dma_start(rows_of(x1_dram, q, n), resid[:, 0:n, :]).then_inc(last_stored, 16)
                            act.wait_ge(h_ps, q + 1)
                            nc.scalar.copy(hrow[:, 0:n, 0:D], bank[6][:, 0:w].rearrange("p (k f) -> p k f", f=D)
                                           ).then_inc(h_ready, 1)
                            act.wait_ge(hc, 3 * q + 2)
                            act.sem_inc(s_tick, 1)
                            act.dma_start(rows_of(table_h, q, n), hrow[:, 0:n, :]).then_inc(last_stored, 16)

                        with act.Fori(0, (NQ - 1) // 2) as i:
                            take(i * 2, 0, QP)
                            take(i * 2 + 1, 1, QP)
                        take(NQ - 1, 0, 1)
                        if last:
                            act.wait_ge(last_stored, 32 * (NQ + 1))
                    with act.Else():
                        n = act.value_load(turns[0:1, 0:1], min_val=1, max_val=P * NCC // U - 2)

                        def fetch(i, u):
                            _, t = chunk_of(act, i * U + u)
                            t = t.with_bounds(min_val=0, max_val=TA - C)
                            nc.scalar.copy(idx[:, u, :], src[:, bass.ds(t, C)]).then_inc(idx_ready[u], 1)
                        for u in range(U):
                            fetch(0, u)
                        with act.Fori(1, n + 1) as i:
                            for u in range(U):
                                act.wait_ge(mm_done, i * U + u + 1)
                                act.sem_inc(s_tick, 1)
                                fetch(i, u)

                @block.sync
                def _(sp):
                    with sp.If(way(sp)):
                        if l == 0:
                            sp.dma_start(acc[:].rearrange("p (k f) -> p k f", f=D),
                                         x.rearrange("(k p) f -> p k f", p=P)).then_inc(rows_in, 16)

                        def read(q, n):
                            for c in range(PC):
                                sp.wait_ge(used, (l * NQ + q) * PC + c + 1)
                                sp.sem_inc(s_tick, 1)
                                sp.dma_start(piece[:, c, 0:n, :], counts.rearrange("s l n -> l s n")[
                                    :, bass.ds(q * QP, n), c * PH * P:(c + 1) * PH * P]).then_inc(piece_got[c], 16)

                        with sp.Fori(0, NQ - 1) as q:
                            read(q, QP)
                        read(NQ - 1, 1)
                    with sp.Else():
                        sp.sem_inc(s_tick, 1)
                        if l == 0:
                            n = sp.value_load(turns[0:1, 0:1], min_val=1, max_val=P * NCC // U - 2)
                            with sp.Fori(0, n) as i:
                                for u in range(U):
                                    _, t = chunk_of(sp, i * U + u)
                                    t = t.with_bounds(min_val=0, max_val=TA - C)
                                    sp.wait_ge(mm_done, i * U + u + 1)
                                    sp.sem_inc(s_tick, 1)
                                    sp.dma_start(eas[:, u, :, :], ea_tiles[:, bass.ds(t, C), :]).then_inc(ea_got[u], 16)

                @block.vector
                def _(dve):
                    with dve.If(way(dve)):
                        if l == 0:
                            dve.wait_ge(rows_in, 16)
                            nc.vector.tensor_reduce(unit[:, 0:1], acc[:], AX.X, ALU.max, apply_absolute_value=True
                                                    ).then_inc(peak_ready, 1)
                        else:
                            nc.vector.tensor_reduce(unit[:, 0:1], largest[:], AX.X, ALU.max).then_inc(peak_ready, 1)
                        dve.wait_ge(peak_row, 2 * l + 1)
                        nc.vector.tensor_reduce(unit[0:1, 1:2], bank[2][0:1, 0:P], AX.X, ALU.max).then_inc(peak_ready, 1)
                        dve.wait_ge(peak_row, 2 * l + 2)
                        nc.vector.tensor_scalar(unit[:, 0:1], bank[3][:, 0:1], 2.0 ** -100, None, ALU.max).then_inc(scaled, 1)
                        dve.wait_ge(scaled, 4 * l + 1)
                        bits = unit[:].bitcast(I32)
                        nc.vector.tensor_scalar(bits[:, 1:2], bits[:, 0:1], EXPONENT, None, ALU.bitwise_and).then_inc(scaled, 1)
                        dve.wait_ge(scaled, 4 * l + 2)
                        nc.vector.tensor_scalar(bits[:, 2:3], bits[:, 1:2], -1.0, float(267 << 23), ALU.mult, ALU.add).then_inc(scaled, 1)
                        nc.vector.tensor_scalar(bits[:, 3:4], bits[:, 1:2], float(13 << 23), None, ALU.subtract).then_inc(scaled, 1)
                        dve.wait_ge(scaled, 4 * l + 4)
                        for c in range(PC):
                            part = slice(c * PH * P, (c + 1) * PH * P)
                            dve.wait_ge(hi_ready, PC * l + c + 1)
                            nc.vector.scalar_tensor_tensor(out=xl[:, part], in0=acc[:, part], scalar=unit[:, 2:3],
                                                           in1=xh[:, part], op0=ALU.mult, op1=ALU.subtract).then_inc(lo_ready, 1)
                        if l == 0:
                            dve.sem_inc(xd_ready, 1)
                            dve.sem_inc(y_ready, 1)
                        if last:
                            dve.sem_inc(x1_ready, 1)
                            dve.sem_inc(h_ready, 1)
                            nc.vector.memset(hrow[:, :, D + 1:ROW], 0.0)

                        def node_steps(q, n):
                            w, at, blocks = n * P, bass.ds(q * QC, n * P), bass.ds(q * QP, n)
                            dve.wait_ge(deg_ps, base_q + q + 1)
                            nc.vector.tensor_tensor(xd[:, 0:w], feat[:, at], bank[2][:, 0:w], ALU.mult).then_inc(xd_ready, 1)
                            dve.wait_ge(lin, base_q + q + 1)
                            mx = nc.vector.scalar_tensor_tensor(out=y[:, 0:w], in0=bank[3][:, 0:w], scalar=slope,
                                                                in1=feat[:, at], op0=ALU.mult, op1=ALU.max)
                            if not last:
                                mx.then_inc(y_ready, 1)
                                dve.wait_ge(y_ready, base_q + q + 2)
                                dve.sem_inc(s_tick, 1)
                                nc.vector.tensor_copy(feat[:, at], y[:, 0:w])
                                nc.vector.tensor_reduce(largest[:, bass.ds(q, 1)], y[:, 0:w], AX.X, ALU.max,
                                                        apply_absolute_value=True)
                                return
                            mx.then_inc(y_done, 1)
                            dve.wait_ge(y_done, q + 1)
                            nc.vector.scalar_tensor_tensor(out=y[:, 0:w], in0=y[:, 0:w], scalar=slope, in1=y[:, 0:w],
                                                           op0=ALU.mult, op1=ALU.max).then_inc(y_ready, 1)
                            dve.wait_ge(tr_ps, base_q + q + 1)
                            dve.wait_ge(res_got, 16 * (q + 1))
                            nc.vector.tensor_tensor(resid[:, 0:n, :], resid[:, 0:n, :],
                                                    bank[4][:, 0:w].rearrange("p (k f) -> p k f", f=D), ALU.add
                                                    ).then_inc(nodes_ready, 1)
                            dve.wait_ge(nodes_ready, base_q + q + 2)
                            for k in range(n):
                                bn = nc.vector.bn_stats(out=stats[:, k, :], in_=resid[:, k, :])
                            bn.then_inc(stat, 1)
                            dve.wait_ge(stat, NL * q + 1)
                            dve.sem_inc(s_tick, 1)
                            for k in range(n):
                                bn = nc.vector.bn_aggr(out=mv[:, k, :], in_=stats[:, k, :])
                            bn.then_inc(stat, 2)
                            dve.wait_ge(sq, q + 1)
                            nc.vector.reciprocal(rstd[:, 0:n], rstd[:, 0:n]).then_inc(hc, 1)
                            dve.wait_ge(hc, 3 * q + 1)
                            for k in range(n):
                                nm = nc.vector.tensor_scalar(resid[:, k, :], resid[:, k, :], mv[:, k, 0:1],
                                                             rstd[:, k:k + 1], ALU.subtract, ALU.mult)
                            nm.then_inc(x1_ready, 1)
                            dve.wait_ge(h_ready, q + 2)
                            for k in range(n):
                                nc.vector.tensor_tensor_reduce(
                                    out=x1t[:, k * P:(k + 1) * P], in0=hrow[:, k, 0:D], in1=att_row[:, 0, :], scale=1.0, scalar=0.0,
                                    op0=ALU.mult, op1=ALU.add, accum_out=hrow[:, k, D:D + 1])
                                tt = nc.vector.tensor_tensor_reduce(
                                    out=y[:, k * P:(k + 1) * P], in0=hrow[:, k, 0:D], in1=att_row[:, 1, :], scale=1.0, scalar=0.0,
                                    op0=ALU.mult, op1=ALU.add, accum_out=adst_t[:, k:k + 1])
                            tt.then_inc(hc, 1)
                            dve.wait_ge(hc, 3 * q + 2)
                            dve.sem_inc(s_tick, 1)
                            nc.vector.tensor_copy(a_dst[:, blocks], adst_t[:, 0:n])
                            nc.vector.tensor_copy(a_src[:, blocks], hrow[:, 0:n, D])
                            nc.vector.tensor_copy(acc[:, at].rearrange("p (k f) -> p k f", f=D), hrow[:, 0:n, 0:D])
                            nc.vector.tensor_tensor(self_e[:, 0:n], adst_t[:, 0:n], hrow[:, 0:n, D], ALU.add).then_inc(hc, 1)
                            dve.wait_ge(hc, 3 * q + 3)
                            dve.sem_inc(s_tick, 1)
                            nc.vector.scalar_tensor_tensor(out=peak[:, blocks], in0=self_e[:, 0:n], scalar=0.2,
                                                           in1=self_e[:, 0:n], op0=ALU.mult, op1=ALU.max)

                        with dve.Fori(0, NQ - 1) as q:
                            node_steps(q, QP)
                        node_steps(NQ - 1, 1)
                        if last:
                            dve.sem_inc(s_dve, NT)
                    with dve.Else():
                        nc.vector.memset(acc[:], 0.0).then_inc(cleared, 1)
                        dve.wait_ge(cleared, l + 1)
                        n = dve.value_load(turns[0:1, 0:1], min_val=1, max_val=P * NCC // U - 2)
                        with dve.Fori(0, n) as i:
                            for u in range(U):
                                b, t = chunk_of(dve, i * U + u)
                                t = t.with_bounds(min_val=0, max_val=TA - C)
                                b = b.with_bounds(min_val=0, max_val=NB - 1)
                                dve.wait_ge(mm_done, i * U + u + U - 1)
                                nc.vector.scalar_tensor_tensor(
                                    out=onehot[:, u % 2, :, :],
                                    in0=dst[:, bass.ds(t, C)].unsqueeze(2).to_broadcast([P, C, P]),
                                    scalar=base[:, bass.ds(b, 1)],
                                    in1=iota[:].unsqueeze(1).to_broadcast([P, C, P]),
                                    op0=ALU.subtract, op1=ALU.is_equal).then_inc(hot_ready, 1)
                                dve.wait_ge(mm_done, i * U + u + U + 1)
                                dve.wait_ge(added, (i * U + u) + 1)
                                cols = acc[:, bass.ds(b * P, P)]
                                if l == 0:
                                    nc.vector.tensor_tensor(eaT[:, bass.ds(b * P, P)], eaT[:, bass.ds(b * P, P)],
                                                            bank[2 + u % 2][0:EA1, 0:P], ALU.add)
                                nc.vector.tensor_tensor(cols, cols, bank[u % 2][:, 0:P], ALU.add).then_inc(added, 1)

                @block.tensor
                def _(pe):
                    with pe.If(way(pe)):
                        if l == 0:
                            pe.sem_inc(used, PC)
                            pe.sem_inc(taken, 2)
                        pe.wait_ge(peak_ready, 2 * l + 1)
                        nc.tensor.transpose(bank[2][0:1, 0:P], unit[:, 0:1], ident[:]).then_inc(peak_row, 1)
                        pe.wait_ge(peak_ready, 2 * l + 2)
                        nc.tensor.matmul(bank[3][:, 0:1], ones[0:1, :], unit[0:1, 1:2], start=True, stop=True).then_inc(peak_row, 1)

                        def degrees(q, n):
                            pe.wait_ge(xd_ready, base_q + q + 1)
                            nc.tensor.matmul(bank[2][:, 0:n * P], sel[:], eaT[:, bass.ds(q * QC, n * P)],
                                             start=True, stop=True).then_inc(deg_ps, 1)

                        def linear(q, v, n):
                            w, at = n * P, bass.ds(q * QC, n * P)
                            pe.wait_ge(taken, base_q + q + 3)
                            pe.wait_ge(xd_ready, base_q + q + 2)
                            pe.wait_ge(y_ready, base_q + q + 1)
                            nc.tensor.matmul(bank[3][:, 0:w], w0[:, l, 0, :], sums[:, v, 0:w], start=True, stop=False)
                            nc.tensor.matmul(bank[3][:, 0:w], w0e[:, l, :], eaT[:, at], start=False, stop=False)
                            nc.tensor.matmul(bank[3][:, 0:w], w0[:, l, 1, :], xd[:, 0:w], start=False, stop=True).then_inc(y_ps, 1)

                        def turn_rows(q, n):
                            pe.wait_ge(y_ready, base_q + q + 2)
                            pe.wait_ge(nodes_ready, base_q + q + 1)
                            for k in range(n):
                                tr = nc.tensor.transpose(bank[4][:, k * P:(k + 1) * P], y[:, k * P:(k + 1) * P], ident[:])
                            tr.then_inc(tr_ps, 1)

                        def turn_x1(q, n):
                            pe.wait_ge(x1_ready, q + 2)
                            pe.wait_ge(x1T, q + 1)
                            for k in range(n):
                                tr = nc.tensor.transpose(bank[5][:, k * P:(k + 1) * P], resid[:, k, :], ident[:])
                            tr.then_inc(x1T_ps, 1)

                        def h_rows(q, n):
                            pe.wait_ge(x1T, q + 2)
                            pe.wait_ge(h_ready, q + 1)
                            for k in range(n):
                                mm = nc.tensor.matmul(bank[6][:, k * P:(k + 1) * P], x1t[:, k * P:(k + 1) * P], w1[:],
                                                      start=True, stop=True)
                            mm.then_inc(h_ps, 1)

                        def node_step(c, q, v, n):
                            if c == 0:
                                degrees(q, n)
                            elif c == 1:
                                linear(q, v, n)
                            elif c == 3:
                                turn_rows(q, n)
                            elif c == 5 and last:
                                turn_x1(q, n)
                            elif c == 6 and last:
                                h_rows(q, n)

                        def group(q, v, n, before):
                            pe.wait_ge(taken, base_q + q + 1)
                            for c in range(PC):
                                pe.wait_ge(lo_ready, PC * l + c + 1)
                                pe.wait_ge(piece_got[c], 16 * (base_q + q + 1))
                                for h in range(PH):
                                    blk_h = c * PH + h
                                    moving = piece[:, c, 0:n, h * P:(h + 1) * P]
                                    nc.tensor.matmul(bank[v][:, 0:n * P], x_hi[:, blk_h, :], moving,
                                                     start=(blk_h == 0), stop=False)
                                    mm = nc.tensor.matmul(bank[v][:, 0:n * P], x_lo[:, blk_h, :], moving,
                                                          start=False, stop=(blk_h == NB - 1))
                                mm.then_inc(used, 1)
                                if before is not None:
                                    node_step(c, *before)

                        group(0, 0, QP, None)
                        with pe.Fori(0, (NQ - 3) // 2) as i:
                            group(i * 2 + 1, 1, QP, (i * 2, 0, QP))
                            group(i * 2 + 2, 0, QP, (i * 2 + 1, 1, QP))
                        group(NQ - 2, 1, QP, (NQ - 3, 0, QP))
                        group(NQ - 1, 0, 1, (NQ - 2, 1, QP))
                        for c in range(PC):
                            node_step(c, NQ - 1, 0, 1)
                    with pe.Else():
                        n = pe.value_load(turns[0:1, 0:1], min_val=1, max_val=P * NCC // U - 2)
                        pe.sem_inc(mm_done, U)
                        pe.sem_inc(added, 1)
                        with pe.Fori(0, n) as i:
                            for u in range(U):
                                pe.wait_ge(hot_ready, i * U + u + 1)
                                if l == 0:
                                    pe.wait_ge(ea_got[u], 16 * (i + 1))
                                    for j in range(C):
                                        nc.tensor.matmul(bank[2 + u % 2][0:EA1, 0:P], eas[:, u, j, :], onehot[:, u % 2, j, :],
                                                         start=(j == 0), stop=(j == C - 1))
                                pe.wait_ge(row_got[u], (i + 1 + n * l) * G16 if l else (i + 1) * G16)
                                for j in range(C):
                                    mm = nc.tensor.matmul(bank[u % 2][:, 0:P], rows_l[:, u * C + j, :],
                                                          onehot[:, u % 2, j, :], start=(j == 0), stop=(j == C - 1))
                                mm.then_inc(mm_done, 1)

            with ExitStack() as c2:
                def sm(name):
                    return ctx.enter_context(nc.semaphore(f"n{l}_{name}"))

                def tile(name, shape, dt=F32):
                    return c2.enter_context(nc.sbuf_tensor(f"n{l}_{name}", shape, dt))
                xd = tile("xd", [P, SB * P])
                y = tile("y", [P, SB * P])
                nodes = tile("nodes", [P, SB, D])
                resid = tile("resid", [P, SB, D])
                hrow = tile("hrow", [P, SB, ROW])
                stats = tile("stats", [P, SB, 6])
                mv = tile("mv", [P, SB, 2])
                rstd = tile("rstd", [P, SB])
                adst_t = tile("adst_t", [P, SB])
                self_e = tile("self_e", [P, SB])
                junk = tile("junk", [P, 2 * SB, D])
                SK = 32 if last else 16
                stored, stat = (last_stored, last_stat) if last else (sm("rows_stored"), sm("stats_step"))
                block = c2.enter_context(nc.Block())
                tb = [(bank[4 + k // 4], (k % 4) * P) for k in range(SB)]
                tc_ = [(bank[6 + k // 4], (k % 4) * P) for k in range(SB)]
                slope = 0.01

                @block.tensor
                def _(pe):
                    with pe.If(way(pe)):
                        pe.sem_inc(s_tick, 1)
                    with pe.Else():
                        with pe.Fori(0, NT) as i:
                            for g in range(2):
                                cols = eaT[:, bass.ds(i * (SB * P) + g * HB, HB)]
                                if g == 0:
                                    pe.wait_ge(xd_ready, 2 * (i + l * NT) + 1)
                                mm = nc.tensor.matmul(bank[g][:, 0:HB], sel[:], cols, start=True, stop=True)
                            mm.then_inc(deg_ps, 1)
                            for g in range(2):
                                at = bass.ds(i * (SB * P) + g * HB, HB)
                                if g == 0:
                                    pe.wait_ge(y_ready, (i + l * NT) + 1)
                                nc.tensor.matmul(bank[2 + g][:, 0:HB], w0[:, l, 0, :], acc[:, at], start=True, stop=False)
                                nc.tensor.matmul(bank[2 + g][:, 0:HB], w0e[:, l, :], eaT[:, at], start=False, stop=False)
                                if g == 0:
                                    pe.wait_ge(xd_ready, 2 * (i + l * NT) + 2 + 1)
                                mm = nc.tensor.matmul(bank[2 + g][:, 0:HB], w0[:, l, 1, :], xd[:, g * HB:(g + 1) * HB],
                                                      start=False, stop=True)
                            mm.then_inc(y_ps, 1)
                            pe.wait_ge(y_ready, (i + l * NT) + 2)
                            pe.wait_ge(nodes_ready, (i + l * NT) + 1)
                            for k in range(SB):
                                bk, o = tb[k]
                                tr = nc.tensor.transpose(bk[:, o:o + P], y[:, k * P:(k + 1) * P], ident[:])
                            tr.then_inc(tr_ps, 1)
                            if last:
                                pe.wait_ge(x1_ready, i + 1)
                                pe.wait_ge(x1T, i + 1)
                                for k in range(SB):
                                    bk, o = tc_[k]
                                    tr = nc.tensor.transpose(bk[:, o:o + P], nodes[:, k, :], ident[:])
                                tr.then_inc(x1T_ps, 1)
                                pe.wait_ge(x1T, i + 2)
                                for k in range(SB):
                                    bk, o = tb[k]
                                    mm = nc.tensor.matmul(bk[:, o:o + P], y[:, k * P:(k + 1) * P], w1[:], start=True, stop=True)
                                mm.then_inc(h_ps, 1)

                @block.vector
                def _(dve):
                    with dve.If(way(dve)):
                        dve.sem_inc(s_tick, 1)
                    with dve.Else():
                        nc.vector.memset(hrow[:, :, D + 1:ROW], 0.0)
                        if l == 0:
                            dve.sem_inc(xd_ready, 1)
                        if l == 0:
                            dve.sem_inc(y_ready, 1)
                        with dve.Fori(0, NT) as i:
                            for g in range(2):
                                at = bass.ds(i * (SB * P) + g * HB, HB)
                                if g == 0:
                                    dve.wait_ge(deg_ps, (i + l * NT) + 1)
                                    dve.wait_ge(y_done, (i + l * NT) + 1)
                                nc.vector.tensor_tensor(xd[:, g * HB:(g + 1) * HB], feat[:, at], bank[g][:, 0:HB],
                                                        ALU.mult).then_inc(xd_ready, 1)
                            dve.wait_ge(lin, (i + l * NT) + 1)
                            for g in range(2):
                                mx = nc.vector.scalar_tensor_tensor(
                                    out=y[:, g * HB:(g + 1) * HB], in0=bank[2 + g][:, 0:HB], scalar=slope,
                                    in1=feat[:, bass.ds(i * (SB * P) + g * HB, HB)], op0=ALU.mult, op1=ALU.max)
                                mx.then_inc(stat, 1)
                            if last:
                                dve.wait_ge(stat, 5 * i + 2)
                                mx = nc.vector.scalar_tensor_tensor(out=y[:], in0=y[:], scalar=slope, in1=y[:],
                                                                    op0=ALU.mult, op1=ALU.max)
                                mx.then_inc(y_ready, 1)
                            else:
                                dve.wait_ge(stat, 2 * i + 2)
                                dve.sem_inc(s_tick, 1)
                                nc.vector.tensor_copy(feat[:, bass.ds(i * (SB * P), SB * P)], y[:]).then_inc(y_ready, 1)
                            if last:
                                dve.wait_ge(trc, i + 1)
                                dve.wait_ge(res_got, 16 * (i + 1))
                                nc.vector.tensor_tensor(resid[:], resid[:], nodes[:], ALU.add).then_inc(stat, 1)
                                dve.wait_ge(stat, 5 * i + 3)
                                for k in range(SB):
                                    bn = nc.vector.bn_stats(out=stats[:, k, :], in_=resid[:, k, :])
                                bn.then_inc(stat, 1)
                                dve.wait_ge(stat, 5 * i + 4)
                                dve.sem_inc(s_tick, 1)
                                for k in range(SB):
                                    bn = nc.vector.bn_aggr(out=mv[:, k, :], in_=stats[:, k, :])
                                bn.then_inc(stat, 1)
                                dve.wait_ge(sq, i + 1)
                                nc.vector.reciprocal(rstd[:], rstd[:]).then_inc(hc, 1)
                                dve.wait_ge(hc, 3 * i + 1)
                                for k in range(SB):
                                    nm = nc.vector.tensor_scalar(nodes[:, k, :], resid[:, k, :], mv[:, k, 0:1],
                                                                 rstd[:, k:k + 1], ALU.subtract, ALU.mult)
                                nm.then_inc(x1_ready, 1)
                                dve.wait_ge(h_ready, i + 1)
                                for k in range(SB):
                                    nc.vector.tensor_tensor_reduce(
                                        out=junk[:, k, :], in0=hrow[:, k, 0:D], in1=att_row[:, 0, :], scale=1.0, scalar=0.0,
                                        op0=ALU.mult, op1=ALU.add, accum_out=hrow[:, k, D:D + 1])
                                    tt = nc.vector.tensor_tensor_reduce(
                                        out=junk[:, SB + k, :], in0=hrow[:, k, 0:D], in1=att_row[:, 1, :], scale=1.0, scalar=0.0,
                                        op0=ALU.mult, op1=ALU.add, accum_out=adst_t[:, k:k + 1])
                                tt.then_inc(hc, 1)
                                dve.wait_ge(hc, 3 * i + 2)
                                dve.sem_inc(s_tick, 1)
                                nc.vector.tensor_copy(a_dst[:, bass.ds(i * SB, SB)], adst_t[:])
                                nc.vector.tensor_copy(a_src[:, bass.ds(i * SB, SB)], hrow[:, :, D])
                                nc.vector.tensor_copy(acc[:, bass.ds(i * (SB * P), SB * P)].rearrange("p (k f) -> p k f", f=D),
                                                      hrow[:, :, 0:D])
                                nc.vector.tensor_tensor(self_e[:], adst_t[:], hrow[:, :, D], ALU.add).then_inc(hc, 1)
                                dve.wait_ge(hc, 3 * i + 3)
                                dve.sem_inc(s_tick, 1)
                                nc.vector.scalar_tensor_tensor(out=peak[:, bass.ds(i * SB, SB)], in0=self_e[:], scalar=0.2,
                                                               in1=self_e[:], op0=ALU.mult, op1=ALU.max).then_inc(s_dve, 1)

                @block.scalar
                def _(act):
                    with act.If(way(act)):
                        act.sem_inc(s_tick, 1)
                    with act.Else():
                        if l == 0:
                            act.sem_inc(y_done, 1)
                        if l == 0:
                            act.sem_inc(nodes_ready, 1)
                        if last:
                            act.sem_inc(x1T, 1)
                        with act.Fori(0, NT) as i:
                            act.wait_ge(y_ps, (i + l * NT) + 1)
                            act.sem_inc(s_tick, 1)
                            for g in range(2):
                                cp = nc.scalar.copy(feat[:, bass.ds(i * (SB * P) + g * HB, HB)], bank[2 + g][:, 0:HB])
                            cp.then_inc(lin, 1)
                            act.wait_ge(tr_ps, (i + l * NT) + 1)
                            act.wait_ge(stored, SK * (i + 1))
                            act.sem_inc(s_tick, 1)
                            nc.scalar.copy(nodes[:, 0:4, :], bank[4][:, 0:512].rearrange("p (k f) -> p k f", f=D))
                            cp = nc.scalar.copy(nodes[:, 4:SB, :], bank[5][:, 0:3 * P].rearrange("p (k f) -> p k f", f=D))
                            if not last:
                                cp.then_inc(nodes_ready, 1)
                                act.sem_inc(y_done, 1)
                            else:
                                cp.then_inc(trc, 1)
                                act.wait_ge(stat, 5 * i + 5)
                                nc.scalar.activation(rstd[:], mv[:, :, 1], ACT.Sqrt, bias=eps[:, 0:1], scale=1.0).then_inc(sq, 1)
                                act.wait_ge(x1T_ps, i + 1)
                                act.sem_inc(s_tick, 1)
                                nc.scalar.copy(y[:, 0:512], bank[6][:, 0:512])
                                nc.scalar.copy(y[:, 512:SB * P], bank[7][:, 0:3 * P]).then_inc(x1T, 1)
                                act.wait_ge(h_ps, i + 1)
                                act.sem_inc(s_tick, 1)
                                nc.scalar.copy(hrow[:, 0:4, 0:D], bank[4][:, 0:512].rearrange("p (k f) -> p k f", f=D))
                                cp = nc.scalar.copy(hrow[:, 4:SB, 0:D], bank[5][:, 0:3 * P].rearrange("p (k f) -> p k f", f=D))
                                cp.then_inc(h_ready, 1)
                                act.wait_ge(h_ready, i + 1)
                                act.sem_inc(nodes_ready, 1)
                                act.sem_inc(y_done, 1)

                @block.sync
                def _(sp):
                    with sp.If(way(sp)):
                        sp.sem_inc(s_tick, 1)
                    with sp.Else():
                        sp.sem_inc(stored, SK)
                        with sp.Fori(0, NT) as i:
                            turn = bass.ds(i * SB, SB)
                            if not last:
                                sp.wait_ge(nodes_ready, (i + l * NT) + 2)
                                sp.sem_inc(s_tick, 1)
                                sp.dma_start(table[l + 1].rearrange("(k p) f -> p k f", p=P)[:, turn, :],
                                             nodes[:]).then_inc(stored, 16)
                            else:
                                sp.dma_start(resid[:], x.rearrange("(k p) f -> p k f", p=P)[:, turn, :]).then_inc(res_got, 16)
                                sp.wait_ge(x1_ready, i + 1)
                                sp.sem_inc(s_tick, 1)
                                sp.dma_start(x1_dram.rearrange("(k p) f -> p k f", p=P)[:, turn, :],
                                             nodes[:]).then_inc(stored, 16)
                                sp.wait_ge(hc, 3 * i + 2)
                                sp.sem_inc(s_tick, 1)
                                sp.dma_start(table_h.rearrange("(k p) f -> p k f", p=P)[:, turn, :],
                                             hrow[:]).then_inc(stored, 16)
                        sp.wait_ge(stored, SK * (NT + 1))

        with ExitStack() as c3:
            def sm(name):
                return ctx.enter_context(nc.semaphore(f"top_{name}"))
            neg_src = c3.enter_context(nc.sbuf_tensor("neg_src0", [P, NB], F32))
            line = c3.enter_context(nc.sbuf_tensor("top_line", [3, 1], F32))
            diag = c3.enter_context(nc.sbuf_tensor("top_diag", [3, 3], F32))
            spread = c3.enter_context(nc.sbuf_tensor("spread", [1, 2], F32))
            step, turned = sm("vector_step"), sm("tensor_step")
            block = c3.enter_context(nc.Block())

            @block.tensor
            def _(pe):
                pe.wait_ge(step, 4)
                nc.tensor.transpose(bank[0][0:3, 0:P], tops[:], ident[:]).then_inc(turned, 1)
                pe.wait_ge(step, 6)
                nc.tensor.matmul(bank[1][:, 0:3], ones[:], diag[:], start=True, stop=True).then_inc(turned, 1)

            @block.vector
            def _(dve):
                n = 0

                def link(ins):
                    nonlocal n
                    n += 1
                    ins.then_inc(step, 1)
                    dve.wait_ge(step, n)
                link(nc.vector.tensor_scalar(neg_src[:], a_src[:], -1.0, None, ALU.mult))
                link(nc.vector.tensor_reduce(tops[:, 0:1], a_src[:], AX.X, ALU.max))
                link(nc.vector.tensor_reduce(tops[:, 1:2], neg_src[:], AX.X, ALU.max))
                link(nc.vector.tensor_reduce(tops[:, 2:3], acc[:], AX.X, ALU.max, apply_absolute_value=True))
                dve.wait_ge(turned, 1)
                link(nc.vector.tensor_reduce(line[:], bank[0][0:3, 0:P], AX.X, ALU.max))
                link(nc.vector.tensor_scalar(diag[:], ident[0:3, 0:3], line[:, 0:1], None, ALU.mult))
                dve.wait_ge(turned, 2)
                link(nc.vector.tensor_copy(tops[:], bank[1][:, 0:3]))
                link(nc.vector.tensor_tensor(spread[:, 0:1], tops[0:1, 0:1], tops[0:1, 1:2], ALU.add))
                link(nc.vector.tensor_scalar(spread[:, 1:2], spread[:, 0:1], SPREAD, None, ALU.is_le))
                link(nc.vector.tensor_tensor(short[:], spread[:, 1:2], fast[:], ALU.mult))

        out_got, out_link, out_sqrt, out_rows, out_stored = (
            sem("x1_got"), sem("out_link"), sem("out_sqrt"), sem("out_rows"), sem("out_stored"))

        def short_way(eng):
            return eng.value_load(short[0:1, 0:1], min_val=0, max_val=1) > 0

        with ExitStack() as c3:
            def sm(name):
                return ctx.enter_context(nc.semaphore(f"att_{name}"))

            def ring(name, shape, dt=F32):
                return c3.enter_context(nc.sbuf_tensor(f"att_{name}", shape, dt))
            NS = 4
            UNITS = ((0, 4), (4, 3))
            NU = len(UNITS)
            MB = UNITS[0][1]
            HE = D + 1
            n_piece, n_mask, n_tmp = NS * QP * PH * P, 2 * 2 * QP * MB * P, 2 * PH * D
            assert (n_piece + n_mask) // 2 + n_tmp <= P * NCC
            room16 = shared[:].bitcast(F16)
            piece = room16[:, 0:n_piece].rearrange("p (c s n) -> p c s n", c=NS, s=QP)
            masks = room16[:, n_piece:n_piece + n_mask].rearrange("p (v k s b n) -> p v k s b n", v=2, k=2, s=QP, b=MB)
            tmp = shared[:, (n_piece + n_mask) // 2:(n_piece + n_mask) // 2 + n_tmp].rearrange("p (v b f) -> p v b f", v=2, b=PH)
            wh = ring("wh", [P, NB, 2, 2, HE], F16)
            ev = ring("ev", [P, QP, 2, 2, HE])
            fin = ring("fin", [P, QP, HE])
            line = ring("line", [NB, P])
            neg_src = ring("neg_src", [P, NB])
            q_top = ring("q_top", [P, NB])
            m_top = ring("m_top", [P, NB])
            z = ring("z", [P, 3, NB])
            f = ring("f", [P, 3, NB])
            e = ring("e", [P, 2, NB])
            es = ring("es", [P, 2, NB])
            ew = ring("ew", [P, 2, NB])
            neg_top = ring("neg_top", [P, 2])
            back = ring("back", [P, 1])
            resid = ring("resid", [P, QP, D])
            den = ring("den", [P, QP])
            stats, mv, rstd = ring("stats", [P, QP, 6]), ring("mv", [P, QP, 2]), ring("rstd", [P, QP])
            SB2 = 2
            sign = ring("sign", [P, QP, SB2, P], F16)
            steps = ring("steps", [P, 2, QP, SB2, P], F16)
            KP = 5
            row = feat
            step, e_ready, f_ready, turned, line_ready, neg_ready, line_out, row_in, hw_ready, high_ready, low_ready, col_ready = (
                sm("vector_step"), sm("e_ready"), sm("f_ready"), sm("a_dst_in_psum"), sm("line_ready"), sm("negated"), sm("line_stored"),
                sm("row_in"), sm("weighted"), sm("high_ready"), sm("low_ready"), sm("columns_ready"))
            pos_ready, rest_ready, mask_used, sums_done, banks_read, halves, pool_link, rows_done, den_ready, sum_ready, sign_ready, step_ready = (
                sm("mask_ready"), sm("rest_ready"), sm("masks_used"), sm("sums_ready"),
                sm("banks_read"), sm("halves_added"), sm("pool_link"), sm("rows_done"), sm("den_ready"),
                sm("sum_ready"), sm("sign_ready"), sm("step_ready"))
            got = [sm(f"piece_got{c}") for c in range(NS)]
            line_dram = nc.dram_tensor("a_dst_line", [NB, P], F32).ap()
            block = c3.enter_context(nc.Block())
            SLOT_USES = [sum(1 for c in range(PC) if c % NS == k) for k in range(NS)]

            def before(c):
                return c - NS if c >= NS else max(k for k in range(PC) if k % NS == c) - PC

            def arrivals(q, c):
                return 16 * (q * SLOT_USES[c % NS] + c // NS + 1)

            @block.sync
            def _(sp):
                with sp.If(short_way(sp)):
                    sp.wait_ge(line_ready, 1)
                    sp.dma_start(line_dram, line[:]).then_inc(line_out, 16)
                    sp.wait_ge(line_out, 16)
                    sp.dma_start(row[:], line_dram.rearrange("(a b) p -> a (b p)", a=1).partition_broadcast(P)).then_inc(row_in, 16)

                    def read(q, n):
                        for c in range(PC):
                            sp.wait_ge(rest_ready, (q * PC + before(c) + 1 + PC) * NU)
                            sp.sem_inc(s_tick, 1)
                            sp.dma_start(piece[:, c % NS, 0:n, :], counts.rearrange("s l n -> l s n")[
                                :, bass.ds(q * QP, n), c * PH * P:(c + 1) * PH * P]).then_inc(got[c % NS], 16)

                    with sp.Fori(0, NQ - 1) as q:
                        read(q, QP)
                    read(NQ - 1, 1)
                with sp.Else():
                    sp.sem_inc(s_tick, 1)

            @block.vector
            def _(dve):
                with dve.If(short_way(dve)):
                    n_link = 0

                    def link(ins):
                        nonlocal n_link
                        n_link += 1
                        ins.then_inc(step, 1)
                        dve.wait_ge(step, n_link)
                    dve.sem_inc(rest_ready, PC * NU)
                    dve.sem_inc(rows_done, 1)
                    link(nc.vector.tensor_scalar(unit[:, 0:1], tops[:, 2:3], 2.0 ** -100, None, ALU.max))
                    bits = unit[:].bitcast(I32)
                    link(nc.vector.tensor_scalar(bits[:, 1:2], bits[:, 0:1], EXPONENT, None, ALU.bitwise_and))
                    link(nc.vector.tensor_scalar(bits[:, 2:3], bits[:, 1:2], -1.0, float(267 << 23), ALU.mult, ALU.add))
                    link(nc.vector.tensor_scalar(bits[:, 3:4], bits[:, 1:2], float(13 << 23), None, ALU.subtract))
                    link(nc.vector.tensor_scalar(back[:], unit[:, 2:3], 2.0 ** -14, None, ALU.mult))
                    nc.vector.tensor_scalar(neg_top[:, 0:1], tops[:, 0:1], -1.0, None, ALU.mult)
                    nc.vector.tensor_scalar(neg_top[:, 1:2], tops[:, 0:1], -0.2, None, ALU.mult).then_inc(neg_ready, 1)
                    nc.vector.tensor_scalar(neg_src[:], a_src[:], -1.0, None, ALU.mult)
                    link(nc.vector.tensor_scalar(q_top[:], a_dst[:], tops[:, 0:1], None, ALU.add))
                    link(nc.vector.scalar_tensor_tensor(out=m_top[:], in0=q_top[:], scalar=0.2, in1=q_top[:],
                                                        op0=ALU.mult, op1=ALU.max))
                    nc.vector.tensor_tensor(z[:, 0, :], q_top[:], m_top[:], ALU.subtract)
                    nc.vector.tensor_tensor(z[:, 2, :], peak[:], m_top[:], ALU.subtract)
                    link(nc.vector.scalar_tensor_tensor(out=z[:, 1, :], in0=q_top[:], scalar=0.2, in1=m_top[:],
                                                        op0=ALU.mult, op1=ALU.subtract))
                    dve.wait_ge(e_ready, 1)
                    nc.vector.tensor_scalar(ew[:], e[:], 2.0 ** 14, None, ALU.mult)
                    link(nc.vector.tensor_scalar(es[:], e[:], unit[:, 2:3], None, ALU.mult))
                    link(nc.vector.tensor_copy(wh[:, :, :, 0, D].rearrange("p b k -> p k b"), ew[:]))
                    nc.vector.tensor_tensor(wh[:, :, :, 1, D].rearrange("p b k -> p k b"), ew[:],
                                            wh[:, :, :, 0, D].rearrange("p b k -> p k b"), ALU.subtract).then_inc(col_ready, 1)
                    for c in range(PC):
                        blocks = slice(c * PH, (c + 1) * PH)
                        h = acc[:, c * PH * P:(c + 1) * PH * P].rearrange("p (b f) -> p b f", f=D)
                        for k in range(2):
                            if c > 0:
                                dve.wait_ge(low_ready, 2 * c + k - 1)
                            nc.vector.tensor_tensor(tmp[:, k, :, :], h, es[:, k, blocks].unsqueeze(2).to_broadcast([P, PH, D]),
                                                    ALU.mult).then_inc(hw_ready, 1)
                    dve.wait_ge(f_ready, 1)
                    link(nc.vector.tensor_scalar(f[:, 0:2, :], f[:, 0:2, :], unit[:, 3:4], None, ALU.mult))
                    dve.wait_ge(row_in, 16)

                    def group(q, n, ending):
                        at = bass.ds(q * (QP * P), n * P)
                        for c in range(PC):
                            dve.wait_ge(got[c % NS], arrivals(q, c))
                            for k, (h0, hn) in enumerate(UNITS):
                                s = (q * PC + c) * NU + k
                                v = (c * NU + k) % 2
                                dve.wait_ge(mask_used, s + 1)
                                own = hn if c == 0 else hn - SB2
                                for h in range(own):
                                    b = c * PH + h0 + h
                                    mk = nc.vector.scalar_tensor_tensor(
                                        out=masks[:, v, 0, 0:n, h, :], in0=row[:, at].rearrange("p (s n) -> p s n", n=P),
                                        scalar=neg_src[:, b:b + 1],
                                        in1=piece[:, c % NS, 0:n, (h0 + h) * P:(h0 + h + 1) * P],
                                        op0=ALU.is_gt, op1=ALU.mult)
                                if own < hn:
                                    dve.wait_ge(step_ready, (q * (PC - 1) + c - 1) * NU + k + 2)
                                    mk = nc.vector.tensor_tensor(
                                        masks[:, v, 0, 0:n, own:hn, :].rearrange("p s b n -> p s (b n)"),
                                        piece[:, c % NS, 0:n, (h0 + own) * P:(h0 + hn) * P],
                                        steps[:, v, 0:n, :, :].rearrange("p s b n -> p s (b n)"), ALU.mult)
                                mk.then_inc(pos_ready, 1)
                                dve.wait_ge(pos_ready, s + 1)
                                nc.vector.tensor_tensor(
                                    masks[:, v, 1, 0:n, 0:hn, :].rearrange("p s b n -> p s (b n)"),
                                    piece[:, c % NS, 0:n, h0 * P:(h0 + hn) * P],
                                    masks[:, v, 0, 0:n, 0:hn, :].rearrange("p s b n -> p s (b n)"),
                                    ALU.subtract).then_inc(rest_ready, 1)
                            if ending is not None:
                                finish(c, *ending)

                    def finish(c, q, n):
                        if c == 2:
                            dve.wait_ge(halves, q + 2)
                            nc.vector.reciprocal(den[:, 0:n], den[:, 0:n]).then_inc(den_ready, 1)
                        elif c == 4:
                            dve.wait_ge(sum_ready, q + 1)
                            for d in range(n):
                                bn = nc.vector.bn_stats(out=stats[:, d, :], in_=fin[:, d, 0:D])
                            bn.then_inc(out_link, 1)
                            dve.wait_ge(out_link, 3 * q + 1)
                            dve.sem_inc(s_tick, 1)
                            for d in range(n):
                                bn = nc.vector.bn_aggr(out=mv[:, d, :], in_=stats[:, d, :])
                            bn.then_inc(out_link, 1)
                        elif c == 5:
                            dve.wait_ge(out_sqrt, q + 1)
                            nc.vector.reciprocal(rstd[:, 0:n], rstd[:, 0:n]).then_inc(out_link, 1)
                            dve.wait_ge(out_link, 3 * q + 3)
                            for d in range(n):
                                nm = nc.vector.tensor_scalar(resid[:, d, :], fin[:, d, 0:D], mv[:, d, 0:1],
                                                             rstd[:, d:d + 1], ALU.subtract, ALU.mult)
                            nm.then_inc(rows_done, 1)

                    group(0, QP, None)
                    with dve.Fori(1, NQ - 1) as q:
                        group(q, QP, (q - 1, QP))
                    group(NQ - 1, 1, (NQ - 2, QP))
                    for c in range(PC):
                        finish(c, NQ - 1, 1)
                with dve.Else():
                    dve.sem_inc(s_tick, 1)

            @block.gpsimd
            def _(pool):
                with pool.If(short_way(pool)):
                    pool.sem_inc(halves, 1)
                    for c in range(PC):
                        for k in range(2):
                            pool.wait_ge(high_ready, 2 * c + k + 1)
                            nc.gpsimd.tensor_tensor(wh[:, c * PH:(c + 1) * PH, k, 1, 0:D], tmp[:, k, :, :],
                                                    wh[:, c * PH:(c + 1) * PH, k, 0, 0:D], ALU.subtract).then_inc(low_ready, 1)

                    def finish(q, n):
                        add_up(q, n)
                        pool.wait_ge(den_ready, q + 1)
                        nc.gpsimd.tensor_tensor(fin[:, 0:n, 0:D], fin[:, 0:n, 0:D],
                                                den[:, 0:n].unsqueeze(2).to_broadcast([P, n, D]), ALU.mult
                                                ).then_inc(pool_link, 1)
                        pool.wait_ge(pool_link, KP * q + KP)
                        nc.gpsimd.tensor_tensor(fin[:, 0:n, 0:D], fin[:, 0:n, 0:D], resid[:, 0:n, :], ALU.add
                                                ).then_inc(sum_ready, 1)

                    def add_up(q, n):
                        cols, blocks = acc[:, bass.ds(q * (QP * P), n * P)], bass.ds(q * QP, n)
                        pool.wait_ge(banks_read, q * (2 * QP) + 2 * n + 2 * QP)
                        nc.gpsimd.tensor_tensor(ev[:, 0:n, 0, :, :], ev[:, 0:n, 0, :, :], ev[:, 0:n, 1, :, :], ALU.add
                                                ).then_inc(pool_link, 1)
                        pool.wait_ge(pool_link, KP * q + 1)
                        pool.wait_ge(rows_done, q + 1)
                        nc.gpsimd.tensor_tensor(fin[:, 0:n, :], ev[:, 0:n, 0, 0, :], ev[:, 0:n, 0, 1, :], ALU.add
                                                ).then_inc(pool_link, 1)
                        own = ev[:, 0:n, 1, 0, 0:D]
                        nc.gpsimd.tensor_tensor(own, cols.rearrange("p (k f) -> p k f", f=D),
                                                f[:, 2, blocks].unsqueeze(2).to_broadcast([P, n, D]), ALU.mult)
                        pool.wait_ge(pool_link, KP * q + 2)
                        nc.gpsimd.tensor_tensor(den[:, 0:n], fin[:, 0:n, D], back[:, 0:1].to_broadcast([P, n]), ALU.mult
                                                ).then_inc(pool_link, 1)
                        pool.wait_ge(pool_link, KP * q + 3)
                        nc.gpsimd.tensor_tensor(fin[:, 0:n, 0:D], fin[:, 0:n, 0:D], own, ALU.add)
                        nc.gpsimd.tensor_tensor(den[:, 0:n], den[:, 0:n], f[:, 2, blocks], ALU.add).then_inc(halves, 1)
                        pool.wait_ge(out_got, 16 * (q + 1))
                        nc.gpsimd.tensor_tensor(resid[:, 0:n, :], resid[:, 0:n, :],
                                                bias_row[:].unsqueeze(1).to_broadcast([P, n, D]), ALU.add
                                                ).then_inc(pool_link, 1)

                    with pool.Fori(0, NQ - 1) as q:
                        finish(q, QP)
                    finish(NQ - 1, 1)
                with pool.Else():
                    pool.sem_inc(s_tick, 1)

            @block.tensor
            def _(pe):
                with pe.If(short_way(pe)):
                    pe.sem_inc(mask_used, 2)
                    nc.tensor.transpose(bank[0][0:NB, 0:P], a_dst[:], ident[:]).then_inc(turned, 1)
                    pe.wait_ge(line_ready, 1)
                    pe.wait_ge(col_ready, 1)

                    def group(q, n):
                        for c in range(PC):
                            for k, (h0, hn) in enumerate(UNITS):
                                s = (q * PC + c) * NU + k
                                v = (c * NU + k) % 2
                                for kind in range(2):
                                    pe.wait_ge(low_ready, 2 * c + kind + 1)
                                    if c == 0 and k == 0:
                                        pe.wait_ge(banks_read, q * (2 * QP) + (kind + 1) * QP)
                                    if kind == 0:
                                        pe.wait_ge(pos_ready, s + 1)
                                    else:
                                        pe.wait_ge(rest_ready, s + 1 + PC * NU)
                                    for h in range(hn):
                                        b = c * PH + h0 + h
                                        for d in range(n):
                                            mm = nc.tensor.matmul(bank[2 * d + kind][:, 0:2 * HE], masks[:, v, kind, d, h, :],
                                                                  wh[:, b, kind, :, :].rearrange("p a f -> p (a f)"),
                                                                  start=(b == 0), stop=(b == NB - 1))
                                    if kind == 1:
                                        mm.then_inc(mask_used, 1)
                                    elif c == PC - 1 and k == NU - 1:
                                        mm.then_inc(sums_done, 1)

                    with pe.Fori(0, NQ - 1) as q:
                        group(q, QP)
                    group(NQ - 1, 1)
                with pe.Else():
                    pe.sem_inc(s_tick, 1)

            @block.scalar
            def _(act):
                with act.If(short_way(act)):
                    act.sem_inc(banks_read, 2 * QP)
                    act.wait_ge(turned, 1)
                    nc.scalar.copy(line[:], bank[0][0:NB, 0:P]).then_inc(line_ready, 1)
                    act.wait_ge(neg_ready, 1)
                    nc.scalar.activation(e[:, 0, :], a_src[:], ACT.Exp, bias=neg_top[:, 0:1], scale=1.0)
                    nc.scalar.activation(e[:, 1, :], a_src[:], ACT.Exp, bias=neg_top[:, 1:2], scale=0.2).then_inc(e_ready, 1)
                    act.wait_ge(step, 8)
                    nc.scalar.activation(f[:], z[:], ACT.Exp).then_inc(f_ready, 1)
                    for c in range(PC):
                        for k in range(2):
                            act.wait_ge(hw_ready, 2 * c + k + 1)
                            nc.scalar.copy(wh[:, c * PH:(c + 1) * PH, k, 0, 0:D], tmp[:, k, :, :]).then_inc(high_ready, 1)
                    act.wait_ge(step, 11)

                    act.sem_inc(out_stored, 16)

                    def rows_of(dram, q, n):
                        return dram[bass.ds(q * (QP * P), n * P), :].rearrange("(k p) f -> p k f", p=P)

                    def load(q, n):
                        act.wait_ge(out_stored, 16 * (q + 1))
                        act.sem_inc(s_tick, 1)
                        act.dma_start(resid[:, 0:n, :], rows_of(x1_dram, q, n)).then_inc(out_got, 16)

                    def root(q, n):
                        act.wait_ge(out_link, 3 * q + 2)
                        act.sem_inc(s_tick, 1)
                        nc.scalar.activation(rstd[:, 0:n], mv[:, 0:n, 1], ACT.Sqrt, bias=eps[:, 0:1], scale=1.0
                                             ).then_inc(out_sqrt, 1)

                    def group(q, n, ending):
                        at = bass.ds(q * (QP * P), n * P)
                        for c in range(1, PC):
                            for k, (h0, hn) in enumerate(UNITS):
                                v = (c * NU + k) % 2
                                act.wait_ge(pos_ready, (q * PC + c) * NU + k - 1)
                                act.wait_ge(step_ready, (q * (PC - 1) + c - 1) * NU + k + 1)
                                act.sem_inc(s_tick, 1)
                                for h in range(SB2):
                                    b = c * PH + h0 + hn - SB2 + h
                                    sg = nc.scalar.activation(sign[:, 0:n, h, :], row[:, at].rearrange("p (s n) -> p s n", n=P),
                                                              ACT.Sign, bias=a_src[:, b:b + 1], scale=1.0)
                                sg.then_inc(sign_ready, 1)
                                act.wait_ge(sign_ready, (q * (PC - 1) + c - 1) * NU + k + 1)
                                act.sem_inc(s_tick, 1)
                                nc.scalar.activation(steps[:, v, 0:n, :, :], sign[:, 0:n, :, :], ACT.Relu
                                                     ).then_inc(step_ready, 1)
                            if c == 5 and ending is not None:
                                root(*ending)
                        if ending is not None:
                            before, _ = ending
                            act.wait_ge(rows_done, before + 2)
                            act.sem_inc(s_tick, 1)
                            act.dma_start(rows_of(out, before, QP), resid[:]).then_inc(out_stored, 16)
                        load(q, n)
                        for kind in range(2):
                            if kind == 0:
                                act.wait_ge(sums_done, q + 1)
                                act.wait_ge(halves, q + 1)
                            else:
                                act.wait_ge(mask_used, (q + 1) * PC * NU + 2)
                            act.sem_inc(s_tick, 1)
                            for d in range(n):
                                nc.scalar.activation(ev[:, d, kind, :, :].rearrange("p a f -> p (a f)"),
                                                     bank[2 * d + kind][:, 0:2 * HE], ACT.Copy,
                                                     scale=f[:, kind, bass.ds(q * QP + d, 1)]).then_inc(banks_read, 1)

                    act.wait_ge(row_in, 16)
                    act.sem_inc(step_ready, 1)
                    group(0, QP, None)
                    with act.Fori(1, NQ - 1) as q:
                        group(q, QP, (q - 1, QP))
                    group(NQ - 1, 1, (NQ - 2, QP))
                    root(NQ - 1, 1)
                    act.wait_ge(rows_done, NQ + 1)
                    act.dma_start(out[(NB - 1) * P:n_nodes, :], resid[0:LAST, 0, :]).then_inc(out_stored, 16)
                    act.wait_ge(out_stored, 16 * (NQ + 1))
                with act.Else():
                    act.sem_inc(s_tick, 1)

        K = 6
        with ExitStack() as c3:
            def sm(name):
                return ctx.enter_context(nc.semaphore(f"gat_{name}"))

            def ring(name, shape, dt=F32):
                return c3.enter_context(nc.sbuf_tensor(f"gat_{name}", shape, dt))
            idx = ring("idx", [P, U, C], U32)
            rows = ring("rows", [P, U, C, ROW])
            other = ring("other", [P, 2, C, P])
            masked = ring("masked", [P, 2, C, P])
            eT = ring("eT", [P, 2, C * P])
            wT = ring("wT", [P, 2, C * P])
            wgt = ring("wgt", [P, 2, C, P])
            ad, top, mtop, fall, scale, wsum = (ring(f"s_{k}", [P, U]) for k in ("ad", "top", "mtop", "fall", "scale", "wsum"))
            idx_ready = [sm(f"idx_ready{u}") for u in range(U)]
            row_got = [sm(f"row_got{u}") for u in range(U)]
            other_ready, masked_ready, mT_ps, link, max_ready, z_ready, e_ready, w_ready, w_ps, wgt_ready, mm_done, added = (
                sm("mask_ready"), sm("masked_ready"), sm("maskedT_in_psum"), sm("vector_link"), sm("max_ready"),
                sm("z_ready"), sm("e_ready"), sm("weightsT_ready"), sm("weights_in_psum"), sm("weights_ready"), sm("sum_ready"),
                sm("sum_added"))
            block = c3.enter_context(nc.Block())

            @block.gpsimd
            def _(pool):
                with pool.If(short_way(pool)):
                    pool.sem_inc(s_tick, 1)
                with pool.Else():
                    n = pool.value_load(turns[0:1, 0:1], min_val=1, max_val=P * NCC // U - 2)
                    with pool.Fori(0, n) as i:
                        for u in range(U):
                            pool.wait_ge(idx_ready[u], i + 1)
                            pool.sem_inc(s_tick, 1)
                            for j in range(C):
                                pool.indirect_dma_start(rows[:, u, j, :], None, table_h,
                                                        bass.IndirectOffsetOnAxis(ap=idx[:, u, j:j + 1], axis=0)
                                                        ).then_inc(row_got[u], 16)

            @block.scalar
            def _(act):
                with act.If(short_way(act)):
                    act.sem_inc(s_tick, 1)
                with act.Else():
                    n = act.value_load(turns[0:1, 0:1], min_val=1, max_val=P * NCC // U - 2)

                    def fetch(i, u):
                        _, t = chunk_of(act, i * U + u)
                        t = t.with_bounds(min_val=0, max_val=TA - C)
                        nc.scalar.copy(idx[:, u, :], src[:, bass.ds(t, C)]).then_inc(idx_ready[u], 1)

                    def shift(s, u):
                        act.wait_ge(mT_ps, s + 3)
                        act.wait_ge(link, s * K + 2)
                        act.wait_ge(w_ps, s + 1)
                        nc.scalar.activation(eT[:, u % 2, :], bank[u % 2][:, 0:C * P], ACT.Identity,
                                             bias=ad[:, u:u + 1], scale=1.0).then_inc(z_ready, 1)

                    def weigh(s, u):
                        act.wait_ge(max_ready, s + 1)
                        nc.scalar.activation(scale[:, u:u + 1], fall[:, u:u + 1], ACT.Exp)
                        act.wait_ge(e_ready, s + 1)
                        nc.scalar.activation(wT[:, u % 2, :], eT[:, u % 2, :], ACT.Exp, bias=mtop[:, u:u + 1],
                                             scale=1.0, accum_out=wsum[:, u:u + 1]).then_inc(w_ready, 1)

                    def keep(s, u):
                        act.wait_ge(w_ps, s + 3)
                        act.sem_inc(s_tick, 1)
                        act.wait_ge(mm_done, s + U - 1)
                        nc.scalar.copy(wgt[:, u % 2, :, :], bank[2 + u % 2][:, 0:C * P].rearrange("p (j d) -> p j d", d=P)
                                       ).then_inc(wgt_ready, 1)

                    for u in range(U):
                        fetch(0, u)
                    with act.Fori(0, n) as i:
                        for ph in range(U + 3):
                            if 1 <= ph <= U:
                                shift(i * U + ph - 1, ph - 1)
                            if 2 <= ph <= U + 1:
                                keep(i * U + ph - 2, ph - 2)
                            if 1 <= ph <= U:
                                weigh(i * U + ph - 1, ph - 1)
                            if ph >= 3:
                                act.wait_ge(mm_done, i * U + ph - 3 + U + 1)
                                act.sem_inc(s_tick, 1)
                                fetch(i + 1, ph - 3)

            @block.vector
            def _(dve):
                with dve.If(short_way(dve)):
                    dve.sem_inc(s_tick, 1)
                with dve.Else():
                    n = dve.value_load(turns[0:1, 0:1], min_val=1, max_val=P * NCC // U - 2)
                    with dve.Fori(0, n) as i:
                        col = [None] * U

                        def mask(s, u):
                            b, t = chunk_of(dve, s)
                            t = t.with_bounds(min_val=0, max_val=TA - C)
                            col[u] = b.with_bounds(min_val=0, max_val=NB - 1)
                            nc.vector.scalar_tensor_tensor(
                                out=other[:, u % 2, :, :],
                                in0=dst[:, bass.ds(t, C)].unsqueeze(2).to_broadcast([P, C, P]),
                                scalar=base[:, bass.ds(col[u], 1)],
                                in1=iota[:].unsqueeze(1).to_broadcast([P, C, P]),
                                op0=ALU.subtract, op1=ALU.not_equal).then_inc(other_ready, 1)
                            dve.wait_ge(other_ready, s + 1)
                            dve.wait_ge(row_got[u], (i + 1) * G16)
                            dve.wait_ge(mT_ps, s + 1)
                            nc.vector.scalar_tensor_tensor(
                                out=masked[:, u % 2, :, :], in0=other[:, u % 2, :, :], scalar=NEG,
                                in1=rows[:, u, :, D:D + 1].to_broadcast([P, C, P]), op0=ALU.mult, op1=ALU.add
                            ).then_inc(masked_ready, 1)

                        def maximum(s, u):
                            c, a, m = bass.ds(col[u], 1), ad[:, u:u + 1], top[:, u:u + 1]
                            dve.wait_ge(mT_ps, s + 3)
                            nc.vector.tensor_reduce(m, bank[u % 2][:, 0:C * P], AX.X, ALU.max).then_inc(link, 1)
                            nc.vector.tensor_copy(a, a_dst[:, c]).then_inc(link, 1)
                            dve.wait_ge(link, s * K + 2)
                            nc.vector.tensor_tensor(m, m, a, ALU.add).then_inc(link, 1)
                            dve.wait_ge(link, s * K + 3)
                            nc.vector.scalar_tensor_tensor(out=m, in0=m, scalar=0.2, in1=m, op0=ALU.mult, op1=ALU.max
                                                           ).then_inc(link, 1)
                            dve.wait_ge(link, s * K + 4)
                            nc.vector.tensor_tensor(m, m, peak[:, c], ALU.max).then_inc(link, 1)
                            dve.wait_ge(link, s * K + 5)
                            nc.vector.tensor_scalar(mtop[:, u:u + 1], m, -1.0, None, ALU.mult)
                            nc.vector.tensor_tensor(fall[:, u:u + 1], peak[:, c], m, ALU.subtract).then_inc(max_ready, 1)
                            dve.wait_ge(max_ready, s + 1)
                            dve.sem_inc(s_tick, 1)
                            nc.vector.tensor_copy(peak[:, c], m).then_inc(link, 1)
                            dve.wait_ge(z_ready, s + 3)
                            nc.vector.scalar_tensor_tensor(out=eT[:, u % 2, :], in0=eT[:, u % 2, :], scalar=0.2,
                                                           in1=eT[:, u % 2, :], op0=ALU.mult, op1=ALU.max).then_inc(e_ready, 1)

                        def add(s, u):
                            c = bass.ds(col[u], 1)
                            dve.wait_ge(mm_done, s + U + 1)
                            dve.wait_ge(added, s + 2)
                            nc.vector.scalar_tensor_tensor(out=denom[:, c], in0=denom[:, c], scalar=scale[:, u:u + 1],
                                                           in1=wsum[:, u:u + 1], op0=ALU.mult, op1=ALU.add)
                            cols = acc[:, bass.ds(col[u] * P, P)]
                            nc.vector.scalar_tensor_tensor(out=cols, in0=cols, scalar=scale[:, u:u + 1],
                                                           in1=bank[4 + u % 2][:, 0:P], op0=ALU.mult, op1=ALU.add
                                                           ).then_inc(added, 1)

                        for ph in range(U + 3):
                            if ph < U:
                                mask(i * U + ph, ph)
                            if 1 <= ph <= U:
                                maximum(i * U + ph - 1, ph - 1)
                            if ph >= 3:
                                add(i * U + ph - 3, ph - 3)

            @block.tensor
            def _(pe):
                with pe.If(short_way(pe)):
                    pe.sem_inc(s_tick, 1)
                with pe.Else():
                    n = pe.value_load(turns[0:1, 0:1], min_val=1, max_val=P * NCC // U - 2)
                    pe.sem_inc(mm_done, U)
                    for s2 in (added, w_ps, mT_ps, z_ready, wgt_ready):
                        pe.sem_inc(s2, 2)

                    def turn_masked(s, u):
                        pe.wait_ge(masked_ready, s + 1)
                        pe.wait_ge(z_ready, s + 1)
                        for j in range(C):
                            tr = nc.tensor.transpose(bank[u % 2][:, j * P:(j + 1) * P], masked[:, u % 2, j, :], ident[:])
                        tr.then_inc(mT_ps, 1)

                    def turn_weights(s, u):
                        pe.wait_ge(w_ready, s + 1)
                        pe.wait_ge(wgt_ready, s + 1)
                        for j in range(C):
                            tr = nc.tensor.transpose(bank[2 + u % 2][:, j * P:(j + 1) * P],
                                                     wT[:, u % 2, j * P:(j + 1) * P], ident[:])
                        tr.then_inc(w_ps, 1)

                    def product(s, u):
                        pe.wait_ge(wgt_ready, s + 3)
                        pe.wait_ge(added, s + 1)
                        for j in range(C):
                            mm = nc.tensor.matmul(bank[4 + u % 2][:, 0:P], wgt[:, u % 2, j, :], rows[:, u, j, 0:D],
                                                  start=(j == 0), stop=(j == C - 1))
                        mm.then_inc(mm_done, 1)

                    with pe.Fori(0, n) as i:
                        for ph in range(U + 3):
                            if ph >= 3:
                                product(i * U + ph - 3, ph - 3)
                            if 2 <= ph <= U + 1:
                                turn_weights(i * U + ph - 2, ph - 2)
                            if ph < U:
                                turn_masked(i * U + ph, ph)

        with ExitStack() as c4:
            def sm(name):
                return ctx.enter_context(nc.semaphore(f"out_{name}"))

            def tile(name, shape, dt=F32):
                return c4.enter_context(nc.sbuf_tensor(f"out_{name}", shape, dt))
            nodes = tile("nodes", [P, SB, D])
            resid = tile("resid", [P, SB, D])
            stats = tile("stats", [P, SB, 6])
            mv = tile("mv", [P, SB, 2])
            rstd = tile("rstd", [P, SB])
            res_got, lnk, sq, rows_ready, stored = out_got, out_link, out_sqrt, out_rows, out_stored
            block = c4.enter_context(nc.Block())
            FULL = NT - 1
            NL = 6

            @block.sync
            def _(sp):
                with sp.If(short_way(sp)):
                    sp.sem_inc(s_tick, 1)
                with sp.Else():
                    sp.sem_inc(stored, 16)
                    x1v = x1_dram.rearrange("(k p) f -> p k f", p=P)
                    with sp.Fori(0, NT) as i:
                        sp.wait_ge(rows_ready, i + 1)
                        sp.sem_inc(s_tick, 1)
                        sp.dma_start(resid[:], x1v[:, bass.ds(i * SB, SB), :]).then_inc(res_got, 16)

            @block.scalar
            def _(act):
                with act.If(short_way(act)):
                    act.sem_inc(s_tick, 1)
                with act.Else():
                    outv = out[0:FULL * SB * P, :].rearrange("(k p) f -> p k f", p=P)
                    with act.Fori(0, FULL) as i:
                        act.wait_ge(lnk, NL * i + NL - 1)
                        act.sem_inc(s_tick, 1)
                        nc.scalar.activation(rstd[:], mv[:, :, 1], ACT.Sqrt, bias=eps[:, 0:1], scale=1.0).then_inc(sq, 1)
                        act.wait_ge(rows_ready, i + 2)
                        act.dma_start(outv[:, bass.ds(i * SB, SB), :], nodes[:]).then_inc(stored, 16)
                    act.wait_ge(lnk, NL * FULL + NL - 1)
                    nc.scalar.activation(rstd[:], mv[:, :, 1], ACT.Sqrt, bias=eps[:, 0:1], scale=1.0).then_inc(sq, 1)
                    act.wait_ge(rows_ready, NT + 1)
                    rest = out[FULL * SB * P:FULL * SB * P + (SB - 1) * P, :].rearrange("(k p) f -> p k f", p=P)
                    act.dma_start(rest, nodes[:, 0:SB - 1, :]).then_inc(stored, 16)
                    act.dma_start(out[(NB - 1) * P:n_nodes, :], nodes[0:LAST, SB - 1, :]).then_inc(stored, 16)
                    act.wait_ge(stored, 16 * (1 + FULL + 2))

            @block.vector
            def _(dve):
                with dve.If(short_way(dve)):
                    dve.sem_inc(s_tick, 1)
                with dve.Else():
                    dve.sem_inc(rows_ready, 1)
                    nc.vector.reciprocal(denom[:], denom[:]).then_inc(s_dve, 1)
                    dve.wait_ge(s_dve, 1 + NT + 1)
                    with dve.Fori(0, NT) as i:
                        dve.wait_ge(res_got, 16 * (i + 1))
                        nc.vector.tensor_tensor(resid[:], resid[:], bias_row[:].unsqueeze(1).to_broadcast([P, SB, D]),
                                                ALU.add).then_inc(lnk, 1)
                        dve.wait_ge(lnk, NL * i + 1)
                        for k in range(SB):
                            a = nc.vector.scalar_tensor_tensor(
                                out=resid[:, k, :], in0=acc[:, bass.ds(i * (SB * P) + k * P, P)],
                                scalar=denom[:, bass.ds(i * SB + k, 1)], in1=resid[:, k, :], op0=ALU.mult, op1=ALU.add)
                        a.then_inc(lnk, 1)
                        dve.wait_ge(lnk, NL * i + 2)
                        for k in range(SB):
                            bn = nc.vector.bn_stats(out=stats[:, k, :], in_=resid[:, k, :])
                        bn.then_inc(lnk, 1)
                        dve.wait_ge(lnk, NL * i + 3)
                        dve.sem_inc(s_tick, 1)
                        for k in range(SB):
                            bn = nc.vector.bn_aggr(out=mv[:, k, :], in_=stats[:, k, :])
                        bn.then_inc(lnk, 2)
                        dve.wait_ge(sq, i + 1)
                        nc.vector.reciprocal(rstd[:], rstd[:]).then_inc(lnk, 1)
                        dve.wait_ge(lnk, NL * i + NL)
                        dve.wait_ge(stored, 16 * (i + 1))
                        for k in range(SB):
                            nm = nc.vector.tensor_scalar(nodes[:, k, :], resid[:, k, :], mv[:, k, 0:1],
                                                         rstd[:, k:k + 1], ALU.subtract, ALU.mult)
                        nm.then_inc(rows_ready, 1)


def kernel(x, src, dst, edge_attr_32, L0_gnn_Wm, L0_gnn_bm, L1_gnn_W, L1_gnn_att_src, L1_gnn_att_dst, L1_gnn_bias):
    import concourse.bacc as bacc
    from concourse.bass_utils import run_bass_kernel_spmd as run

    x, src, dst, ea = (np.asarray(a) for a in (x, src, dst, edge_attr_32))
    n, e = x.shape[0], src.shape[0]
    nb, tiles, ta, _ = shapes(n, e)
    xp = np.concatenate([x, np.zeros((nb * P - n, D), x.dtype)])
    ee = (ta + GT) * P
    src_line = np.concatenate([src, np.zeros(ee - e, src.dtype)])
    dst_line = np.concatenate([dst, np.full(ee + 1 - e, NO_NODE, dst.dtype)])
    src_p, dst_p = (a[:ta * P].reshape(ta, P) for a in (src_line, dst_line))
    ea_p = np.concatenate([ea, np.zeros((ee - e, EA), ea.dtype)])
    ea_p = np.concatenate([ea_p, np.ones((ee, 1), ea.dtype)], axis=1)
    W0 = np.concatenate([np.asarray(L0_gnn_Wm).transpose(0, 2, 1), np.asarray(L0_gnn_bm)[:, None, :]], axis=1)
    arrays = {
        "in_x": xp, "in_xT": xp.T, "in_srcT": src_p.T, "in_dstT": dst_p.T, "in_src_line": src_line,
        "in_dst_line": dst_line, "in_ea": ea_p,
        "in_W0": W0, "in_W1": np.asarray(L1_gnn_W),
        "in_att": np.stack([np.asarray(L1_gnn_att_src), np.asarray(L1_gnn_att_dst)]),
        "in_bias": np.asarray(L1_gnn_bias)[None, :],
    }
    arrays = {k: np.ascontiguousarray(a) for k, a in arrays.items()}
    nc = bacc.Bacc("TRN2", target_bir_lowering=False, num_devices=1)
    args = [nc.dram_tensor(k, a.shape, mybir.dt.from_np(a.dtype), kind="ExternalInput").ap() for k, a in arrays.items()]
    out = nc.dram_tensor("out", [n, D], F32, kind="ExternalOutput").ap()
    build(nc, *args, out)
    return run(nc, [arrays], core_ids=[0]).results[0]["out"]
```
